# Optimizing a Trainium2 kernel written in Bass

```python
import numpy as np
import jax
import jax.numpy as jnp

def _softmax(x, axis=-1):
    return jax.nn.softmax(x, axis=axis)

def _gelu(x):
    return jax.nn.gelu(x, approximate=True)

def _silu(x):
    return jax.nn.silu(x)

def _sigmoid(x):
    return jax.nn.sigmoid(x)

def _layernorm(x, axis=-1, eps=1e-05):
    m = jnp.mean(x, axis=axis, keepdims=True)
    v = jnp.var(x, axis=axis, keepdims=True)
    return (x - m) / jnp.sqrt(v + eps)

def _scatter_add(tgt, idx, src, axis=0):
    return tgt.at[idx].add(src)

def _segment_sum(src, seg, n):
    return jax.ops.segment_sum(src, seg, n)
kernel_name = 'mk_recurrent_d1_jaxref_r8_f075e5'

def setup_inputs(seed: int=0):
    np.random.seed(seed)
    _w = jnp.asarray

    def _L0_attn_setup():
        import jax, jax.numpy as jnp
        import numpy as np
        DIM = 128
        HIDDEN = 192
        K = 4
        ALPHA_LOG_SCALE = -8.0

        def _causal_depthwise_conv(x, w, b):
            T = x.shape[1]
            xp = jnp.pad(x, ((0, 0), (K - 1, 0), (0, 0)))
            y = b
            for k in range(K):
                y = y + w[:, k] * xp[:, k:k + T, :]
            return y

        def _rglru_scan(alpha, xs):

            def combine(c1, c2):
                a1, x1 = c1
                a2, x2 = c2
                return (a1 * a2, a2 * x1 + x2)
            _, h = jax.lax.associative_scan(combine, (alpha, xs), axis=1)
            return h
        key = jax.random.key(seed)
        ks = jax.random.split(key, 7)
        x = jax.random.normal(ks[0], (8, 256, DIM), dtype=jnp.float32)
        W_in = jax.random.normal(ks[1], (2 * HIDDEN, DIM), dtype=jnp.float32) * DIM ** (-0.5)
        conv_w = jax.random.normal(ks[2], (HIDDEN, K), dtype=jnp.float32) * (1.0 / K) ** 0.5
        conv_b = jax.random.normal(ks[3], (HIDDEN,), dtype=jnp.float32) * 0.02
        W_gates = jax.random.normal(ks[4], (2 * HIDDEN, HIDDEN), dtype=jnp.float32) * HIDDEN ** (-0.5)
        b_gates = jnp.zeros((2 * HIDDEN,), dtype=jnp.float32)
        forget_base = jnp.linspace(-4.323, -9.0, HIDDEN, dtype=jnp.float32)
        W_out = jax.random.normal(ks[5], (DIM, HIDDEN), dtype=jnp.float32) * HIDDEN ** (-0.5)
        return {'x': x, 'W_in': W_in, 'conv_w': conv_w, 'conv_b': conv_b, 'W_gates': W_gates, 'b_gates': b_gates, 'forget_base': forget_base, 'W_out': W_out}
    _L0_attn_in = _L0_attn_setup()

    def _L0_ffn_setup():
        import jax, jax.numpy as jnp
        import numpy as np
        DIM = 128
        DEPTH = 6
        HEADS = 16
        DIM_HEAD = 64
        WINDOW = 32
        INNER = HEADS * DIM_HEAD
        DIM_INNER = int(DIM * 4 * 2 / 3)
        QK_SCALE = 8.0

        def shift_tokens(t):
            a, s = jnp.split(t, 2, -1)
            s = jnp.pad(s, ((0, 0), (1, 0), (0, 0)))[:, :-1]
            return jnp.concatenate([a, s], -1)

        def l2norm(t):
            return t / jnp.maximum(jnp.linalg.norm(t, axis=-1, keepdims=True), 1e-12)

        def rotate_half(x):
            x1, x2 = jnp.split(x, 2, -1)
            return jnp.concatenate([-x2, x1], -1)

        def rotary_tables(n):
            half = jnp.arange(0, DIM_HEAD, 2, dtype=jnp.float32)
            inv_freq = 1.0 / 10000.0 ** (half / DIM_HEAD)
            t = jnp.arange(n, dtype=jnp.float32)
            freqs = t[:, None] * inv_freq[None, :]
            freqs = jnp.concatenate([freqs, freqs], -1)
            base_scale = (half + 0.4 * DIM_HEAD) / (1.4 * DIM_HEAD)
            power = (t - n // 2) / (WINDOW // 2)
            scale = base_scale[None, :] ** power[:, None]
            scale = jnp.concatenate([scale, scale], -1)
            return (freqs, scale)

        def local_attention(q, k, v):
            b, h, n, d = q.shape
            w = WINDOW
            nw = n // w
            bq = q.reshape(b, h, nw, w, d)
            bk = k.reshape(b, h, nw, w, d)
            bv = v.reshape(b, h, nw, w, d)

            def look(t):
                p = jnp.pad(t, ((0, 0), (0, 0), (1, 0), (0, 0), (0, 0)))
                return jnp.concatenate([p[:, :, :nw], p[:, :, 1:]], axis=3)
            bk2, bv2 = (look(bk), look(bv))
            seq = jnp.arange(n).reshape(nw, w)
            seq_p = jnp.pad(seq, ((1, 0), (0, 0)), constant_values=-1)
            jt = jnp.concatenate([seq_p[:nw], seq_p[1:]], axis=1)
            it = seq[:, :, None]
            jb = jt[:, None, :]
            mask = (it < jb) | (it > jb + w) | (jb == -1)
            sim = jnp.einsum('bhwie,bhwje->bhwij', bq, bk2) * QK_SCALE
            sim = jnp.where(mask, -jnp.finfo(sim.dtype).max, sim)
            attn = jax.nn.softmax(sim, -1)
            out = jnp.einsum('bhwij,bhwje->bhwie', attn, bv2)
            return out.reshape(b, h, n, d)

        def attn_layer(x, Wqkv, qs, ksc, Wo):
            b, n, _ = x.shape
            qkv = x @ Wqkv
            q, k, v = jnp.split(qkv, 3, -1)
            sh = lambda t: t.reshape(b, n, HEADS, DIM_HEAD).transpose(0, 2, 1, 3)
            q, k, v = (sh(q), sh(k), sh(v))
            q = l2norm(q) * qs
            k = l2norm(k) * ksc
            freqs, scale = rotary_tables(n)
            cos, sin = (jnp.cos(freqs), jnp.sin(freqs))
            q = q * cos * scale + rotate_half(q) * sin * scale
            inv = 1.0 / scale
            k = k * cos * inv + rotate_half(k) * sin * inv
            out = local_attention(q, k, v)
            out = out.transpose(0, 2, 1, 3).reshape(b, n, INNER)
            return out @ Wo

        def ffn_layer(x, g, bln, W1, b1, W2, b2):
            mu = x.mean(-1, keepdims=True)
            var = ((x - mu) ** 2).mean(-1, keepdims=True)
            xn = (x - mu) / jnp.sqrt(var + 1e-05) * g + bln
            hg = xn @ W1 + b1
            a, gate = jnp.split(hg, 2, -1)
            return a * jax.nn.gelu(gate, approximate=False) @ W2 + b2
        key = jax.random.key(seed)
        ks = jax.random.split(key, 8)
        B, N = (2, 256)
        init = lambda k, shape: jax.random.normal(k, shape, jnp.float32) * 0.02
        return {'x': jax.random.normal(ks[0], (B, N, DIM), jnp.float32), 'Wqkv': init(ks[1], (DEPTH, DIM, 3 * INNER)), 'q_scale': jnp.ones((DEPTH, DIM_HEAD), jnp.float32), 'k_scale': jnp.ones((DEPTH, DIM_HEAD), jnp.float32), 'Wo': init(ks[2], (DEPTH, INNER, DIM)), 'ln_g': jnp.ones((DEPTH, DIM), jnp.float32), 'ln_b': jnp.zeros((DEPTH, DIM), jnp.float32), 'W1': init(ks[3], (DEPTH, DIM, 2 * DIM_INNER)), 'b1': jnp.zeros((DEPTH, 2 * DIM_INNER), jnp.float32), 'W2': init(ks[4], (DEPTH, DIM_INNER, DIM)), 'b2': jnp.zeros((DEPTH, DIM), jnp.float32)}
    _L0_ffn_in = _L0_ffn_setup()
    _d = {'L0_attn_x': _L0_attn_in['x'], 'L0_attn_W_in': _L0_attn_in['W_in'], 'L0_attn_conv_w': _L0_attn_in['conv_w'], 'L0_attn_conv_b': _L0_attn_in['conv_b'], 'L0_attn_W_gates': _L0_attn_in['W_gates'], 'L0_attn_b_gates': _L0_attn_in['b_gates'], 'L0_attn_forget_base': _L0_attn_in['forget_base'], 'L0_attn_W_out': _L0_attn_in['W_out'], 'L0_ffn_Wqkv': _L0_ffn_in['Wqkv'], 'L0_ffn_q_scale': _L0_ffn_in['q_scale'], 'L0_ffn_k_scale': _L0_ffn_in['k_scale'], 'L0_ffn_Wo': _L0_ffn_in['Wo'], 'L0_ffn_ln_g': _L0_ffn_in['ln_g'], 'L0_ffn_ln_b': _L0_ffn_in['ln_b'], 'L0_ffn_W1': _L0_ffn_in['W1'], 'L0_ffn_b1': _L0_ffn_in['b1'], 'L0_ffn_W2': _L0_ffn_in['W2'], 'L0_ffn_b2': _L0_ffn_in['b2']}
    _x0 = _d['L0_attn_x']
    _d['L0_attn_x'] = jax.random.normal(jax.random.fold_in(jax.random.key(seed), 1), (2, 1024, 128), dtype=_x0.dtype)
    del _x0
    return _d

def reference(L0_attn_x, L0_attn_W_in, L0_attn_conv_w, L0_attn_conv_b, L0_attn_W_gates, L0_attn_b_gates, L0_attn_forget_base, L0_attn_W_out, L0_ffn_Wqkv, L0_ffn_q_scale, L0_ffn_k_scale, L0_ffn_Wo, L0_ffn_ln_g, L0_ffn_ln_b, L0_ffn_W1, L0_ffn_b1, L0_ffn_W2, L0_ffn_b2):

    def _L0_attn_ref(x, W_in, conv_w, conv_b, W_gates, b_gates, forget_base, W_out):
        import jax, jax.numpy as jnp
        import numpy as np
        DIM = 128
        HIDDEN = 192
        K = 4
        ALPHA_LOG_SCALE = -8.0

        def _causal_depthwise_conv(x, w, b):
            T = x.shape[1]
            xp = jnp.pad(x, ((0, 0), (K - 1, 0), (0, 0)))
            y = b
            for k in range(K):
                y = y + w[:, k] * xp[:, k:k + T, :]
            return y

        def _rglru_scan(alpha, xs):

            def combine(c1, c2):
                a1, x1 = c1
                a2, x2 = c2
                return (a1 * a2, a2 * x1 + x2)
            _, h = jax.lax.associative_scan(combine, (alpha, xs), axis=1)
            return h
        u = jnp.einsum('ntc,hc->nth', x, W_in)
        gate, xh = jnp.split(u, 2, axis=-1)
        xh = _causal_depthwise_conv(xh, conv_w, conv_b)
        g = jnp.einsum('nth,gh->ntg', xh, W_gates) + b_gates
        forget, inp = jnp.split(g, 2, axis=-1)
        log_alpha = ALPHA_LOG_SCALE * jax.nn.softplus(forget_base) * jax.nn.sigmoid(forget)
        alpha = jnp.exp(log_alpha)
        beta = jnp.sqrt(1.0 - alpha ** 2 + 1e-06)
        xs = beta * jax.nn.sigmoid(inp) * xh
        h = _rglru_scan(alpha, xs)
        out = jnp.einsum('nth,dh->ntd', jax.nn.gelu(gate, approximate=False) * h, W_out)
        return out

    def _L0_ffn_ref(x, Wqkv, q_scale, k_scale, Wo, ln_g, ln_b, W1, b1, W2, b2):
        import jax, jax.numpy as jnp
        import numpy as np
        DIM = 128
        DEPTH = 6
        HEADS = 16
        DIM_HEAD = 64
        WINDOW = 32
        INNER = HEADS * DIM_HEAD
        DIM_INNER = int(DIM * 4 * 2 / 3)
        QK_SCALE = 8.0

        def shift_tokens(t):
            a, s = jnp.split(t, 2, -1)
            s = jnp.pad(s, ((0, 0), (1, 0), (0, 0)))[:, :-1]
            return jnp.concatenate([a, s], -1)

        def l2norm(t):
            return t / jnp.maximum(jnp.linalg.norm(t, axis=-1, keepdims=True), 1e-12)

        def rotate_half(x):
            x1, x2 = jnp.split(x, 2, -1)
            return jnp.concatenate([-x2, x1], -1)

        def rotary_tables(n):
            half = jnp.arange(0, DIM_HEAD, 2, dtype=jnp.float32)
            inv_freq = 1.0 / 10000.0 ** (half / DIM_HEAD)
            t = jnp.arange(n, dtype=jnp.float32)
            freqs = t[:, None] * inv_freq[None, :]
            freqs = jnp.concatenate([freqs, freqs], -1)
            base_scale = (half + 0.4 * DIM_HEAD) / (1.4 * DIM_HEAD)
            power = (t - n // 2) / (WINDOW // 2)
            scale = base_scale[None, :] ** power[:, None]
            scale = jnp.concatenate([scale, scale], -1)
            return (freqs, scale)

        def local_attention(q, k, v):
            b, h, n, d = q.shape
            w = WINDOW
            nw = n // w
            bq = q.reshape(b, h, nw, w, d)
            bk = k.reshape(b, h, nw, w, d)
            bv = v.reshape(b, h, nw, w, d)

            def look(t):
                p = jnp.pad(t, ((0, 0), (0, 0), (1, 0), (0, 0), (0, 0)))
                return jnp.concatenate([p[:, :, :nw], p[:, :, 1:]], axis=3)
            bk2, bv2 = (look(bk), look(bv))
            seq = jnp.arange(n).reshape(nw, w)
            seq_p = jnp.pad(seq, ((1, 0), (0, 0)), constant_values=-1)
            jt = jnp.concatenate([seq_p[:nw], seq_p[1:]], axis=1)
            it = seq[:, :, None]
            jb = jt[:, None, :]
            mask = (it < jb) | (it > jb + w) | (jb == -1)
            sim = jnp.einsum('bhwie,bhwje->bhwij', bq, bk2) * QK_SCALE
            sim = jnp.where(mask, -jnp.finfo(sim.dtype).max, sim)
            attn = jax.nn.softmax(sim, -1)
            out = jnp.einsum('bhwij,bhwje->bhwie', attn, bv2)
            return out.reshape(b, h, n, d)

        def attn_layer(x, Wqkv, qs, ksc, Wo):
            b, n, _ = x.shape
            qkv = x @ Wqkv
            q, k, v = jnp.split(qkv, 3, -1)
            sh = lambda t: t.reshape(b, n, HEADS, DIM_HEAD).transpose(0, 2, 1, 3)
            q, k, v = (sh(q), sh(k), sh(v))
            q = l2norm(q) * qs
            k = l2norm(k) * ksc
            freqs, scale = rotary_tables(n)
            cos, sin = (jnp.cos(freqs), jnp.sin(freqs))
            q = q * cos * scale + rotate_half(q) * sin * scale
            inv = 1.0 / scale
            k = k * cos * inv + rotate_half(k) * sin * inv
            out = local_attention(q, k, v)
            out = out.transpose(0, 2, 1, 3).reshape(b, n, INNER)
            return out @ Wo

        def ffn_layer(x, g, bln, W1, b1, W2, b2):
            mu = x.mean(-1, keepdims=True)
            var = ((x - mu) ** 2).mean(-1, keepdims=True)
            xn = (x - mu) / jnp.sqrt(var + 1e-05) * g + bln
            hg = xn @ W1 + b1
            a, gate = jnp.split(hg, 2, -1)
            return a * jax.nn.gelu(gate, approximate=False) @ W2 + b2
        for i in range(DEPTH):
            x = attn_layer(shift_tokens(x), Wqkv[i], q_scale[i], k_scale[i], Wo[i]) + x
            x = ffn_layer(shift_tokens(x), ln_g[i], ln_b[i], W1[i], b1[i], W2[i], b2[i]) + x
        return x
    x = L0_attn_x
    xn = _layernorm(x, axis=-1)
    s = _L0_attn_ref(xn, L0_attn_W_in, L0_attn_conv_w, L0_attn_conv_b, L0_attn_W_gates, L0_attn_b_gates, L0_attn_forget_base, L0_attn_W_out)
    g = _silu(_L0_ffn_ref(xn, L0_ffn_Wqkv, L0_ffn_q_scale, L0_ffn_k_scale, L0_ffn_Wo, L0_ffn_ln_g, L0_ffn_ln_b, L0_ffn_W1, L0_ffn_b1, L0_ffn_W2, L0_ffn_b2))
    x = x + s * g
    return x

_drawn_inputs = setup_inputs


def setup_inputs(seed=0):
    import zlib

    import numpy as np

    out = dict(_drawn_inputs(seed))
    spreads = {'L0_attn_b_gates': (0.0, 0.692),
     'L0_ffn_q_scale': (1.0, 0.6),
     'L0_ffn_k_scale': (1.0, 0.6),
     'L0_ffn_ln_g': (1.0, 0.6),
     'L0_ffn_ln_b': (0.0, 0.8),
     'L0_ffn_b1': (0.0, 0.8),
     'L0_ffn_b2': (0.0, 0.527)}
    factors = {'L0_ffn_W1': 6.828, 'L0_ffn_W2': 6.684}
    for name, (base, spread) in spreads.items():
        noise = np.random.default_rng([zlib.crc32(name.encode()), seed]).standard_normal(out[name].shape)
        drawn = base * np.exp(spread * noise) if base else spread * noise
        out[name] = jnp.asarray(drawn.astype(out[name].dtype))
    for name, factor in factors.items():
        out[name] = (out[name] * factor).astype(out[name].dtype)
    return out
```

```python
import math
from contextlib import ExitStack

import numpy as np

import concourse.bass as bass
from concourse import mybir

F32 = mybir.dt.float32
ALU = mybir.AluOpType
ACT = mybir.ActivationFunctionType
AX = mybir.AxisListType

P = 128
B, SEQ, DIM = 2, 1024, 128
TILES = SEQ // P
HIDDEN, CONV_K = 192, 4
HID_LO, HID_HI = P, HIDDEN - P
DEPTH, HEADS, DH, WINDOW = 6, 16, 64, 32
INNER = HEADS * DH
HP = HEADS // 2
FF = int(DIM * 4 * 2 / 3)
FF_CHUNKS = [(c, min(P, FF - c)) for c in range(0, FF, P)]
QK_SCALE = 8.0
MASKED = -1e30
LN_EPS = 1e-5
NORM_FLOOR_SQ = 1e-24
STEPS = DEPTH * TILES
COLS = 512

SM_G, SM_B, SM_B2, SM_VAL, SM_GATE = 0, 1, 2, 3, 6
SMALL = 9


def qn_order(front, ffn):
    order = []
    if front:
        order += [("qkv", 0, c) for c in range(6)]
    if ffn:
        order += ["mean", "var"]
    if front:
        order += [("qkv", 1, c) for c in range(6)]
    if ffn:
        order += [("up", c) for c in range(3)] + ["down"]
    return order


def qn_fill(step, what):
    if isinstance(step, int) and step < 2:
        n = 12 * step + qn_order(True, False).index(what)
        return n % 2, n // 2 + 1
    if isinstance(step, int) and step >= STEPS:
        n = 24 + 18 * (STEPS - 2) + 6 * (step - STEPS) + qn_order(False, True).index(what)
        return n % 2, n // 2 + 1
    n = 24 + qn_order(True, True).index(what)
    return n % 2, (step - 2) * 9 + (n // 2 + 1)


def tr_fill(step, n):
    return n % 2, step * 6 + (n // 2 + 1)


def pv_fill(step, n):
    return n % 2, step * 5 + (n // 2 + 1)


def build(nc, a):
    with ExitStack() as ctx:
        def sb(name, shape, dt=F32):
            return ctx.enter_context(nc.sbuf_tensor(name, shape, dt))

        def sem(name):
            return ctx.enter_context(nc.semaphore(name))

        x = sb("x", [P, B, 1 + SEQ])
        xmid = sb("xmid", [P, B, 1 + SEQ])
        branch = sb("branch", [P, B, SEQ])
        ident = sb("ident", [P, P])
        eps_col = sb("eps_col", [P, 1])
        s_const = sem("const_loaded")

        recurrent_branch(nc, a, x, branch, ident, eps_col, s_const)
        layers(nc, a, x, xmid, ident)
        combine(nc, a, x, branch, ident)


def recurrent_branch(nc, a, x, branch, ident, eps_col, s_const):
    with ExitStack() as ctx:
        def sb(name, shape, dt=F32):
            return ctx.enter_context(nc.sbuf_tensor(name, shape, dt))

        def sem(name):
            return ctx.enter_context(nc.semaphore(name))

        NT = B * TILES
        xt = sb("xt", [P, NT, DIM])
        stats = sb("stats", [P, NT, 6])
        mv = sb("mv", [P, NT, 2])
        lnv = sb("lnv", [P, NT])
        rstd = sb("rstd", [P, NT])
        nw = sb("nw", [P, NT])
        ve = sb("ve", [P, NT])
        w_in = sb("w_in", [P, 2 * HIDDEN])
        wg_lo = sb("wg_lo", [P, 2 * HIDDEN])
        wg_hi = sb("wg_hi", [P, 2 * HIDDEN])
        wo_lo = sb("wo_lo", [P, DIM])
        wo_hi = sb("wo_hi", [P, DIM])
        par = sb("par", [P, 2, 8])
        c8 = sb("c8", [P, 2, 1])
        one_col = sb("one_col", [P, 1])
        tmp = [sb(f"sp{i}", [P, 2, 1]) for i in range(8)]
        xh = sb("xh", [P, 3, CONV_K - 1 + SEQ])
        y = sb("y", [P, 3, SEQ])
        alpha = sb("alpha", [P, 3, SEQ])
        sig_in = sb("sig_in", [P, 3, SEQ])
        beta = sb("beta", [P, 3, SEQ])
        gate = sb("gate", [P, 3, SEQ])
        ps = ctx.enter_context(nc.psum_tensor("ps_rec", [P, 8, COLS], F32))

        s_x, s_w, s_set = sem("r_x"), sem("r_w"), sem("r_set")
        s_st, s_ve, s_ln, s_y0, s_nw, s_xn = sem("r_stats"), sem("r_var"), sem("r_lnv"), sem("r_rstd0"), sem("r_newton"), sem("r_xn")
        s_tr, s_xT = sem("r_transposed"), sem("r_xT")
        s_sp, s_spe = sem("r_softplus"), sem("r_softplus_exp")
        s_pe = sem("r_phase_done")
        s_xh, s_conv, s_f, s_i, s_al, s_a2, s_be, s_g = (sem("r_xh"), sem("r_conv"), sem("r_forget"), sem("r_input"),
                                                         sem("r_alpha"), sem("r_alpha_sq"), sem("r_beta"), sem("r_gate"))
        s_dr, s_h = sem("r_drive"), sem("r_h")
        s_out = sem("r_branch")

        def bank(g, half):
            return 2 * g + half

        def proj(pe, lhs_of, first):
            pass

        with nc.Block() as block:
            @block.sync
            def _(sp):
                sp.dma_start(xt[:, :, :], a["x"].rearrange("b (t p) d -> p (b t) d", p=P)).then_inc(s_x, 16)
                sp.dma_start(ident[:, :], a["ident"]).then_inc(s_const, 16)
                sp.dma_start(w_in[:, :], a["w_in_t"]).then_inc(s_w, 16)
                sp.dma_start(par[:, :, :], a["rec_par"]).then_inc(s_w, 16)
                sp.dma_start(wg_lo[:, :], a["w_gates_t"][0:HID_LO, :]).then_inc(s_w, 16)
                sp.dma_start(wg_hi[0:HID_HI, :], a["w_gates_t"][HID_LO:HIDDEN, :]).then_inc(s_w, 16)
                sp.dma_start(wg_hi[HID_HI:P, :], a["w_gates_t"][HID_LO:HIDDEN, :]).then_inc(s_w, 16)
                sp.dma_start(wo_lo[:, :], a["w_out_t"][0:HID_LO, :]).then_inc(s_w, 16)
                sp.dma_start(wo_hi[0:HID_HI, :], a["w_out_t"][HID_LO:HIDDEN, :]).then_inc(s_w, 16)
                sp.dma_start(wo_hi[HID_HI:P, :], a["w_out_t"][HID_LO:HIDDEN, :]).then_inc(s_w, 16)
                sp.wait_ge(s_w, 8 * 16)
                sp.wait_ge(s_const, 16)

            @block.gpsimd
            def _(pool):
                nc.gpsimd.memset(eps_col[:, :], LN_EPS).then_inc(s_set, 1)
                nc.gpsimd.memset(one_col[:, :], 1e-6).then_inc(s_set, 1)
                nc.gpsimd.memset(xh[:, :, 0:CONV_K - 1], 0.0).then_inc(s_set, 1)
                nc.gpsimd.memset(x[:, :, 0:1], 0.0).then_inc(s_set, 1)

            @block.vector
            def _(dve):
                v = nc.vector
                dve.wait_ge(s_x, 16)
                for t in range(NT):
                    v.bn_stats(stats[:, t, :], xt[:, t, :]).then_inc(s_st, 1)
                dve.wait_ge(s_st, NT)
                for t in range(NT):
                    v.bn_aggr(mv[:, t, :], stats[:, t, :]).then_inc(s_st, 1)
                dve.wait_ge(s_st, 2 * NT)
                v.tensor_scalar(ve[:, :], mv[:, :, 1], LN_EPS, None, ALU.add).then_inc(s_ve, 1)
                dve.wait_ge(s_y0, 1)
                v.tensor_tensor(nw[:, :], rstd[:, :], rstd[:, :], ALU.mult).then_inc(s_nw, 1)
                dve.wait_ge(s_nw, 1)
                v.tensor_tensor(nw[:, :], nw[:, :], ve[:, :], ALU.mult).then_inc(s_nw, 1)
                dve.wait_ge(s_nw, 2)
                v.tensor_scalar(nw[:, :], nw[:, :], -0.5, 1.5, ALU.mult, ALU.add).then_inc(s_nw, 1)
                dve.wait_ge(s_nw, 3)
                v.tensor_tensor(rstd[:, :], rstd[:, :], nw[:, :], ALU.mult).then_inc(s_nw, 1)
                dve.wait_ge(s_nw, 4)
                for t in range(NT):
                    v.tensor_scalar(xt[:, t, :], xt[:, t, :], mv[:, t, 0:1], rstd[:, t:t + 1],
                                    ALU.subtract, ALU.mult).then_inc(s_xn, 1)
                dve.wait_ge(s_w, 8 * 16)
                n = 0
                fb = par[:, :, 7:8]

                def link(ins):
                    nonlocal n
                    n += 1
                    ins.then_inc(s_sp, 1)
                    dve.wait_ge(s_sp, n)

                link(v.tensor_scalar(tmp[0][:, :, :], fb, -1.0, None, ALU.mult))
                link(v.tensor_tensor(tmp[0][:, :, :], tmp[0][:, :, :], fb, ALU.max))
                dve.wait_ge(s_spe, 1)
                e = tmp[1]
                link(v.tensor_scalar(tmp[2][:, :, :], e[:, :, :], 2.0, None, ALU.add))
                link(v.reciprocal(tmp[3][:, :, :], tmp[2][:, :, :]))
                link(v.tensor_tensor(tmp[3][:, :, :], tmp[3][:, :, :], e[:, :, :], ALU.mult))
                link(v.tensor_tensor(tmp[4][:, :, :], tmp[3][:, :, :], tmp[3][:, :, :], ALU.mult))
                link(v.tensor_scalar(tmp[5][:, :, :], tmp[4][:, :, :], 1.0 / 17, 1.0 / 15, ALU.mult, ALU.add))
                for k in (13, 11, 9, 7, 5, 3, 1):
                    link(v.tensor_tensor(tmp[5][:, :, :], tmp[5][:, :, :], tmp[4][:, :, :], ALU.mult))
                    link(v.tensor_scalar(tmp[5][:, :, :], tmp[5][:, :, :], 1.0 / k, None, ALU.add))
                link(v.tensor_tensor(tmp[5][:, :, :], tmp[5][:, :, :], tmp[3][:, :, :], ALU.mult))
                link(v.tensor_scalar(tmp[6][:, :, :], fb, 0.0, None, ALU.max))
                link(v.tensor_scalar(tmp[5][:, :, :], tmp[5][:, :, :], 2.0, None, ALU.mult))
                link(v.tensor_tensor(tmp[6][:, :, :], tmp[6][:, :, :], tmp[5][:, :, :], ALU.add))
                link(v.tensor_scalar(c8[:, :, :], tmp[6][:, :, :], -8.0, None, ALU.mult))
                for t in range(0, NT, 4):
                    dve.wait_ge(s_tr, t // 4 + 1)
                    v.tensor_copy(x[:, t // TILES, 1 + (t % TILES) * P:1 + (t % TILES + 4) * P],
                                  ps[:, t // 4, :]).then_inc(s_xT, 1)
                for g in range(3):
                    dve.wait_ge(s_xh, g + 1)
                    pg = g // 2
                    for k in range(CONV_K):
                        src = xh[:, g, k:k + SEQ]
                        if k == 0:
                            v.tensor_scalar(y[:, g, :], src, par[:, pg, 0:1], par[:, pg, 4:5],
                                            ALU.mult, ALU.add).then_inc(s_conv, 1)
                        else:
                            dve.wait_ge(s_conv, CONV_K * g + k)
                            v.scalar_tensor_tensor(y[:, g, :], src, par[:, pg, k:k + 1], y[:, g, :],
                                                   ALU.mult, ALU.add).then_inc(s_conv, 1)
                for g in range(3):
                    dve.wait_ge(s_al, g + 1)
                    v.tensor_tensor(beta[:, g, :], alpha[:, g, :], alpha[:, g, :], ALU.mult).then_inc(s_a2, 1)
                    dve.wait_ge(s_a2, 2 * g + 1)
                    v.tensor_scalar(beta[:, g, :], beta[:, g, :], -1.0, 1.0, ALU.mult, ALU.add).then_inc(s_a2, 1)
                for g in range(3):
                    dve.wait_ge(s_i, g + 1)
                    v.tensor_tensor(y[:, g, :], y[:, g, :], sig_in[:, g, :], ALU.mult).then_inc(s_dr, 1)
                for g in range(3):
                    dve.wait_ge(s_be, g + 1)
                    dve.wait_ge(s_dr, 3 + g)
                    v.tensor_tensor(y[:, g, :], y[:, g, :], beta[:, g, :], ALU.mult).then_inc(s_dr, 1)
                for g in range(3):
                    dve.wait_ge(s_dr, 4 + g)
                    v.tensor_tensor_scan(sig_in[:, g, :], alpha[:, g, :], y[:, g, :], 0.0,
                                         ALU.mult, ALU.add).then_inc(s_h, 1)
                for g in range(3):
                    dve.wait_ge(s_h, 3 + g)
                    dve.wait_ge(s_g, g + 1)
                    v.tensor_tensor(gate[:, g, :], gate[:, g, :], sig_in[:, g, :], ALU.mult).then_inc(s_h, 1)
                for q in range(4):
                    dve.wait_ge(s_pe, 5)
                    v.tensor_copy(branch[:, q // 2, (q % 2) * COLS:(q % 2 + 1) * COLS], ps[:, q, :]).then_inc(s_out, 1)
                dve.wait_ge(s_out, 4)

            @block.scalar
            def _(act):
                s = nc.scalar
                act.wait_ge(s_ve, 1)
                act.wait_ge(s_set, 4)
                s.activation(lnv[:, :], ve[:, :], ACT.Ln).then_inc(s_ln, 1)
                act.wait_ge(s_ln, 1)
                s.activation(rstd[:, :], lnv[:, :], ACT.Exp, scale=-0.5).then_inc(s_y0, 1)
                act.wait_ge(s_sp, 2)
                s.activation(tmp[1][:, :, :], tmp[0][:, :, :], ACT.Exp, scale=-1.0).then_inc(s_spe, 1)
                act.wait_ge(s_pe, 1)
                for g in range(3):
                    s.activation(xh[:, g, CONV_K - 1:CONV_K - 1 + SEQ],
                                 ps[:, 2 * g:2 * g + 2, :].rearrange("p a b -> p (a b)"), ACT.Copy).then_inc(s_xh, 1)
                act.wait_ge(s_pe, 2)
                for g in range(3):
                    s.activation(alpha[:, g, :], ps[:, 2 * g:2 * g + 2, :].rearrange("p a b -> p (a b)"), ACT.Sigmoid,
                                 bias=par[:, g // 2, 5:6], scale=1.0).then_inc(s_f, 1)
                act.wait_ge(s_pe, 3)
                for g in range(3):
                    s.activation(sig_in[:, g, :], ps[:, 2 * g:2 * g + 2, :].rearrange("p a b -> p (a b)"), ACT.Sigmoid,
                                 bias=par[:, g // 2, 6:7], scale=1.0).then_inc(s_i, 1)
                act.wait_ge(s_sp, 26)
                for g in range(3):
                    act.wait_ge(s_f, g + 1)
                    s.activation(alpha[:, g, :], alpha[:, g, :], ACT.Exp, scale=c8[:, g // 2, :]).then_inc(s_al, 1)
                for g in range(3):
                    act.wait_ge(s_a2, 2 * g + 2)
                    s.activation(beta[:, g, :], beta[:, g, :], ACT.Sqrt, bias=one_col[:, :], scale=1.0).then_inc(s_be, 1)
                act.wait_ge(s_pe, 4)
                for g in range(3):
                    s.activation(gate[:, g, :], ps[:, 2 * g:2 * g + 2, :].rearrange("p a b -> p (a b)"),
                                 ACT.Gelu).then_inc(s_g, 1)

            @block.tensor
            def _(pe):
                pe.wait_ge(s_const, 16)
                for t in range(NT):
                    pe.wait_ge(s_xn, t + 1)
                    m = nc.tensor.transpose(ps[:, t // 4, (t % 4) * P:(t % 4 + 1) * P], xt[:, t, :], ident[:, :])
                    if t % 4 == 3:
                        m.then_inc(s_tr, 1)
                pe.wait_ge(s_xT, 4)
                pe.wait_ge(s_w, 8 * 16)

                def from_x(c0):
                    for half in range(2):
                        for b in range(B):
                            rhs = x[:, b, 1 + half * COLS:1 + (half + 1) * COLS]
                            nc.tensor.matmul(ps[:, bank(b, half), :], w_in[:, c0:c0 + HID_LO], rhs, start=True, stop=True)
                            m = nc.tensor.matmul(ps[HID_HI * b:HID_HI * (b + 1), bank(2, half), :],
                                                 w_in[:, c0 + HID_LO:c0 + HIDDEN], rhs, start=True, stop=True)
                    m.then_inc(s_pe, 1)

                def from_y(c0):
                    for half in range(2):
                        cols = slice(half * COLS, (half + 1) * COLS)
                        for b in range(B):
                            hi = slice(HID_HI * b, HID_HI * (b + 1))
                            for out, m0, m1 in ((ps[:, bank(b, half), :], c0, c0 + HID_LO),
                                                (ps[hi, bank(2, half), :], c0 + HID_LO, c0 + HIDDEN)):
                                nc.tensor.matmul(out, wg_lo[:, m0:m1], y[:, b, cols], start=True, stop=False)
                                m = nc.tensor.matmul(out, wg_hi[hi, m0:m1], y[hi, 2, cols], start=False, stop=True)
                    m.then_inc(s_pe, 1)

                from_x(HIDDEN)
                pe.wait_ge(s_conv, 3 * CONV_K)
                pe.wait_ge(s_xh, 3)
                from_y(0)
                pe.wait_ge(s_f, 3)
                from_y(HIDDEN)
                pe.wait_ge(s_i, 3)
                from_x(0)
                pe.wait_ge(s_g, 3)
                pe.wait_ge(s_h, 6)
                for b in range(B):
                    hi = slice(HID_HI * b, HID_HI * (b + 1))
                    for half in range(2):
                        cols = slice(half * COLS, (half + 1) * COLS)
                        nc.tensor.matmul(ps[:, 2 * b + half, :], wo_lo[:, :], gate[:, b, cols], start=True, stop=False)
                        m = nc.tensor.matmul(ps[:, 2 * b + half, :], wo_hi[hi, :], gate[hi, 2, cols], start=False, stop=True)
                m.then_inc(s_pe, 1)


def layers(nc, a, x, xmid, ident):
    with ExitStack() as ctx:
        def sb(name, shape, dt=F32):
            return ctx.enter_context(nc.sbuf_tensor(name, shape, dt))

        def sem(name):
            return ctx.enter_context(nc.semaphore(name))

        def per_stream(name, shape):
            return [sb(f"{name}{b}", shape) for b in range(B)]

        wqkv = sb("wqkv", [P, 3 * INNER])
        wo = sb("wo", [P, HP, DIM])
        w1 = sb("w1", [P, 2 * FF])
        w2 = sb("w2", [P, len(FF_CHUNKS), DIM])
        small = sb("small", [P, SMALL])
        rot = sb("rot", [P, TILES, 4 * DH])
        scales = sb("scales", [P, DEPTH, 4 * DH])
        mask = sb("mask", [P, TILES, P])
        first = sb("first", [P, TILES, WINDOW])
        mean_w = sb("mean_w", [P, P])
        tab = sb("tab", [P, 4, DH])
        xs = per_stream("xs", [P, P])
        qk = per_stream("qk", [P, 2 * INNER])
        sq = sb("sq", [P, 2 * INNER])
        ss, lss, y0, rinv = (per_stream(n, [P, 2 * HEADS]) for n in ("ss", "lss", "yz", "rinv"))
        t2 = sb("t2", [P, 2 * INNER])
        qkr = per_stream("qkr", [P, 2 * INNER])
        v_new = per_stream("v_new", [P, INNER])
        v_own = per_stream("v_own", [P, INNER])
        v_back = per_stream("v_back", [P, INNER])
        qbd = per_stream("qbd", [P, HP, 4, 2, WINDOW])
        kT = per_stream("kT", [P, HP, WINDOW + P])
        pr = per_stream("pr", [P, HP, 2, 2 * WINDOW])
        rmax, rsum, rrec = (per_stream(n, [P, 2 * HP]) for n in ("rmax", "rsum", "rrec"))
        pbd = per_stream("pbd", [P, HP, 2, 2, 2, WINDOW])
        oT = per_stream("oT", [P, HP, 2, 2 * WINDOW])
        fx, fc, fv, fy, fn, fxn = (sb(n, [P, B, P]) for n in ("fx", "fc", "fv", "fy", "fn", "fxn"))
        fsq, fl = fx, fn
        gel = sb("gel", [P, B, P])
        hid = sb("hid", [P, len(FF_CHUNKS), B, P])

        ps_qn = [ctx.enter_context(nc.psum_tensor(f"ps_qn{i}", [P, COLS], F32)) for i in range(2)]
        ps_tr = [ctx.enter_context(nc.psum_tensor(f"ps_tr{i}", [P, COLS], F32)) for i in range(2)]
        ps_s = ctx.enter_context(nc.psum_tensor("ps_s", [P, HP, 2, 2 * WINDOW], F32))
        ps_pv = [ctx.enter_context(nc.psum_tensor(f"ps_pv{i}", [P, COLS], F32)) for i in range(2)]

        consts, cleared = sem("consts_loaded"), sem("cleared")
        wqkv_in, wo_in, ffn_in = sem("wqkv_loaded"), sem("wo_loaded"), sem("ffn_loaded")
        qn_full, qn_done = [[sem(f"qn_{n}{i}") for i in range(2)] for n in ("filled", "evacuated")]
        tr_full, tr_done = [[sem(f"tr_{n}{i}") for i in range(2)] for n in ("filled", "evacuated")]
        pv_full, pv_done = [[sem(f"pv_{n}{i}") for i in range(2)] for n in ("filled", "evacuated")]

        def streams(name):
            return [sem(f"{name}{b}") for b in range(B)]

        tab_ready = sem("tab_ready")
        xs_ready, ss_sum, ss_ready, lss_ready, y0_ready, newton, rinv_ready = map(streams, (
            "xs_ready", "ss_sum", "ss_ready", "lss_ready", "y0_ready", "newton", "rinv_ready"))
        rotated, added, qk_ready = map(streams, ("rotated", "added", "qk_ready"))
        v_carried, v_moved = map(streams, ("v_carried", "v_moved"))
        k_carried = streams("k_carried")
        s_full, s_read = sem("scores_filled"), sem("scores_read")
        max_ready, shifted, exp_ready, sum_ready, rec_ready, probs_ready = map(streams, (
            "max_ready", "shifted", "exp_ready", "sum_ready", "rec_ready", "probs_ready"))
        fx_ready, fsq_ready, fl_ready, fy_ready, fnewton, fxn_ready, gel_ready = map(sem, (
            "fx_ready", "fsq_ready", "fl_ready", "fy_ready", "fnewton", "fxn_ready", "gel_ready"))

        def tile_of(step):
            return step % TILES

        def layer_of(step):
            return step // TILES

        def cols(step, lead):
            return bass.ds(tile_of(step) * P + lead, P)

        def wait_prev(eng, semaphore, value, step):
            if not (isinstance(step, int) and step == 0):
                eng.wait_ge(semaphore, value)

        def ring_free(eng, done, bank, count, per):
            if not (isinstance(count, int) and count == 1):
                eng.wait_ge(done[bank], (count - 1) * per)

        def run(front, attend, ffn_a, ffn_b, step_order):
            pass

        def steps(eng, body):
            body(0, True, False, False)
            body(1, True, True, False)
            body(2, True, True, True)
            with eng.Fori(3, STEPS) as i:
                body(i, True, True, True)
            body(STEPS, False, True, True)
            body(STEPS + 1, False, False, True)

        with nc.Block() as block:
            @block.sync
            def _(sp):
                def load_wqkv(l):
                    sp.dma_start(wqkv[:, :], a["Wqkv"][l, :, :]).then_inc(wqkv_in, 16)

                def load_wo(l):
                    sp.dma_start(wo[:, :, :], a["Wo"][l, :, :].rearrange("(c p) n -> p c n", p=P)).then_inc(wo_in, 16)

                def load_ffn(l):
                    sp.dma_start(w1[:, :], a["W1"][l, :, :]).then_inc(ffn_in, 16)
                    sp.dma_start(w2[:, 0:2, :], a["W2"][l, 0:2 * P, :].rearrange("(c p) n -> p c n", p=P)).then_inc(ffn_in, 16)
                    sp.dma_start(w2[0:FF - 2 * P, 2, :], a["W2"][l, 2 * P:FF, :]).then_inc(ffn_in, 16)
                    sp.dma_start(small[:, :], a["small"][l, :, :]).then_inc(ffn_in, 16)

                load_wqkv(0)
                sp.dma_start(rot[:, :, :], a["rot"]).then_inc(consts, 16)
                sp.dma_start(scales[:, :, :].rearrange("p l d -> p (l d)"), a["scales"].partition_broadcast(P)).then_inc(consts, 16)
                sp.dma_start(mask[:, :, :], a["mask"]).then_inc(consts, 16)
                sp.dma_start(first[:, :, :], a["first"]).then_inc(consts, 16)
                load_wo(0)
                load_ffn(0)

                def move_v(j):
                    for b in range(B):
                        if isinstance(j, int) and j == 0:
                            sp.wait_ge(cleared, 1)
                        else:
                            bank, n = pv_fill(j - 1, 5 * b + 3)
                            sp.wait_ge(pv_full[bank], n)
                        sp.dma_start(v_back[b][0:WINDOW, :], v_own[b][P - WINDOW:P, :]).then_inc(v_carried[b], 16)
                        for c in (4, 5):
                            bank, n = qn_fill(j, ("qkv", b, c))
                            sp.wait_ge(qn_done[bank], n)
                        sp.dma_start(v_back[b][WINDOW:P, :], v_new[b][0:P - WINDOW, :]).then_inc(v_moved[b], 16)
                        sp.wait_ge(v_carried[b], (j + 1) * 16)
                        sp.dma_start(v_own[b][:, :], v_new[b][:, :]).then_inc(v_moved[b], 16)

                def layer(l, load_this, load_next):
                    j = l * TILES
                    move_v(j)
                    if load_this:
                        bank, n = pv_fill(j - 1, 9)
                        sp.wait_ge(pv_full[bank], n)
                        load_wo(l)
                    move_v(j + 1)
                    if load_this:
                        bank, n = qn_fill(j + 1, "down")
                        sp.wait_ge(qn_done[bank], n)
                        load_ffn(l)
                    with sp.Fori(2, TILES - 1) as t:
                        move_v(j + t)
                    if load_next:
                        bank, n = qn_fill(j + TILES - 1, ("qkv", 1, 5))
                        sp.wait_ge(qn_full[bank], n)
                        load_wqkv(l + 1)
                    move_v(j + TILES - 1)

                for l in range(DEPTH):
                    layer(l, l > 0, l < DEPTH - 1)

            @block.tensor
            def _(pe):
                mm, tr = nc.tensor.matmul, nc.tensor.transpose

                def qkv(i, b):
                    pe.wait_ge(xs_ready[b], i + 1)
                    pe.wait_ge(wqkv_in, (layer_of(i) + 1) * 16)
                    for c in range(6):
                        bank, n = qn_fill(i, ("qkv", b, c))
                        ring_free(pe, qn_done, bank, n, 1)
                        mm(ps_qn[bank][:, :], xs[b][:, :], wqkv[:, c * COLS:(c + 1) * COLS],
                           start=True, stop=True).then_inc(qn_full[bank], 1)

                def transpose_qk(j, b):
                    pe.wait_ge(qk_ready[b], 2 * (j + 1))
                    for f in range(4):
                        bank, n = tr_fill(j, 4 * b + f)
                        ring_free(pe, tr_done, bank, n, 2)
                        for m in range(4):
                            last = tr(ps_tr[bank][:, m * P:(m + 1) * P], qkr[b][:, (4 * f + m) * P:(4 * f + m + 1) * P],
                                      ident[:, :])
                        last.then_inc(tr_full[bank], 1)

                def scores(j, b):
                    for f in (2, 3):
                        bank, n = tr_fill(j, 4 * b + f)
                        pe.wait_ge(tr_done[bank], n * 2)
                    if b:
                        pe.wait_ge(s_read, 2 * j + 1)
                    else:
                        wait_prev(pe, s_read, 2 * j, j)
                    for hp in range(HP):
                        for u in range(2):
                            for odd in range(2):
                                w = 2 * u + odd
                                last = mm(ps_s[64 * odd:64 * odd + 64, hp, u, :],
                                          qbd[b][:, hp, w, :, :].rearrange("p h q -> p (h q)"),
                                          kT[b][:, hp, WINDOW * w:WINDOW * (w + 2)], start=True, stop=True)
                    last.then_inc(s_full, 1)

                def attend(j, b):
                    pe.wait_ge(probs_ready[b], j + 1)
                    for f in range(2):
                        bank, n = tr_fill(j, 8 + 2 * b + f)
                        ring_free(pe, tr_done, bank, n, 2)
                        for m in range(4):
                            last = tr(ps_tr[bank][:, m * P:(m + 1) * P],
                                      pr[b][:, 4 * f + m, :, :].rearrange("p u k -> p (u k)"), ident[:, :])
                        last.then_inc(tr_full[bank], 1)
                    pe.wait_ge(v_moved[b], (j + 1) * 32)
                    pe.wait_ge(v_carried[b], (j + 1) * 16)
                    for f in range(4):
                        tbank, tn = tr_fill(j, 8 + 2 * b + f // 2)
                        pe.wait_ge(tr_done[tbank], tn * 2)
                        bank, n = pv_fill(j, 5 * b + f)
                        ring_free(pe, pv_done, bank, n, 2)
                        for m in range(4):
                            hp, odd = 2 * f + m // 2, m % 2
                            v = (v_own if odd else v_back)[b]
                            last = mm(ps_pv[bank][:, m * P:(m + 1) * P], v[:, hp * P:(hp + 1) * P],
                                      pbd[b][:, hp, odd, :, :, :].rearrange("p h u q -> p (h u q)"), start=True, stop=True)
                        last.then_inc(pv_full[bank], 1)
                    pe.wait_ge(wo_in, (layer_of(j) + 1) * 16)
                    for f in (2, 3):
                        fb, fnum = pv_fill(j, 5 * b + f)
                        pe.wait_ge(pv_done[fb], fnum * 2)
                    bank, n = pv_fill(j, 5 * b + 4)
                    ring_free(pe, pv_done, bank, n, 2)
                    for hp in range(HP):
                        last = mm(ps_pv[bank][:, 0:P], wo[:, hp, :], oT[b][:, hp, :, :].rearrange("p a c -> p (a c)"),
                                  start=(hp == 0), stop=(hp == HP - 1))
                    last.then_inc(pv_full[bank], 1)

                def flat(t):
                    return t[:, :, :].rearrange("p b t -> p (b t)")

                def ffn_mean(i, n):
                    pe.wait_ge(fx_ready, n + 1)
                    bank, k = qn_fill(i, "mean")
                    ring_free(pe, qn_done, bank, k, 1)
                    mm(ps_qn[bank][:, 0:B * P], mean_w[:, :], flat(fx), start=True, stop=True).then_inc(qn_full[bank], 1)

                def ffn_var(i, n):
                    pe.wait_ge(fsq_ready, n + 1)
                    bank, k = qn_fill(i, "var")
                    ring_free(pe, qn_done, bank, k, 1)
                    mm(ps_qn[bank][:, 0:B * P], mean_w[:, :], flat(fsq), start=True, stop=True).then_inc(qn_full[bank], 1)

                def ffn_up(i, n):
                    pe.wait_ge(ffn_in, (layer_of(n) + 1) * 64)
                    pe.wait_ge(fxn_ready, n + 1)
                    for c, (r, m) in enumerate(FF_CHUNKS):
                        bank, k = qn_fill(i, ("up", c))
                        ring_free(pe, qn_done, bank, k, 1)
                        mm(ps_qn[bank][0:m, 0:B * P], w1[:, r:r + m], flat(fxn), start=True, stop=True)
                        mm(ps_qn[bank][0:m, B * P:2 * B * P], w1[:, FF + r:FF + r + m], flat(fxn),
                           start=True, stop=True).then_inc(qn_full[bank], 1)

                def ffn_down(i, n):
                    for c in (1, 2):
                        cb, ck = qn_fill(i, ("up", c))
                        pe.wait_ge(qn_done[cb], ck)
                    bank, k = qn_fill(i, "down")
                    ring_free(pe, qn_done, bank, k, 1)
                    for c, (r, m) in enumerate(FF_CHUNKS):
                        last = mm(ps_qn[bank][:, 0:B * P], w2[0:m, c, :], hid[0:m, c, :, :].rearrange("p b t -> p (b t)"),
                                  start=(c == 0), stop=(c == len(FF_CHUNKS) - 1))
                    last.then_inc(qn_full[bank], 1)

                def body(i, front, attention, ffn):
                    j, n = i - 1, i - 2
                    if front:
                        qkv(i, 0)
                    if attention:
                        transpose_qk(j, 0)
                        transpose_qk(j, 1)
                    if ffn:
                        ffn_mean(i, n)
                    if attention:
                        scores(j, 0)
                    if ffn:
                        ffn_var(i, n)
                    if attention:
                        scores(j, 1)
                    if front:
                        qkv(i, 1)
                    if attention:
                        attend(j, 0)
                    if ffn:
                        ffn_up(i, n)
                        ffn_down(i, n)
                    if attention:
                        attend(j, 1)

                pe.wait_ge(cleared, 1)
                steps(pe, body)

            @block.scalar
            def _(act):
                f = nc.scalar.activation

                def qkv(i, b):
                    wait_prev(act, added[b], i * 2, i)
                    for c in range(4):
                        bank, n = qn_fill(i, ("qkv", b, c))
                        act.wait_ge(qn_full[bank], n)
                        f(qk[b][:, c * COLS:(c + 1) * COLS], ps_qn[bank][:, :], ACT.Copy)
                        if c == 0:
                            if b:
                                act.wait_ge(ss_sum[0], i + 1)
                            else:
                                wait_prev(act, ss_sum[1], i, i)
                        f(sq[:, c * COLS:(c + 1) * COLS], ps_qn[bank][:, :], ACT.Square).then_inc(qn_done[bank], 1)
                    wait_prev(act, v_moved[b], i * 32, i)
                    for c in range(2):
                        bank, n = qn_fill(i, ("qkv", b, 4 + c))
                        act.wait_ge(qn_full[bank], n)
                        f(v_new[b][:, c * COLS:(c + 1) * COLS], ps_qn[bank][:, :], ACT.Copy).then_inc(qn_done[bank], 1)

                def inv_norm(i, b):
                    act.wait_ge(ss_ready[b], i + 1)
                    f(lss[b][:, :], ss[b][:, :], ACT.Ln).then_inc(lss_ready[b], 1)
                    act.wait_ge(lss_ready[b], i + 1)
                    wait_prev(act, rinv_ready[b], i, i)
                    f(y0[b][:, :], lss[b][:, :], ACT.Exp, scale=-0.5).then_inc(y0_ready[b], 1)

                def evac_qk(j, b):
                    if b:
                        wait_prev(act, s_full, 2 * j, j)
                    else:
                        wait_prev(act, s_full, 2 * j - 1, j)
                    for k in range(2):
                        bank, n = tr_fill(j, 4 * b + k)
                        act.wait_ge(tr_full[bank], n)
                        f(qbd[b][0:DH, 4 * k:4 * k + 4, :, 0, :],
                          ps_tr[bank][0:DH, :].rearrange("p (m w q) -> p m w q", m=4, w=4), ACT.Copy).then_inc(tr_done[bank], 1)
                    act.wait_ge(k_carried[b], j + 1)
                    for k in range(2):
                        bank, n = tr_fill(j, 4 * b + 2 + k)
                        act.wait_ge(tr_full[bank], n)
                        f(kT[b][:, 4 * k:4 * k + 4, WINDOW:],
                          ps_tr[bank][:, :].rearrange("p (m t) -> p m t", m=4), ACT.Copy).then_inc(tr_done[bank], 2)

                def exps(j, b):
                    act.wait_ge(shifted[b], j + 1)
                    f(pr[b][:, :, :, :], pr[b][:, :, :, :], ACT.Exp, scale=QK_SCALE).then_inc(exp_ready[b], 1)

                def evac_attend(j, b):
                    bank, n = pv_fill(j - 1, 5 * b + 3)
                    wait_prev(act, pv_full[bank], n, j)
                    for k in range(2):
                        bank, n = tr_fill(j, 8 + 2 * b + k)
                        act.wait_ge(tr_full[bank], n)
                        f(pbd[b][0:DH, 4 * k:4 * k + 4, :, :, 0, :].rearrange("p m a h q -> p (m a h) q"),
                          ps_tr[bank][0:DH, :].rearrange("p (x q) -> p x q", q=WINDOW), ACT.Copy).then_inc(tr_done[bank], 1)
                    bank, n = pv_fill(j - 1, 5 * b + 4)
                    wait_prev(act, pv_full[bank], n, j)
                    for k in range(4):
                        bank, n = pv_fill(j, 5 * b + k)
                        act.wait_ge(pv_full[bank], n)
                        f(oT[b][0:DH, 2 * k:2 * k + 2, :, :].rearrange("p m a c -> p (m a) c"),
                          ps_pv[bank][0:DH, :].rearrange("p (x h c) -> p x h c", h=2, c=DH)[:, :, 0, :],
                          ACT.Copy).then_inc(pv_done[bank], 1)

                def ffn_square(i, n):
                    bank, k = qn_fill(i, "mean")
                    act.wait_ge(qn_done[bank], k)
                    f(fsq[:, :, :], fc[:, :, :], ACT.Square).then_inc(fsq_ready, 1)

                def ffn_rstd(i, n):
                    bank, k = qn_fill(i, "var")
                    act.wait_ge(qn_done[bank], k)
                    f(fl[:, :, :], fv[:, :, :], ACT.Ln).then_inc(fl_ready, 1)
                    act.wait_ge(fl_ready, n + 1)
                    f(fy[:, :, :], fl[:, :, :], ACT.Exp, scale=-0.5).then_inc(fy_ready, 1)

                def ffn_gelu(i, n):
                    for c, (r, m) in enumerate(FF_CHUNKS):
                        bank, k = qn_fill(i, ("up", c))
                        act.wait_ge(qn_full[bank], k)
                        if c:
                            pb, pk = qn_fill(i, ("up", c - 1))
                            act.wait_ge(qn_done[pb], pk)
                        f(gel[0:m, :, :].rearrange("p b t -> p (b t)"), ps_qn[bank][0:m, B * P:2 * B * P], ACT.Gelu,
                          bias=small[0:m, SM_GATE + c:SM_GATE + c + 1], scale=1.0).then_inc(gel_ready, 1)

                def body(i, front, attention, ffn):
                    j, n = i - 1, i - 2
                    if front:
                        qkv(i, 0)
                    if attention:
                        evac_qk(j, 0)
                        evac_qk(j, 1)
                        exps(j, 0)
                    if ffn:
                        ffn_square(i, n)
                    if attention:
                        exps(j, 1)
                    if front:
                        inv_norm(i, 0)
                    if ffn:
                        ffn_rstd(i, n)
                    if front:
                        qkv(i, 1)
                    if attention:
                        evac_attend(j, 0)
                    if ffn:
                        ffn_gelu(i, n)
                    if front:
                        inv_norm(i, 1)
                    if attention:
                        evac_attend(j, 1)

                act.wait_ge(cleared, 1)
                steps(act, body)

            @block.vector
            def _(dve):
                v = nc.vector

                def shift_in(i, b):
                    bank, n = qn_fill(i - 1, ("qkv", b, 5)) if not (isinstance(i, int) and i == 0) else (0, 0)
                    wait_prev(dve, qn_full[bank], n, i)
                    v.tensor_copy(xs[b][0:64, :], x[0:64, b, cols(i, 1)])
                    v.tensor_copy(xs[b][64:P, :], x[64:P, b, cols(i, 0)]).then_inc(xs_ready[b], 1)

                def rotate(i, b):
                    for c in (2, 3):
                        bank, n = qn_fill(i, ("qkv", b, c))
                        dve.wait_ge(qn_done[bank], n)
                    wait_prev(dve, rinv_ready[b], i, i)
                    v.tensor_reduce(ss[b][:, :], sq[:, :].rearrange("p (h d) -> p h d", d=DH), AX.X, ALU.add).then_inc(ss_sum[b], 1)
                    dve.wait_ge(ss_sum[b], i + 1)
                    v.tensor_scalar(ss[b][:, :], ss[b][:, :], NORM_FLOOR_SQ, None, ALU.max).then_inc(ss_ready[b], 1)
                    if b:
                        dve.wait_ge(added[0], (i + 1) * 2)
                    else:
                        wait_prev(dve, added[1], i * 2, i)
                    dve.wait_ge(tab_ready, i + 1)
                    for k in range(2):
                        part = slice(k * INNER, (k + 1) * INNER)
                        src = qk[b][:, part].rearrange("p (h d) -> p h d", d=DH)
                        swapped = qk[b][:, part].rearrange("p (h s d) -> p h s d", s=2, d=DH // 2)[:, :, ::-1, :]
                        v.tensor_tensor(t2[:, part].rearrange("p (h s d) -> p h s d", s=2, d=DH // 2), swapped,
                                        tab[:, 2 * k + 1:2 * k + 2, :].rearrange("p o (s d) -> p o s d", s=2)
                                        .broadcast_to([P, HEADS, 2, DH // 2]), ALU.mult).then_inc(rotated[b], 1)
                        dve.wait_ge(rotated[b], 4 * i + 2 * k + 1)
                        v.tensor_tensor(src, src, tab[:, 2 * k:2 * k + 1, :].broadcast_to([P, HEADS, DH]),
                                        ALU.mult).then_inc(rotated[b], 1)
                    dve.wait_ge(y0_ready[b], i + 1)
                    wait_prev(dve, qk_ready[b], 2 * i, i)
                    v.tensor_tensor(rinv[b][:, :], y0[b][:, :], y0[b][:, :], ALU.mult).then_inc(newton[b], 1)
                    dve.wait_ge(newton[b], 3 * i + 1)
                    v.tensor_tensor(rinv[b][:, :], rinv[b][:, :], ss[b][:, :], ALU.mult).then_inc(newton[b], 1)
                    dve.wait_ge(newton[b], 3 * i + 2)
                    v.tensor_scalar(rinv[b][:, :], rinv[b][:, :], -0.5, 1.5, ALU.mult, ALU.add).then_inc(newton[b], 1)
                    dve.wait_ge(newton[b], 3 * i + 3)
                    v.tensor_tensor(rinv[b][:, :], rinv[b][:, :], y0[b][:, :], ALU.mult).then_inc(rinv_ready[b], 1)

                def evac_q(j, b):
                    if b:
                        wait_prev(dve, s_full, 2 * j, j)
                    else:
                        wait_prev(dve, s_full, 2 * j - 1, j)
                    v.tensor_tensor(kT[b][:, :, 0:WINDOW], kT[b][:, :, P:P + WINDOW],
                                    first[:, bass.ds(tile_of(j), 1), :].broadcast_to([P, HP, WINDOW]),
                                    ALU.mult).then_inc(k_carried[b], 1)
                    for k in range(2):
                        bank, n = tr_fill(j, 4 * b + k)
                        dve.wait_ge(tr_full[bank], n)
                        v.tensor_copy(qbd[b][DH:P, 4 * k:4 * k + 4, :, 1, :],
                                      ps_tr[bank][DH:P, :].rearrange("p (m w q) -> p m w q", m=4, w=4)).then_inc(tr_done[bank], 1)

                def shift_scores(j, b):
                    dve.wait_ge(s_full, 2 * j + b + 1)
                    bank, n = tr_fill(j - 1, 8 + 2 * b + 1)
                    wait_prev(dve, tr_full[bank], n, j)
                    flat = pr[b][:, :, :, :].rearrange("p m u k -> p m (u k)")
                    v.tensor_tensor(flat, ps_s[:, :, :, :].rearrange("p m u k -> p m (u k)"),
                                    mask[:, bass.ds(tile_of(j), 1), :].broadcast_to([P, HP, P]), ALU.add).then_inc(s_read, 1)
                    dve.wait_ge(s_read, 2 * j + b + 1)
                    rows = pr[b][:, :, :, :].rearrange("p m u k -> p (m u) k")
                    v.tensor_reduce(rmax[b][:, :], rows, AX.X, ALU.max).then_inc(max_ready[b], 1)
                    dve.wait_ge(max_ready[b], j + 1)
                    v.tensor_tensor(rows, rows, rmax[b][:, :].unsqueeze(2).broadcast_to([P, 2 * HP, 2 * WINDOW]),
                                    ALU.subtract).then_inc(shifted[b], 1)

                def row_sums(j, b):
                    dve.wait_ge(exp_ready[b], j + 1)
                    v.tensor_reduce(rsum[b][:, :], pr[b][:, :, :, :].rearrange("p m u k -> p (m u) k"), AX.X,
                                    ALU.add).then_inc(sum_ready[b], 1)
                    dve.wait_ge(sum_ready[b], j + 1)
                    wait_prev(dve, probs_ready[b], j, j)
                    v.reciprocal(rrec[b][:, :], rsum[b][:, :]).then_inc(rec_ready[b], 1)

                def evac_attend(j, b):
                    bank, n = pv_fill(j - 1, 5 * b + 3)
                    wait_prev(dve, pv_full[bank], n, j)
                    for k in range(2):
                        bank, n = tr_fill(j, 8 + 2 * b + k)
                        dve.wait_ge(tr_full[bank], n)
                        v.tensor_copy(pbd[b][DH:P, 4 * k:4 * k + 4, :, :, 1, :].rearrange("p m a h q -> p (m a h) q"),
                                      ps_tr[bank][DH:P, :].rearrange("p (x q) -> p x q", q=WINDOW)).then_inc(tr_done[bank], 1)
                    bank, n = pv_fill(j - 1, 5 * b + 4)
                    wait_prev(dve, pv_full[bank], n, j)
                    for k in range(4):
                        bank, n = pv_fill(j, 5 * b + k)
                        dve.wait_ge(pv_full[bank], n)
                        v.tensor_copy(oT[b][DH:P, 2 * k:2 * k + 2, :, :].rearrange("p m a c -> p (m a) c"),
                                      ps_pv[bank][DH:P, :].rearrange("p (x h c) -> p x h c", h=2, c=DH)[:, :, 1, :]
                                      ).then_inc(pv_done[bank], 1)
                    bank, n = pv_fill(j, 5 * b + 4)
                    dve.wait_ge(pv_full[bank], n)
                    v.tensor_tensor(xmid[:, b, cols(j, 1)].rearrange("p (u a q) -> p a u q", u=2, a=2),
                                    ps_pv[bank][:, 0:P].rearrange("p (a u q) -> p a u q", u=2, a=2),
                                    x[:, b, cols(j, 1)].rearrange("p (u a q) -> p a u q", u=2, a=2),
                                    ALU.add).then_inc(pv_done[bank], 2)

                def ffn_shift(i, n):
                    for b in range(B):
                        bank, k = pv_fill(n, 5 * b + 4)
                        dve.wait_ge(pv_done[bank], k * 2)
                    v.tensor_copy(fx[0:64, :, :], xmid[0:64, :, cols(n, 1)])
                    v.tensor_copy(fx[64:P, :, :], xmid[64:P, :, cols(n, 0)]).then_inc(fx_ready, 1)

                def ffn_centre(i, n):
                    bank, k = qn_fill(i, "mean")
                    dve.wait_ge(qn_full[bank], k)
                    dve.wait_ge(fx_ready, n + 1)
                    v.tensor_tensor(fc[:, :, :].rearrange("p b t -> p (b t)"), fx[:, :, :].rearrange("p b t -> p (b t)"),
                                    ps_qn[bank][:, 0:B * P], ALU.subtract).then_inc(qn_done[bank], 1)

                def ffn_variance(i, n):
                    bank, k = qn_fill(i, "var")
                    dve.wait_ge(qn_full[bank], k)
                    v.tensor_scalar(fv[:, :, :].rearrange("p b t -> p (b t)"), ps_qn[bank][:, 0:B * P], LN_EPS, None,
                                    ALU.add).then_inc(qn_done[bank], 1)

                def ffn_normalise(i, n):
                    dve.wait_ge(fy_ready, n + 1)
                    v.tensor_tensor(fn[:, :, :], fy[:, :, :], fy[:, :, :], ALU.mult).then_inc(fnewton, 1)
                    dve.wait_ge(fnewton, 5 * n + 1)
                    v.tensor_tensor(fn[:, :, :], fn[:, :, :], fv[:, :, :], ALU.mult).then_inc(fnewton, 1)
                    dve.wait_ge(fnewton, 5 * n + 2)
                    v.tensor_scalar(fn[:, :, :], fn[:, :, :], -0.5, 1.5, ALU.mult, ALU.add).then_inc(fnewton, 1)
                    dve.wait_ge(fnewton, 5 * n + 3)
                    v.tensor_tensor(fn[:, :, :], fn[:, :, :], fy[:, :, :], ALU.mult).then_inc(fnewton, 1)
                    dve.wait_ge(fnewton, 5 * n + 4)
                    v.tensor_tensor(fxn[:, :, :], fc[:, :, :], fn[:, :, :], ALU.mult).then_inc(fnewton, 1)
                    dve.wait_ge(fnewton, 5 * n + 5)
                    dve.wait_ge(ffn_in, (layer_of(n) + 1) * 64)
                    v.tensor_scalar(fxn[:, :, :], fxn[:, :, :], small[:, SM_G:SM_G + 1], small[:, SM_B:SM_B + 1],
                                    ALU.mult, ALU.add).then_inc(fxn_ready, 1)

                def ffn_gate(i, n):
                    for c, (r, m) in enumerate(FF_CHUNKS):
                        bank, k = qn_fill(i, ("up", c))
                        dve.wait_ge(gel_ready, 3 * n + c + 1)
                        v.scalar_tensor_tensor(hid[0:m, c, :, :].rearrange("p b t -> p (b t)"), ps_qn[bank][0:m, 0:B * P],
                                               small[0:m, SM_VAL + c:SM_VAL + c + 1],
                                               gel[0:m, :, :].rearrange("p b t -> p (b t)"),
                                               ALU.add, ALU.mult).then_inc(qn_done[bank], 1)

                def ffn_out(i, n):
                    bank, k = qn_fill(i, "down")
                    dve.wait_ge(qn_full[bank], k)
                    v.scalar_tensor_tensor(x[:, :, cols(n, 1)], ps_qn[bank][:, 0:B * P].rearrange("p (b t) -> p b t", b=B),
                                           small[:, SM_B2:SM_B2 + 1], xmid[:, :, cols(n, 1)],
                                           ALU.add, ALU.add).then_inc(qn_done[bank], 1)

                def body(i, front, attention, ffn):
                    j, n = i - 1, i - 2
                    if front:
                        shift_in(i, 0)
                        shift_in(i, 1)
                    if attention:
                        evac_q(j, 0)
                        evac_q(j, 1)
                    if ffn:
                        ffn_shift(i, n)
                        ffn_centre(i, n)
                    if attention:
                        shift_scores(j, 0)
                    if ffn:
                        ffn_variance(i, n)
                    if attention:
                        shift_scores(j, 1)
                        row_sums(j, 0)
                    if front:
                        rotate(i, 0)
                    if ffn:
                        ffn_normalise(i, n)
                    if attention:
                        row_sums(j, 1)
                        evac_attend(j, 0)
                    if ffn:
                        ffn_gate(i, n)
                        ffn_out(i, n)
                    if front:
                        rotate(i, 1)
                    if attention:
                        evac_attend(j, 1)

                for b in range(B):
                    v.memset(qbd[b][:, :, :, :, :], 0.0)
                    v.memset(kT[b][:, :, :], 0.0)
                    v.memset(pbd[b][:, :, :, :, :, :], 0.0)
                    v.memset(v_own[b][:, :], 0.0)
                    v.memset(v_back[b][:, :], 0.0)
                v.memset(xmid[:, :, 0:1], 0.0)
                v.memset(mean_w[:, :], 1.0 / DIM).then_inc(cleared, 1)
                dve.wait_ge(cleared, 1)
                dve.wait_ge(consts, 64)
                steps(dve, body)
                bank, n = qn_fill(STEPS + 1, "down")
                dve.wait_ge(qn_done[bank], n)

            @block.gpsimd
            def _(pool):
                g = nc.gpsimd

                def tables(i):
                    wait_prev(pool, rotated[1], 4 * i, i)
                    g.tensor_tensor(tab[:, :, :].rearrange("p k d -> p (k d)").unsqueeze(1),
                                    rot[:, bass.ds(tile_of(i), 1), :], scales[:, bass.ds(layer_of(i), 1), :],
                                    ALU.mult).then_inc(tab_ready, 1)

                def add_scale(i, b):
                    if not (isinstance(i, int) and i == 0):
                        for k in (2, 3):
                            bank, n = tr_fill(i - 1, 4 * b + k)
                            pool.wait_ge(tr_full[bank], n)
                    for k in range(2):
                        part = slice(k * INNER, (k + 1) * INNER)
                        pool.wait_ge(rotated[b], 4 * i + 2 * k + 2)
                        g.tensor_tensor(qkr[b][:, part], qk[b][:, part], t2[:, part], ALU.add).then_inc(added[b], 1)
                    pool.wait_ge(rinv_ready[b], i + 1)
                    for k in range(2):
                        pool.wait_ge(added[b], 2 * i + k + 1)
                        part = qkr[b][:, k * INNER:(k + 1) * INNER].rearrange("p (h d) -> p h d", d=DH)
                        g.tensor_tensor(part, part, rinv[b][:, k * HEADS:(k + 1) * HEADS].unsqueeze(2)
                                        .broadcast_to([P, HEADS, DH]), ALU.mult).then_inc(qk_ready[b], 1)

                def scale_probs(j, b):
                    pool.wait_ge(rec_ready[b], j + 1)
                    rows = pr[b][:, :, :, :].rearrange("p m u k -> p (m u) k")
                    g.tensor_tensor(rows, rows, rrec[b][:, :].unsqueeze(2).broadcast_to([P, 2 * HP, 2 * WINDOW]),
                                    ALU.mult).then_inc(probs_ready[b], 1)

                def body(i, front, attention, ffn):
                    j = i - 1
                    if front:
                        tables(i)
                    if attention:
                        scale_probs(j, 0)
                    if front:
                        add_scale(i, 0)
                    if attention:
                        scale_probs(j, 1)
                    if front:
                        add_scale(i, 1)

                pool.wait_ge(consts, 64)
                steps(pool, body)


def combine(nc, a, x, branch, ident):
    with ExitStack() as ctx:
        def sem(name):
            return ctx.enter_context(nc.semaphore(name))

        NT = B * TILES
        sig = ctx.enter_context(nc.sbuf_tensor("sig", [P, B, SEQ], F32))
        xin = ctx.enter_context(nc.sbuf_tensor("xin", [P, NT, DIM], F32))
        out = ctx.enter_context(nc.sbuf_tensor("outs", [P, NT, DIM], F32))
        ps = ctx.enter_context(nc.psum_tensor("ps_out", [P, 4, COLS], F32))
        xin_in, sig_ready, silu_ready, prod_ready, tr_full, sum_ready, out_sent = map(sem, (
            "c_input", "c_sigmoid", "c_silu", "c_product", "c_transposed", "c_sum", "c_out"))
        with nc.Block() as block:
            @block.sync
            def _(sp):
                sp.dma_start(xin[:, :, :], a["x"].rearrange("b (t p) d -> p (b t) d", p=P)).then_inc(xin_in, 16)
                for q in range(4):
                    sp.wait_ge(sum_ready, q + 1)
                    sp.dma_start(a["out"].rearrange("b (t p) d -> p (b t) d", p=P)[:, 4 * q:4 * q + 4, :],
                                 out[:, 4 * q:4 * q + 4, :]).then_inc(out_sent, 16)
                sp.wait_ge(out_sent, 64)

            @block.scalar
            def _(act):
                for b in range(B):
                    nc.scalar.activation(sig[:, b, :], x[:, b, 1:1 + SEQ], ACT.Sigmoid).then_inc(sig_ready, 1)

            @block.vector
            def _(dve):
                for b in range(B):
                    dve.wait_ge(sig_ready, b + 1)
                    nc.vector.tensor_tensor(sig[:, b, :], sig[:, b, :], x[:, b, 1:1 + SEQ], ALU.mult).then_inc(silu_ready, 1)
                    dve.wait_ge(silu_ready, b + 1)
                    nc.vector.tensor_tensor(sig[:, b, :], sig[:, b, :], branch[:, b, :], ALU.mult).then_inc(prod_ready, 1)
                dve.wait_ge(xin_in, 16)
                for q in range(4):
                    dve.wait_ge(tr_full, q + 1)
                    nc.vector.tensor_tensor(out[:, 4 * q:4 * q + 4, :].rearrange("p t d -> p (t d)"), ps[:, q, :],
                                            xin[:, 4 * q:4 * q + 4, :].rearrange("p t d -> p (t d)"), ALU.add).then_inc(sum_ready, 1)

            @block.tensor
            def _(pe):
                for t in range(NT):
                    b, k = t // TILES, t % TILES
                    if k == 0:
                        pe.wait_ge(prod_ready, b + 1)
                    m = nc.tensor.transpose(ps[:, t // 4, (t % 4) * P:(t % 4 + 1) * P], sig[:, b, k * P:(k + 1) * P], ident[:, :])
                    if t % 4 == 3:
                        m.then_inc(tr_full, 1)


def rotary_constants():
    f = np.float32
    half = np.arange(0, DH, 2, dtype=f)
    inv_freq = (f(1.0) / np.power(f(10000.0), half / f(DH))).astype(f)
    t = np.arange(SEQ, dtype=f)
    freqs = (t[:, None] * inv_freq[None, :]).astype(f)
    base = ((half + f(0.4 * DH)) / f(1.4 * DH)).astype(f)
    power = ((t - f(SEQ // 2)) / f(WINDOW // 2)).astype(f)
    scale = np.power(base[None, :], power[:, None]).astype(f)
    cos, sin, inv = np.cos(freqs), np.sin(freqs), (f(1.0) / scale)
    parts = []
    for s in (scale, inv):
        c, n = cos * s, sin * s
        parts += [c, c, -n, n]
    tab = np.concatenate(parts, 1).astype(f)
    return np.ascontiguousarray(tab.reshape(TILES, P, 4 * DH).transpose(1, 0, 2))


def mask_constants():
    m = np.full((2, 2, WINDOW, TILES, 2, 2 * WINDOW), MASKED, np.float32)
    q = np.arange(WINDOW)[:, None]
    k = np.arange(2 * WINDOW)[None, :]
    ok = (k >= q) & (k <= q + WINDOW)
    for par in range(2):
        for t in range(TILES):
            for u in range(2):
                valid = ok & ((k >= WINDOW) if t == 0 and u == 0 and par == 0 else True)
                m[par, :, :, t, u, :] = np.where(valid, 0.0, MASKED)
    return m.reshape(P, TILES, P)


def kernel(L0_attn_x, L0_attn_W_in, L0_attn_conv_w, L0_attn_conv_b, L0_attn_W_gates, L0_attn_b_gates,
           L0_attn_forget_base, L0_attn_W_out, L0_ffn_Wqkv, L0_ffn_q_scale, L0_ffn_k_scale, L0_ffn_Wo, L0_ffn_ln_g,
           L0_ffn_ln_b, L0_ffn_W1, L0_ffn_b1, L0_ffn_W2, L0_ffn_b2):
    import concourse.bacc as bacc
    from concourse.bass_utils import run_bass_kernel_spmd

    def arr(v):
        return np.ascontiguousarray(v)

    by_channel = np.stack([*np.asarray(L0_attn_conv_w).T, np.asarray(L0_attn_conv_b),
                           *np.asarray(L0_attn_b_gates).reshape(2, HIDDEN), np.asarray(L0_attn_forget_base)], 1)
    rec_par = np.stack([by_channel[0:HID_LO], np.concatenate([by_channel[HID_LO:], by_channel[HID_LO:]])], 1)
    qs, ks = np.asarray(L0_ffn_q_scale), np.asarray(L0_ffn_k_scale)
    swap = np.r_[DH // 2:DH, 0:DH // 2]
    scales = np.concatenate([qs, qs[:, swap], ks, ks[:, swap]], 1).reshape(-1)
    small = np.zeros((DEPTH, P, SMALL), np.float32)
    small[:, :, SM_G], small[:, :, SM_B], small[:, :, SM_B2] = np.asarray(L0_ffn_ln_g), np.asarray(L0_ffn_ln_b), np.asarray(L0_ffn_b2)
    b1 = np.asarray(L0_ffn_b1)
    for c, (r, m) in enumerate(FF_CHUNKS):
        small[:, 0:m, SM_VAL + c] = b1[:, r:r + m]
        small[:, 0:m, SM_GATE + c] = b1[:, FF + r:FF + r + m]
    first = np.ones((P, TILES, WINDOW), np.float32)
    first[:, 0, :] = 0.0
    arrays = {
        "x": arr(L0_attn_x), "w_in_t": arr(np.asarray(L0_attn_W_in).T), "w_gates_t": arr(np.asarray(L0_attn_W_gates).T),
        "w_out_t": arr(np.asarray(L0_attn_W_out).T), "rec_par": arr(rec_par), "Wqkv": arr(L0_ffn_Wqkv), "Wo": arr(L0_ffn_Wo),
        "W1": arr(L0_ffn_W1), "W2": arr(L0_ffn_W2), "scales": arr(scales), "small": small,
        "rot": rotary_constants(), "mask": mask_constants(), "first": first, "ident": np.eye(P, dtype=np.float32),
    }
    nc = bacc.Bacc("TRN2", target_bir_lowering=False, num_devices=1)
    aps = {n: nc.dram_tensor(f"in_{n}", v.shape, F32, kind="ExternalInput").ap() for n, v in arrays.items()}
    aps["out"] = nc.dram_tensor("out", (B, SEQ, DIM), F32, kind="ExternalOutput").ap()
    build(nc, aps)
    r = run_bass_kernel_spmd(nc, [{f"in_{n}": v for n, v in arrays.items()}], core_ids=[0])
    return r.results[0]["out"]
```

```python
import math
from contextlib import ExitStack

import numpy as np

import concourse.bass as bass
from concourse import mybir

F32 = mybir.dt.float32
I32 = mybir.dt.int32
ALU = mybir.AluOpType
ACT = mybir.ActivationFunctionType
AX = mybir.AxisListType

P = 128
B, SEQ, DIM = 2, 1024, 128
TILES = SEQ // P
HIDDEN, CONV_K = 192, 4
HID_LO, HID_HI = P, HIDDEN - P
DEPTH, HEADS, DH, WINDOW = 6, 16, 64, 32
INNER = HEADS * DH
HP = HEADS // 2
FF = int(DIM * 4 * 2 / 3)
FF_CHUNKS = [(c, min(P, FF - c)) for c in range(0, FF, P)]
QK_SCALE = 8.0
MASKED = -1e30
LN_EPS = 1e-5
NORM_FLOOR_SQ = 1e-24
STEPS = DEPTH * TILES
LOOP = 6
DRAIN = 5
COLS = 512

SM_G, SM_B, SM_B2, SM_VAL, SM_GATE = 0, 1, 2, 3, 6
SMALL = 9


def valid(step):
    return not isinstance(step, int) or 0 <= step < STEPS


def qn_order(i):
    order = []
    for b in range(B):
        if valid(i):
            order += [("qkv", b, 0), ("qkv", b, 1)]
        if b == 0 and valid(i - 3):
            order += ["centre"]
        if valid(i):
            order += [("qkv", b, 2), ("qkv", b, 3)]
        if b == 1 and valid(i - 4):
            order += [("up", 0), ("up", 1)]
        if valid(i):
            order += [("qkv", b, 4), ("qkv", b, 5)]
        if b == 1 and valid(i - 4):
            order += [("up", 2)]
    return order


def tr_order(i):
    order = []
    for b in range(B):
        if valid(i - 2):
            order += [("probs", b, f) for f in range(2)]
        if valid(i - 1):
            order += [("qk", b, f) for f in range(4)]
    return order


def pv_order(i):
    order = []
    for b in range(B):
        if valid(i - 2):
            order += [("pv", b, f) for f in range(4)]
        if valid(i - 2) or valid(i - 3) or (b == 0 and valid(i - 5)):
            order += [("out", b)]
    return order


def fill(order, i, what):
    if isinstance(i, int):
        n = sum(len(order(k)) for k in range(i)) + order(i).index(what)
        return n % 2, n // 2 + 1
    full = order(LOOP)
    n = sum(len(order(k)) for k in range(LOOP)) + full.index(what)
    return n % 2, (i - LOOP) * (len(full) // 2) + (n // 2 + 1)


def exists(order, i, what):
    return not isinstance(i, int) or (i >= 0 and what in order(i))


def build(nc, a):
    with ExitStack() as ctx:
        def sb(name, shape, dt=F32):
            return ctx.enter_context(nc.sbuf_tensor(name, shape, dt))

        def sem(name):
            return ctx.enter_context(nc.semaphore(name))

        x = sb("x", [P, B, 1 + SEQ])
        xmid = sb("xmid", [P, B, 1 + SEQ])
        branch = sb("branch", [P, B, SEQ])
        ident = sb("ident", [P, P])
        eps_col = sb("eps_col", [P, 1])
        s_const = sem("const_loaded")

        recurrent_branch(nc, a, x, branch, ident, eps_col, s_const)
        layers(nc, a, x, xmid, ident)
        combine(nc, a, x, branch, ident)


def recurrent_branch(nc, a, x, branch, ident, eps_col, s_const):
    with ExitStack() as ctx:
        def sb(name, shape, dt=F32):
            return ctx.enter_context(nc.sbuf_tensor(name, shape, dt))

        def sem(name):
            return ctx.enter_context(nc.semaphore(name))

        NT = B * TILES
        xt = sb("xt", [P, NT, DIM])
        stats = sb("stats", [P, NT, 6])
        mv = sb("mv", [P, NT, 2])
        lnv = sb("lnv", [P, NT])
        rstd = sb("rstd", [P, NT])
        nw = sb("nw", [P, NT])
        ve = sb("ve", [P, NT])
        w_in = sb("w_in", [P, 2 * HIDDEN])
        wg_lo = sb("wg_lo", [P, 2 * HIDDEN])
        wg_hi = sb("wg_hi", [P, 2 * HIDDEN])
        wo_lo = sb("wo_lo", [P, DIM])
        wo_hi = sb("wo_hi", [P, DIM])
        par = sb("par", [P, 2, 8])
        c8 = sb("c8", [P, 2, 1])
        one_col = sb("one_col", [P, 1])
        tmp = [sb(f"sp{i}", [P, 2, 1]) for i in range(8)]
        xh = sb("xh", [P, 3, CONV_K - 1 + SEQ])
        y = sb("y", [P, 3, SEQ])
        alpha = sb("alpha", [P, 3, SEQ])
        sig_in = sb("sig_in", [P, 3, SEQ])
        beta = sb("beta", [P, 3, SEQ])
        gate = sb("gate", [P, 3, SEQ])
        ps = ctx.enter_context(nc.psum_tensor("ps_rec", [P, 8, COLS], F32))

        s_x, s_w, s_set = sem("r_x"), sem("r_w"), sem("r_set")
        s_st, s_ve, s_ln, s_y0, s_nw, s_xn = sem("r_stats"), sem("r_var"), sem("r_lnv"), sem("r_rstd0"), sem("r_newton"), sem("r_xn")
        s_tr, s_xT = sem("r_transposed"), sem("r_xT")
        s_sp, s_spe = sem("r_softplus"), sem("r_softplus_exp")
        s_pe = sem("r_phase_done")
        s_xh, s_conv, s_f, s_i, s_al, s_a2, s_be, s_g = (sem("r_xh"), sem("r_conv"), sem("r_forget"), sem("r_input"),
                                                         sem("r_alpha"), sem("r_alpha_sq"), sem("r_beta"), sem("r_gate"))
        s_dr, s_h = sem("r_drive"), sem("r_h")
        s_out = sem("r_branch")

        def bank(g, half):
            return 2 * g + half

        def proj(pe, lhs_of, first):
            pass

        with nc.Block() as block:
            @block.sync
            def _(sp):
                sp.dma_start(xt[:, :, :], a["x"].rearrange("b (t p) d -> p (b t) d", p=P)).then_inc(s_x, 16)
                sp.dma_start(ident[:, :], a["ident"]).then_inc(s_const, 16)
                sp.dma_start(w_in[:, :], a["w_in_t"]).then_inc(s_w, 16)
                sp.dma_start(par[:, :, :], a["rec_par"]).then_inc(s_w, 16)
                sp.dma_start(wg_lo[:, :], a["w_gates_t"][0:HID_LO, :]).then_inc(s_w, 16)
                sp.dma_start(wg_hi[0:HID_HI, :], a["w_gates_t"][HID_LO:HIDDEN, :]).then_inc(s_w, 16)
                sp.dma_start(wg_hi[HID_HI:P, :], a["w_gates_t"][HID_LO:HIDDEN, :]).then_inc(s_w, 16)
                sp.dma_start(wo_lo[:, :], a["w_out_t"][0:HID_LO, :]).then_inc(s_w, 16)
                sp.dma_start(wo_hi[0:HID_HI, :], a["w_out_t"][HID_LO:HIDDEN, :]).then_inc(s_w, 16)
                sp.dma_start(wo_hi[HID_HI:P, :], a["w_out_t"][HID_LO:HIDDEN, :]).then_inc(s_w, 16)
                sp.wait_ge(s_w, 8 * 16)
                sp.wait_ge(s_const, 16)

            @block.gpsimd
            def _(pool):
                nc.gpsimd.memset(eps_col[:, :], LN_EPS).then_inc(s_set, 1)
                nc.gpsimd.memset(one_col[:, :], 1e-6).then_inc(s_set, 1)
                nc.gpsimd.memset(xh[:, :, 0:CONV_K - 1], 0.0).then_inc(s_set, 1)
                nc.gpsimd.memset(x[:, :, 0:1], 0.0).then_inc(s_set, 1)

            @block.vector
            def _(dve):
                v = nc.vector
                dve.wait_ge(s_x, 16)
                for t in range(NT):
                    v.bn_stats(stats[:, t, :], xt[:, t, :]).then_inc(s_st, 1)
                dve.wait_ge(s_st, NT)
                for t in range(NT):
                    v.bn_aggr(mv[:, t, :], stats[:, t, :]).then_inc(s_st, 1)
                dve.wait_ge(s_st, 2 * NT)
                v.tensor_scalar(ve[:, :], mv[:, :, 1], LN_EPS, None, ALU.add).then_inc(s_ve, 1)
                dve.wait_ge(s_y0, 1)
                v.tensor_tensor(nw[:, :], rstd[:, :], rstd[:, :], ALU.mult).then_inc(s_nw, 1)
                dve.wait_ge(s_nw, 1)
                v.tensor_tensor(nw[:, :], nw[:, :], ve[:, :], ALU.mult).then_inc(s_nw, 1)
                dve.wait_ge(s_nw, 2)
                v.tensor_scalar(nw[:, :], nw[:, :], -0.5, 1.5, ALU.mult, ALU.add).then_inc(s_nw, 1)
                dve.wait_ge(s_nw, 3)
                v.tensor_tensor(rstd[:, :], rstd[:, :], nw[:, :], ALU.mult).then_inc(s_nw, 1)
                dve.wait_ge(s_nw, 4)
                for t in range(NT):
                    v.tensor_scalar(xt[:, t, :], xt[:, t, :], mv[:, t, 0:1], rstd[:, t:t + 1],
                                    ALU.subtract, ALU.mult).then_inc(s_xn, 1)
                dve.wait_ge(s_w, 8 * 16)
                n = 0
                fb = par[:, :, 7:8]

                def link(ins):
                    nonlocal n
                    n += 1
                    ins.then_inc(s_sp, 1)
                    dve.wait_ge(s_sp, n)

                link(v.tensor_scalar(tmp[0][:, :, :], fb, -1.0, None, ALU.mult))
                link(v.tensor_tensor(tmp[0][:, :, :], tmp[0][:, :, :], fb, ALU.max))
                dve.wait_ge(s_spe, 1)
                e = tmp[1]
                link(v.tensor_scalar(tmp[2][:, :, :], e[:, :, :], 2.0, None, ALU.add))
                link(v.reciprocal(tmp[3][:, :, :], tmp[2][:, :, :]))
                link(v.tensor_tensor(tmp[3][:, :, :], tmp[3][:, :, :], e[:, :, :], ALU.mult))
                link(v.tensor_tensor(tmp[4][:, :, :], tmp[3][:, :, :], tmp[3][:, :, :], ALU.mult))
                link(v.tensor_scalar(tmp[5][:, :, :], tmp[4][:, :, :], 1.0 / 17, 1.0 / 15, ALU.mult, ALU.add))
                for k in (13, 11, 9, 7, 5, 3, 1):
                    link(v.tensor_tensor(tmp[5][:, :, :], tmp[5][:, :, :], tmp[4][:, :, :], ALU.mult))
                    link(v.tensor_scalar(tmp[5][:, :, :], tmp[5][:, :, :], 1.0 / k, None, ALU.add))
                link(v.tensor_tensor(tmp[5][:, :, :], tmp[5][:, :, :], tmp[3][:, :, :], ALU.mult))
                link(v.tensor_scalar(tmp[6][:, :, :], fb, 0.0, None, ALU.max))
                link(v.tensor_scalar(tmp[5][:, :, :], tmp[5][:, :, :], 2.0, None, ALU.mult))
                link(v.tensor_tensor(tmp[6][:, :, :], tmp[6][:, :, :], tmp[5][:, :, :], ALU.add))
                link(v.tensor_scalar(c8[:, :, :], tmp[6][:, :, :], -8.0, None, ALU.mult))
                for t in range(0, NT, 4):
                    dve.wait_ge(s_tr, t // 4 + 1)
                    v.tensor_copy(x[:, t // TILES, 1 + (t % TILES) * P:1 + (t % TILES + 4) * P],
                                  ps[:, t // 4, :]).then_inc(s_xT, 1)
                for g in range(3):
                    dve.wait_ge(s_xh, g + 1)
                    pg = g // 2
                    for k in range(CONV_K):
                        src = xh[:, g, k:k + SEQ]
                        if k == 0:
                            v.tensor_scalar(y[:, g, :], src, par[:, pg, 0:1], par[:, pg, 4:5],
                                            ALU.mult, ALU.add).then_inc(s_conv, 1)
                        else:
                            dve.wait_ge(s_conv, CONV_K * g + k)
                            v.scalar_tensor_tensor(y[:, g, :], src, par[:, pg, k:k + 1], y[:, g, :],
                                                   ALU.mult, ALU.add).then_inc(s_conv, 1)
                for g in range(3):
                    dve.wait_ge(s_al, g + 1)
                    v.tensor_tensor(beta[:, g, :], alpha[:, g, :], alpha[:, g, :], ALU.mult).then_inc(s_a2, 1)
                    dve.wait_ge(s_a2, 2 * g + 1)
                    v.tensor_scalar(beta[:, g, :], beta[:, g, :], -1.0, 1.0, ALU.mult, ALU.add).then_inc(s_a2, 1)
                for g in range(3):
                    dve.wait_ge(s_i, g + 1)
                    v.tensor_tensor(y[:, g, :], y[:, g, :], sig_in[:, g, :], ALU.mult).then_inc(s_dr, 1)
                for g in range(3):
                    dve.wait_ge(s_be, g + 1)
                    dve.wait_ge(s_dr, 3 + g)
                    v.tensor_tensor(y[:, g, :], y[:, g, :], beta[:, g, :], ALU.mult).then_inc(s_dr, 1)
                for g in range(3):
                    dve.wait_ge(s_dr, 4 + g)
                    v.tensor_tensor_scan(sig_in[:, g, :], alpha[:, g, :], y[:, g, :], 0.0,
                                         ALU.mult, ALU.add).then_inc(s_h, 1)
                for g in range(3):
                    dve.wait_ge(s_h, 3 + g)
                    dve.wait_ge(s_g, g + 1)
                    v.tensor_tensor(gate[:, g, :], gate[:, g, :], sig_in[:, g, :], ALU.mult).then_inc(s_h, 1)
                for q in range(4):
                    dve.wait_ge(s_pe, 5)
                    v.tensor_copy(branch[:, q // 2, (q % 2) * COLS:(q % 2 + 1) * COLS], ps[:, q, :]).then_inc(s_out, 1)
                dve.wait_ge(s_out, 4)

            @block.scalar
            def _(act):
                s = nc.scalar
                act.wait_ge(s_ve, 1)
                act.wait_ge(s_set, 4)
                s.activation(lnv[:, :], ve[:, :], ACT.Ln).then_inc(s_ln, 1)
                act.wait_ge(s_ln, 1)
                s.activation(rstd[:, :], lnv[:, :], ACT.Exp, scale=-0.5).then_inc(s_y0, 1)
                act.wait_ge(s_sp, 2)
                s.activation(tmp[1][:, :, :], tmp[0][:, :, :], ACT.Exp, scale=-1.0).then_inc(s_spe, 1)
                act.wait_ge(s_pe, 1)
                for g in range(3):
                    s.activation(xh[:, g, CONV_K - 1:CONV_K - 1 + SEQ],
                                 ps[:, 2 * g:2 * g + 2, :].rearrange("p a b -> p (a b)"), ACT.Copy).then_inc(s_xh, 1)
                act.wait_ge(s_pe, 2)
                for g in range(3):
                    s.activation(alpha[:, g, :], ps[:, 2 * g:2 * g + 2, :].rearrange("p a b -> p (a b)"), ACT.Sigmoid,
                                 bias=par[:, g // 2, 5:6], scale=1.0).then_inc(s_f, 1)
                act.wait_ge(s_pe, 3)
                for g in range(3):
                    s.activation(sig_in[:, g, :], ps[:, 2 * g:2 * g + 2, :].rearrange("p a b -> p (a b)"), ACT.Sigmoid,
                                 bias=par[:, g // 2, 6:7], scale=1.0).then_inc(s_i, 1)
                act.wait_ge(s_sp, 26)
                for g in range(3):
                    act.wait_ge(s_f, g + 1)
                    s.activation(alpha[:, g, :], alpha[:, g, :], ACT.Exp, scale=c8[:, g // 2, :]).then_inc(s_al, 1)
                for g in range(3):
                    act.wait_ge(s_a2, 2 * g + 2)
                    s.activation(beta[:, g, :], beta[:, g, :], ACT.Sqrt, bias=one_col[:, :], scale=1.0).then_inc(s_be, 1)
                act.wait_ge(s_pe, 4)
                for g in range(3):
                    s.activation(gate[:, g, :], ps[:, 2 * g:2 * g + 2, :].rearrange("p a b -> p (a b)"),
                                 ACT.Gelu).then_inc(s_g, 1)

            @block.tensor
            def _(pe):
                pe.wait_ge(s_const, 16)
                for t in range(NT):
                    pe.wait_ge(s_xn, t + 1)
                    m = nc.tensor.transpose(ps[:, t // 4, (t % 4) * P:(t % 4 + 1) * P], xt[:, t, :], ident[:, :])
                    if t % 4 == 3:
                        m.then_inc(s_tr, 1)
                pe.wait_ge(s_xT, 4)
                pe.wait_ge(s_w, 8 * 16)

                def from_x(c0):
                    for half in range(2):
                        for b in range(B):
                            rhs = x[:, b, 1 + half * COLS:1 + (half + 1) * COLS]
                            nc.tensor.matmul(ps[:, bank(b, half), :], w_in[:, c0:c0 + HID_LO], rhs, start=True, stop=True)
                            m = nc.tensor.matmul(ps[HID_HI * b:HID_HI * (b + 1), bank(2, half), :],
                                                 w_in[:, c0 + HID_LO:c0 + HIDDEN], rhs, start=True, stop=True)
                    m.then_inc(s_pe, 1)

                def from_y(c0):
                    for half in range(2):
                        cols = slice(half * COLS, (half + 1) * COLS)
                        for b in range(B):
                            hi = slice(HID_HI * b, HID_HI * (b + 1))
                            for out, m0, m1 in ((ps[:, bank(b, half), :], c0, c0 + HID_LO),
                                                (ps[hi, bank(2, half), :], c0 + HID_LO, c0 + HIDDEN)):
                                nc.tensor.matmul(out, wg_lo[:, m0:m1], y[:, b, cols], start=True, stop=False)
                                m = nc.tensor.matmul(out, wg_hi[hi, m0:m1], y[hi, 2, cols], start=False, stop=True)
                    m.then_inc(s_pe, 1)

                from_x(HIDDEN)
                pe.wait_ge(s_conv, 3 * CONV_K)
                pe.wait_ge(s_xh, 3)
                from_y(0)
                pe.wait_ge(s_f, 3)
                from_y(HIDDEN)
                pe.wait_ge(s_i, 3)
                from_x(0)
                pe.wait_ge(s_g, 3)
                pe.wait_ge(s_h, 6)
                for b in range(B):
                    hi = slice(HID_HI * b, HID_HI * (b + 1))
                    for half in range(2):
                        cols = slice(half * COLS, (half + 1) * COLS)
                        nc.tensor.matmul(ps[:, 2 * b + half, :], wo_lo[:, :], gate[:, b, cols], start=True, stop=False)
                        m = nc.tensor.matmul(ps[:, 2 * b + half, :], wo_hi[hi, :], gate[hi, 2, cols], start=False, stop=True)
                m.then_inc(s_pe, 1)


def layers(nc, a, x, xmid, ident):
    with ExitStack() as ctx:
        def sb(name, shape, dt=F32):
            return ctx.enter_context(nc.sbuf_tensor(name, shape, dt))

        def sem(name):
            return ctx.enter_context(nc.semaphore(name))

        def per_stream(name, shape):
            return [sb(f"{name}{b}", shape) for b in range(B)]

        wqkv = sb("wqkv", [P, 3 * INNER])
        wo = sb("wo", [P, HP, DIM])
        w1 = sb("w1", [P, 2 * FF])
        w2 = sb("w2", [P, len(FF_CHUNKS), DIM])
        ln_gb = sb("ln_gb", [P, SM_B2])
        b2 = sb("b2", [P, 2])
        b1 = sb("b1", [P, SMALL - SM_VAL])
        rot = sb("rot", [P, TILES, 4 * DH])
        scales = sb("scales", [P, DEPTH, 4 * DH])
        mask = sb("mask", [P, TILES, P])
        first = sb("first", [P, TILES, WINDOW])
        centre_w = sb("centre_w", [P, P])
        mean_col = sb("mean_col", [P, 1])
        ones = sb("ones", [P, P])
        tab = sb("tab", [P, 4, DH])
        xs = per_stream("xs", [P, P])
        qk = per_stream("qk", [P, 2 * INNER])
        sq = per_stream("sq", [P, 2 * INNER])
        ss, rinv, newt = (per_stream(n, [P, 2 * HEADS + B]) for n in ("ss", "rinv", "newt"))
        t2 = sb("t2", [P, 2 * INNER])
        qkr = per_stream("qkr", [P, 2 * INNER])
        v_new = per_stream("v_new", [P, INNER])
        v_own = per_stream("v_own", [P, INNER])
        v_back = per_stream("v_back", [P, INNER])
        qbd = sb("qbd", [P, HP, 4, 2, WINDOW])
        kT = per_stream("kT", [P, HP, WINDOW + P])
        pr = per_stream("pr", [P, HP, 2, 2 * WINDOW])
        rmax, rsum, rrec = (per_stream(n, [P, 2 * HP]) for n in ("rmax", "rsum", "rrec"))
        pbd = sb("pbd", [P, HP, 2, 2, 2, WINDOW])
        oT = sb("oT", [P, HP, 2, 2 * WINDOW])
        fx, fc, fsq, fxn, diag = (sb(n, [P, B, P]) for n in ("fx", "fc", "fsq", "fxn", "diag"))
        hid = sb("hid", [P, len(FF_CHUNKS), B, P])

        ps_qn = [ctx.enter_context(nc.psum_tensor(f"ps_qn{i}", [P, COLS], F32)) for i in range(2)]
        ps_tr = [ctx.enter_context(nc.psum_tensor(f"ps_tr{i}", [P, COLS], F32)) for i in range(2)]
        ps_s = ctx.enter_context(nc.psum_tensor("ps_s", [P, HP, 2, 2 * WINDOW], F32))
        ps_pv = [ctx.enter_context(nc.psum_tensor(f"ps_pv{i}", [P, COLS], F32)) for i in range(2)]
        DOWN = slice(P, P + B * P)
        VAR = P + B * P

        consts, cleared, centre_ready = sem("consts_loaded"), sem("cleared"), sem("centre_w_ready")
        wqkv_in = [sem(f"w{n}_loaded") for n in "qkv"]
        wo_in, gb_in, w1_in, w2_in, b2_in = map(sem, ("wo_loaded", "ln_gb_loaded", "w1_loaded", "w2_loaded", "b2_loaded"))
        qn_full, qn_done = [[sem(f"qn_{n}{i}") for i in range(2)] for n in ("filled", "evacuated")]
        tr_full, tr_done = [[sem(f"tr_{n}{i}") for i in range(2)] for n in ("filled", "evacuated")]
        pv_full, pv_done = [[sem(f"pv_{n}{i}") for i in range(2)] for n in ("filled", "evacuated")]

        def streams(name):
            return [sem(f"{name}{b}") for b in range(B)]

        tab_ready = sem("tab_ready")
        xs_ready, ss_sum, ss_ready, newton = map(streams, ("xs_ready", "ss_sum", "ss_ready", "newton"))
        rotated, added, qk_ready = map(streams, ("rotated", "added", "qk_ready"))
        v_carried, v_moved = map(streams, ("v_carried", "v_moved"))
        k_carried = streams("k_carried")
        s_full, s_read = sem("scores_filled"), sem("scores_read")
        max_ready, shifted, exp_ready, sum_ready, rec_ready, probs_ready = map(streams, (
            "max_ready", "shifted", "exp_ready", "sum_ready", "rec_ready", "probs_ready"))
        fx_ready, diag_ready, fxn_ready, gel_ready = map(sem, (
            "fx_ready", "diag_ready", "fxn_ready", "gelu_ready"))
        NEWTON = 11

        def layer_of(step):
            return step // TILES

        def cols(step, lead):
            return bass.ds((step % TILES) * P + lead, P)

        def at(step):
            return bass.ds(step % TILES, 1)

        def wait_prev(eng, semaphore, value, step):
            if not (isinstance(step, int) and step == 0):
                eng.wait_ge(semaphore, value)

        def wait_fill(eng, sems, order, i, what, per=1):
            if exists(order, i, what):
                bank, n = fill(order, i, what)
                eng.wait_ge(sems[bank], n * per)

        def ring_free(eng, done, bank, count, per=1):
            if not (isinstance(count, int) and count == 1):
                eng.wait_ge(done[bank], (count - 1) * per)

        def steps(eng, half):
            for i in range(LOOP):
                half(i, 0)
                half(i, 1)
            with eng.Fori(LOOP, STEPS) as i:
                half(i, 0)
                half(i, 1)
            for i in range(STEPS, STEPS + DRAIN):
                half(i, 0)
                half(i, 1)

        with nc.Block() as block:
            @block.sync
            def _(sp):
                def load_wqkv(l, part):
                    c = slice(part * INNER, (part + 1) * INNER)
                    sp.dma_start(wqkv[:, c], a["Wqkv"][l, :, c]).then_inc(wqkv_in[part], 16)

                def load_wo(l):
                    sp.dma_start(wo[:, :, :], a["Wo"][l, :, :].rearrange("(c p) n -> p c n", p=P)).then_inc(wo_in, 16)

                def load_gb(l):
                    sp.dma_start(ln_gb[:, :], a["small"][l, :, 0:SM_B2]).then_inc(gb_in, 16)

                def load_w1(l):
                    sp.dma_start(w1[:, :], a["W1"][l, :, :]).then_inc(w1_in, 16)

                def load_b1(l):
                    sp.dma_start(b1[:, :], a["small"][l, :, SM_VAL:SMALL]).then_inc(w1_in, 16)

                def load_w2(l):
                    sp.dma_start(w2[:, 0:2, :], a["W2"][l, 0:2 * P, :].rearrange("(c p) n -> p c n", p=P)).then_inc(w2_in, 16)
                    sp.dma_start(w2[0:FF - 2 * P, 2, :], a["W2"][l, 2 * P:FF, :]).then_inc(w2_in, 16)

                def load_b2(l):
                    sp.dma_start(b2[:, :], a["small"][l, :, SM_B2:SM_B2 + 2]).then_inc(b2_in, 16)

                for part in range(3):
                    load_wqkv(0, part)
                sp.dma_start(rot[:, :, :], a["rot"]).then_inc(consts, 16)
                sp.dma_start(scales[:, :, :].rearrange("p l d -> p (l d)"), a["scales"].partition_broadcast(P)).then_inc(consts, 16)
                sp.dma_start(mask[:, :, :], a["mask"]).then_inc(consts, 16)
                sp.dma_start(first[:, :, :], a["first"]).then_inc(consts, 16)
                load_wo(0)
                load_gb(0)
                load_w1(0)
                load_b1(0)
                load_w2(0)
                load_b2(0)

                def move_v(i, b):
                    j = i - 1
                    if not valid(j):
                        return
                    if isinstance(j, int) and j == 0:
                        sp.wait_ge(cleared, 1)
                    else:
                        wait_fill(sp, pv_full, pv_order, i, ("pv", b, 3))
                    sp.dma_start(v_back[b][0:WINDOW, :], v_own[b][P - WINDOW:P, :]).then_inc(v_carried[b], 16)
                    wait_fill(sp, qn_done, qn_order, j, ("qkv", b, 5))
                    sp.dma_start(v_back[b][WINDOW:P, :], v_new[b][0:P - WINDOW, :]).then_inc(v_moved[b], 16)
                    sp.wait_ge(v_carried[b], (j + 1) * 16)
                    sp.dma_start(v_own[b][:, :], v_new[b][:, :]).then_inc(v_moved[b], 16)

                def load_next_wqkv(l):
                    i = l * TILES + TILES - 1
                    wait_fill(sp, qn_full, qn_order, i, ("qkv", 1, 1))
                    load_wqkv(l + 1, 0)
                    move_v(i, 1)
                    wait_fill(sp, qn_full, qn_order, i, ("qkv", 1, 3))
                    load_wqkv(l + 1, 1)
                    wait_fill(sp, qn_full, qn_order, i, ("qkv", 1, 5))
                    load_wqkv(l + 1, 2)

                for l in range(DEPTH + 1):
                    i = l * TILES
                    again = 0 < l < DEPTH
                    for b in range(B):
                        move_v(i, b)
                    for b in range(B):
                        move_v(i + 1, b)
                    if again:
                        wait_fill(sp, pv_full, pv_order, i + 1, ("out", 1))
                        load_wo(l)
                    for b in range(B):
                        move_v(i + 2, b)
                    if again:
                        sp.wait_ge(fxn_ready, i)
                        load_gb(l)
                    for b in range(B):
                        move_v(i + 3, b)
                    if again:
                        wait_fill(sp, qn_full, qn_order, i + 3, ("up", 2))
                        load_w1(l)
                        wait_fill(sp, qn_done, qn_order, i + 3, ("up", 2))
                        load_b1(l)
                    move_v(i + 4, 0)
                    if again:
                        wait_fill(sp, pv_full, pv_order, i + 4, ("out", 0))
                        load_w2(l)
                        wait_fill(sp, pv_done, pv_order, i + 4, ("out", 0))
                        load_b2(l)
                    move_v(i + 4, 1)
                    if l == 0:
                        for t in range(5, TILES - 1):
                            for b in range(B):
                                move_v(t, b)
                    elif l < DEPTH:
                        with sp.Fori(5, TILES - 1) as t:
                            for b in range(B):
                                move_v(i + t, b)
                    move_v(i + TILES - 1, 0)
                    if l < DEPTH - 1:
                        load_next_wqkv(l)
                    else:
                        move_v(i + TILES - 1, 1)

            @block.tensor
            def _(pe):
                mm, tr = nc.tensor.matmul, nc.tensor.transpose

                def flat(t):
                    return t[:, :, :].rearrange("p b t -> p (b t)")

                def next_bank(i, what):
                    bank, n = fill(qn_order, i, what)
                    ring_free(pe, qn_done, bank, n)
                    return bank

                def qkv(i, b, chunks):
                    if not valid(i):
                        return
                    if 0 in chunks:
                        pe.wait_ge(xs_ready[b], i + 1)
                    pe.wait_ge(wqkv_in[chunks[0] // 2], (layer_of(i) + 1) * 16)
                    for c in chunks:
                        bank = next_bank(i, ("qkv", b, c))
                        mm(ps_qn[bank][:, :], xs[b][:, :], wqkv[:, c * COLS:(c + 1) * COLS],
                           start=True, stop=True).then_inc(qn_full[bank], 1)

                def transpose_probs(i, b):
                    j = i - 2
                    if not valid(j):
                        return
                    pe.wait_ge(probs_ready[b], j + 1)
                    for f in range(2):
                        bank, n = fill(tr_order, i, ("probs", b, f))
                        ring_free(pe, tr_done, bank, n, 2)
                        for m in range(4):
                            last = tr(ps_tr[bank][:, m * P:(m + 1) * P],
                                      pr[b][:, 4 * f + m, :, :].rearrange("p u k -> p (u k)"), ident[:, :])
                        last.then_inc(tr_full[bank], 1)

                def transpose_qk(i, b, k):
                    j = i - 1
                    if not valid(j):
                        return
                    pe.wait_ge(qk_ready[b], 2 * j + k + 1)
                    for f in (2 * k, 2 * k + 1):
                        bank, n = fill(tr_order, i, ("qk", b, f))
                        ring_free(pe, tr_done, bank, n, 2)
                        for m in range(4):
                            last = tr(ps_tr[bank][:, m * P:(m + 1) * P], qkr[b][:, (4 * f + m) * P:(4 * f + m + 1) * P],
                                      ident[:, :])
                        last.then_inc(tr_full[bank], 1)

                def scores(i, b):
                    j = i - 1
                    if not valid(j):
                        return
                    for f in (2, 3):
                        wait_fill(pe, tr_done, tr_order, i, ("qk", b, f), 2)
                    if b:
                        pe.wait_ge(s_read, 2 * j + 1)
                    else:
                        wait_prev(pe, s_read, 2 * j, j)
                    for hp in range(HP):
                        for u in range(2):
                            for odd in range(2):
                                w = 2 * u + odd
                                last = mm(ps_s[64 * odd:64 * odd + 64, hp, u, :],
                                          qbd[:, hp, w, :, :].rearrange("p h q -> p (h q)"),
                                          kT[b][:, hp, WINDOW * w:WINDOW * (w + 2)], start=True, stop=True)
                    last.then_inc(s_full, 1)

                def probs_v(i, b):
                    j = i - 2
                    if not valid(j):
                        return
                    pe.wait_ge(v_moved[b], (j + 1) * 32)
                    pe.wait_ge(v_carried[b], (j + 1) * 16)
                    for f in range(4):
                        if f % 2 == 0:
                            wait_fill(pe, tr_done, tr_order, i, ("probs", b, f // 2), 2)
                        bank, n = fill(pv_order, i, ("pv", b, f))
                        ring_free(pe, pv_done, bank, n)
                        for m in range(4):
                            hp, odd = 2 * f + m // 2, m % 2
                            v = (v_own if odd else v_back)[b]
                            last = mm(ps_pv[bank][:, m * P:(m + 1) * P], v[:, hp * P:(hp + 1) * P],
                                      pbd[:, hp, odd, :, :, :].rearrange("p h u q -> p (h u q)"), start=True, stop=True)
                        last.then_inc(pv_full[bank], 1)

                def out_projection(i, b):
                    if not exists(pv_order, i, ("out", b)):
                        return
                    j, n, m = i - 2, i - 3, i - 5
                    bank, k = fill(pv_order, i, ("out", b))
                    ring_free(pe, pv_done, bank, k)
                    if valid(j):
                        pe.wait_ge(wo_in, (layer_of(j) + 1) * 16)
                        for f in (2, 3):
                            wait_fill(pe, pv_done, pv_order, i, ("pv", b, f))
                        for hp in range(HP):
                            last = mm(ps_pv[bank][:, 0:P], wo[:, hp, :], oT[:, hp, :, :].rearrange("p a c -> p (a c)"),
                                      start=(hp == 0), stop=(hp == HP - 1))
                    if b == 0 and valid(m):
                        pe.wait_ge(w2_in, (layer_of(m) + 1) * 32)
                        wait_fill(pe, qn_done, qn_order, i - 1, ("up", 2))
                        for c, (r, w) in enumerate(FF_CHUNKS):
                            last = mm(ps_pv[bank][:, DOWN], w2[0:w, c, :], hid[0:w, c, :, :].rearrange("p b t -> p (b t)"),
                                      start=(c == 0), stop=(c == len(FF_CHUNKS) - 1))
                    if b == 0 and valid(n):
                        wait_fill(pe, qn_done, qn_order, i, "centre")
                        for s in range(B):
                            last = mm(ps_pv[bank][:, VAR + s:VAR + s + 1], fsq[:, s, :], mean_col[:, :], start=True, stop=True)
                    if b == 0 or not valid(n):
                        last.then_inc(pv_full[bank], 1)

                def ffn_broadcast(i):
                    n = i - 3
                    if not valid(n):
                        return
                    bank, k = fill(pv_order, i, ("out", 1))
                    pe.wait_ge(diag_ready, n + 1)
                    mm(ps_pv[bank][:, DOWN], ones[:, :], flat(diag), start=True, stop=True).then_inc(pv_full[bank], 1)

                def ffn_centre(i):
                    n = i - 3
                    if not valid(n):
                        return
                    pe.wait_ge(fx_ready, n + 1)
                    bank = next_bank(i, "centre")
                    mm(ps_qn[bank][:, 0:B * P], centre_w[:, :], flat(fx), start=True, stop=True).then_inc(qn_full[bank], 1)

                def ffn_up(i, c):
                    m = i - 4
                    if not valid(m):
                        return
                    if c == 0:
                        pe.wait_ge(w1_in, (layer_of(m) + 1) * 32)
                        pe.wait_ge(fxn_ready, m + 1)
                    r, w = FF_CHUNKS[c]
                    bank = next_bank(i, ("up", c))
                    mm(ps_qn[bank][0:w, 0:B * P], w1[:, r:r + w], flat(fxn), start=True, stop=True)
                    mm(ps_qn[bank][0:w, B * P:2 * B * P], w1[:, FF + r:FF + r + w], flat(fxn),
                       start=True, stop=True).then_inc(qn_full[bank], 1)

                def half(i, b):
                    transpose_probs(i, b)
                    qkv(i, b, (0, 1))
                    probs_v(i, b)
                    if b == 0:
                        ffn_centre(i)
                    qkv(i, b, (2, 3))
                    out_projection(i, b)
                    transpose_qk(i, b, 0)
                    if b == 0:
                        qkv(i, b, (4,))
                    else:
                        ffn_up(i, 0)
                    transpose_qk(i, b, 1)
                    if b == 0:
                        qkv(i, b, (5,))
                    else:
                        ffn_up(i, 1)
                    scores(i, b)
                    if b == 1:
                        qkv(i, b, (4, 5))
                        ffn_up(i, 2)
                        ffn_broadcast(i)

                pe.wait_ge(cleared, 1)
                pe.wait_ge(centre_ready, 1)
                steps(pe, half)

            @block.scalar
            def _(act):
                f = nc.scalar.activation

                def before(i, b):
                    return (i, 0) if b else (i - 1, 1)

                def evac_probs(i, b):
                    j = i - 2
                    if not valid(j):
                        return
                    pi, pb = before(i, b)
                    wait_fill(act, pv_full, pv_order, pi, ("pv", pb, 3))
                    for k in range(2):
                        bank, n = fill(tr_order, i, ("probs", b, k))
                        act.wait_ge(tr_full[bank], n)
                        f(pbd[0:DH, 4 * k:4 * k + 4, :, :, 0, :].rearrange("p m a h q -> p (m a h) q"),
                          ps_tr[bank][0:DH, :].rearrange("p (x q) -> p x q", q=WINDOW), ACT.Copy).then_inc(tr_done[bank], 1)

                def evac_qkv(i, b, chunks):
                    if not valid(i):
                        return
                    for c in chunks:
                        bank, n = fill(qn_order, i, ("qkv", b, c))
                        act.wait_ge(qn_full[bank], n)
                        if c < 4:
                            if c == 0:
                                wait_prev(act, added[b], i * 2, i)
                            f(qk[b][:, c * COLS:(c + 1) * COLS], ps_qn[bank][:, :], ACT.Copy)
                            if c == 0:
                                wait_prev(act, ss_sum[b], i, i)
                            f(sq[b][:, c * COLS:(c + 1) * COLS], ps_qn[bank][:, :], ACT.Square).then_inc(qn_done[bank], 1)
                        else:
                            if c == 4:
                                wait_prev(act, v_moved[b], i * 32, i)
                            f(v_new[b][:, (c - 4) * COLS:(c - 3) * COLS], ps_qn[bank][:, :], ACT.Copy).then_inc(qn_done[bank], 1)

                def evac_pv(i, b):
                    j = i - 2
                    if not valid(j):
                        return
                    pi, pb = before(i, b)
                    wait_fill(act, pv_full, pv_order, pi, ("out", pb))
                    for k in range(4):
                        bank, n = fill(pv_order, i, ("pv", b, k))
                        act.wait_ge(pv_full[bank], n)
                        for h in range(2):
                            rows = slice(DH * h, DH * (h + 1))
                            last = f(oT[rows, 2 * k:2 * k + 2, :, :].rearrange("p m a c -> p (m a) c"),
                                     ps_pv[bank][rows, :].rearrange("p (x h c) -> p x h c", h=2, c=DH)[:, :, h, :], ACT.Copy)
                        last.then_inc(pv_done[bank], 1)

                def evac_qk(i, b):
                    j = i - 1
                    if not valid(j):
                        return
                    if b:
                        act.wait_ge(s_full, 2 * j + 1)
                    else:
                        wait_prev(act, s_full, 2 * j, j)
                    for k in range(2):
                        bank, n = fill(tr_order, i, ("qk", b, k))
                        act.wait_ge(tr_full[bank], n)
                        for h in range(2):
                            rows = slice(DH * h, DH * (h + 1))
                            last = f(qbd[rows, 4 * k:4 * k + 4, :, h, :],
                                     ps_tr[bank][rows, :].rearrange("p (m w q) -> p m w q", m=4, w=4), ACT.Copy)
                        last.then_inc(tr_done[bank], 2)
                    act.wait_ge(k_carried[b], j + 1)
                    for k in range(2):
                        bank, n = fill(tr_order, i, ("qk", b, 2 + k))
                        act.wait_ge(tr_full[bank], n)
                        f(kT[b][:, 4 * k:4 * k + 4, WINDOW:],
                          ps_tr[bank][:, :].rearrange("p (m t) -> p m t", m=4), ACT.Copy).then_inc(tr_done[bank], 2)

                def exps(j, b):
                    if not valid(j):
                        return
                    act.wait_ge(shifted[b], j + 1)
                    f(pr[b][:, :, :, :], pr[b][:, :, :, :], ACT.Exp, scale=QK_SCALE).then_inc(exp_ready[b], 1)

                def ffn_square(i):
                    n = i - 3
                    if not valid(n):
                        return
                    bank, k = fill(qn_order, i, "centre")
                    act.wait_ge(qn_full[bank], k)
                    if not (isinstance(n, int) and n == 0):
                        wait_fill(act, pv_done, pv_order, i - 1, ("out", 1))
                    f(fc[:, :, :].rearrange("p b t -> p (b t)"), ps_qn[bank][:, 0:B * P], ACT.Copy)
                    if not (isinstance(n, int) and n == 0):
                        wait_fill(act, pv_full, pv_order, i - 1, ("out", 0))
                    f(fsq[:, :, :].rearrange("p b t -> p (b t)"), ps_qn[bank][:, 0:B * P], ACT.Square).then_inc(qn_done[bank], 1)

                def ffn_gelu(i, c):
                    m = i - 4
                    if not valid(m):
                        return
                    bank, k = fill(qn_order, i, ("up", c))
                    act.wait_ge(qn_full[bank], k)
                    if c == 0 and not (isinstance(m, int) and m == 0):
                        wait_fill(act, pv_full, pv_order, i, ("out", 0))
                    w = FF_CHUNKS[c][1]
                    f(hid[0:w, c, :, :].rearrange("p b t -> p (b t)"), ps_qn[bank][0:w, B * P:2 * B * P], ACT.Gelu,
                      bias=b1[0:w, len(FF_CHUNKS) + c:len(FF_CHUNKS) + c + 1], scale=1.0).then_inc(gel_ready, 1)

                def half(i, b):
                    evac_probs(i, b)
                    evac_qkv(i, b, (0, 1))
                    evac_pv(i, b)
                    if b == 0:
                        ffn_square(i)
                    evac_qkv(i, b, (2, 3))
                    if b == 0:
                        exps(i - 2, 1)
                    else:
                        exps(i - 1, 0)
                    evac_qk(i, b)
                    if b == 1:
                        ffn_gelu(i, 0)
                        ffn_gelu(i, 1)
                    evac_qkv(i, b, (4, 5))
                    if b == 1:
                        ffn_gelu(i, 2)

                act.wait_ge(cleared, 1)
                steps(act, half)

            @block.vector
            def _(dve):
                v = nc.vector

                def shift_in(i, b):
                    if not valid(i):
                        return
                    if not (isinstance(i, int) and i == 0):
                        wait_fill(dve, qn_full, qn_order, i - 1, ("qkv", b, 5))
                    v.tensor_copy(xs[b][0:64, :], x[0:64, b, cols(i, 1)])
                    v.tensor_copy(xs[b][64:P, :], x[64:P, b, cols(i, 0)]).then_inc(xs_ready[b], 1)

                def square_sums(s, b):
                    if not valid(s):
                        return
                    for c in (2, 3):
                        wait_fill(dve, qn_done, qn_order, s, ("qkv", b, c))
                    wait_prev(dve, newton[b], NEWTON * s, s)
                    v.tensor_reduce(ss[b][:, 0:2 * HEADS], sq[b][:, :].rearrange("p (h d) -> p h d", d=DH),
                                    AX.X, ALU.add).then_inc(ss_sum[b], 1)

                def floor(s, b):
                    if not valid(s):
                        return
                    dve.wait_ge(ss_sum[b], s + 1)
                    v.tensor_scalar(ss[b][:, 0:2 * HEADS], ss[b][:, 0:2 * HEADS], NORM_FLOOR_SQ, None,
                                    ALU.max).then_inc(ss_ready[b], 1)

                def sine(s, b, k):
                    if not valid(s):
                        return
                    if b:
                        dve.wait_ge(added[0], 2 * s + k + 1)
                    elif not (isinstance(s, int) and s == 0):
                        dve.wait_ge(added[1], 2 * (s - 1) + k + 1)
                    dve.wait_ge(tab_ready, s + 1)
                    for c in (2 * k, 2 * k + 1):
                        wait_fill(dve, qn_done, qn_order, s, ("qkv", b, c))
                    part = slice(k * INNER, (k + 1) * INNER)
                    swapped = qk[b][:, part].rearrange("p (h s d) -> p h s d", s=2, d=DH // 2)[:, :, ::-1, :]
                    v.tensor_tensor(t2[:, part].rearrange("p (h s d) -> p h s d", s=2, d=DH // 2), swapped,
                                    tab[:, 2 * k + 1:2 * k + 2, :].rearrange("p o (s d) -> p o s d", s=2)
                                    .broadcast_to([P, HEADS, 2, DH // 2]), ALU.mult).then_inc(rotated[b], 1)

                def cosine(s, b, k):
                    if not valid(s):
                        return
                    dve.wait_ge(rotated[b], 4 * s + 2 * k + 1)
                    src = qk[b][:, k * INNER:(k + 1) * INNER].rearrange("p (h d) -> p h d", d=DH)
                    v.tensor_tensor(src, src, tab[:, 2 * k:2 * k + 1, :].broadcast_to([P, HEADS, DH]),
                                    ALU.mult).then_inc(rotated[b], 1)

                def inverse_root(s, b, n, k):
                    lo = 0 if valid(s) else 2 * HEADS
                    hi = 2 * HEADS + B if b == 0 and valid(n) else 2 * HEADS
                    if lo == hi:
                        return
                    y, t, w = rinv[b][:, lo:hi], newt[b][:, lo:hi], ss[b][:, lo:hi]
                    if k > 0:
                        dve.wait_ge(newton[b], NEWTON * s + k)
                    if k == 0:
                        if valid(s):
                            dve.wait_ge(ss_ready[b], s + 1)
                            wait_prev(dve, qk_ready[b], 2 * s, s)
                        if hi > 2 * HEADS:
                            wait_fill(dve, pv_done, pv_order, s, ("out", 0))
                            wait_prev(dve, diag_ready, n, n)
                        ins = v.tensor_scalar(y.bitcast(I32), w.bitcast(I32), 1, None, ALU.logical_shift_right)
                    elif k == 1:
                        ins = v.tensor_scalar(y.bitcast(I32), y.bitcast(I32), -1.0, float(0x5f3759df), ALU.mult, ALU.add)
                    elif k % 3 == 2:
                        ins = v.tensor_tensor(t, y, y, ALU.mult)
                    elif k % 3 == 0:
                        ins = v.scalar_tensor_tensor(t, t, -0.5, w, ALU.mult, ALU.mult)
                    else:
                        ins = v.scalar_tensor_tensor(y, t, 1.5, y, ALU.add, ALU.mult)
                    ins.then_inc(newton[b], 1)

                def carry_k(i, b):
                    j = i - 1
                    if not valid(j):
                        return
                    wait_prev(dve, s_full, 2 * j + b - 1, j)
                    v.tensor_tensor(kT[b][:, :, 0:WINDOW], kT[b][:, :, P:P + WINDOW],
                                    first[:, at(j), :].broadcast_to([P, HP, WINDOW]), ALU.mult).then_inc(k_carried[b], 1)

                def masked(j, b):
                    if not valid(j):
                        return
                    dve.wait_ge(s_full, 2 * j + b + 1)
                    wait_fill(dve, tr_full, tr_order, j + 1, ("probs", b, 1))
                    flat = pr[b][:, :, :, :].rearrange("p m u k -> p m (u k)")
                    v.tensor_tensor(flat, ps_s[:, :, :, :].rearrange("p m u k -> p m (u k)"),
                                    mask[:, at(j), :].broadcast_to([P, HP, P]), ALU.add).then_inc(s_read, 1)

                def maxima(j, b):
                    if not valid(j):
                        return
                    dve.wait_ge(s_read, 2 * j + b + 1)
                    v.tensor_reduce(rmax[b][:, :], pr[b][:, :, :, :].rearrange("p m u k -> p (m u) k"), AX.X,
                                    ALU.max).then_inc(max_ready[b], 1)

                def less_max(j, b):
                    if not valid(j):
                        return
                    dve.wait_ge(max_ready[b], j + 1)
                    rows = pr[b][:, :, :, :].rearrange("p m u k -> p (m u) k")
                    v.tensor_tensor(rows, rows, rmax[b][:, :].unsqueeze(2).broadcast_to([P, 2 * HP, 2 * WINDOW]),
                                    ALU.subtract).then_inc(shifted[b], 1)

                def row_sums(j, b):
                    if not valid(j):
                        return
                    dve.wait_ge(exp_ready[b], j + 1)
                    v.tensor_reduce(rsum[b][:, :], pr[b][:, :, :, :].rearrange("p m u k -> p (m u) k"), AX.X,
                                    ALU.add).then_inc(sum_ready[b], 1)

                def row_recips(j, b):
                    if not valid(j):
                        return
                    dve.wait_ge(sum_ready[b], j + 1)
                    wait_prev(dve, probs_ready[b], j, j)
                    v.reciprocal(rrec[b][:, :], rsum[b][:, :]).then_inc(rec_ready[b], 1)

                def evac_probs(i, b):
                    j = i - 2
                    if not valid(j):
                        return
                    wait_fill(dve, pv_full, pv_order, *((i, ("pv", 0, 3)) if b else (i - 1, ("pv", 1, 3))))
                    for k in range(2):
                        bank, n = fill(tr_order, i, ("probs", b, k))
                        dve.wait_ge(tr_full[bank], n)
                        v.tensor_copy(pbd[DH:P, 4 * k:4 * k + 4, :, :, 1, :].rearrange("p m a h q -> p (m a h) q"),
                                      ps_tr[bank][DH:P, :].rearrange("p (x q) -> p x q", q=WINDOW)).then_inc(tr_done[bank], 1)

                def residual(bank, j, b):
                    return v.tensor_tensor(xmid[:, b, cols(j, 1)].rearrange("p (u a q) -> p a u q", u=2, a=2),
                                           ps_pv[bank][:, 0:P].rearrange("p (a u q) -> p a u q", u=2, a=2),
                                           x[:, b, cols(j, 1)].rearrange("p (u a q) -> p a u q", u=2, a=2), ALU.add)

                def take_out0(i):
                    if not exists(pv_order, i, ("out", 0)):
                        return
                    j, n, m = i - 2, i - 3, i - 5
                    bank, k = fill(pv_order, i, ("out", 0))
                    dve.wait_ge(pv_full[bank], k)
                    if valid(n):
                        if not (isinstance(n, int) and n == 0):
                            dve.wait_ge(newton[0], NEWTON * i)
                        last = v.tensor_scalar(ss[0][:, 2 * HEADS:], ps_pv[bank][:, VAR:VAR + B], LN_EPS, None, ALU.add)
                    if valid(j):
                        last = residual(bank, j, 0)
                    if valid(m):
                        dve.wait_ge(b2_in, (layer_of(m) + 1) * 16)
                        last = v.scalar_tensor_tensor(x[:, :, cols(m, 1)],
                                                      ps_pv[bank][:, DOWN].rearrange("p (b t) -> p b t", b=B),
                                                      b2[:, 0:1], xmid[:, :, cols(m, 1)], ALU.add, ALU.add)
                    last.then_inc(pv_done[bank], 1)

                def take_out1(i):
                    if not exists(pv_order, i - 1, ("out", 1)):
                        return
                    j, m = i - 3, i - 4
                    bank, k = fill(pv_order, i - 1, ("out", 1))
                    dve.wait_ge(pv_full[bank], k)
                    if valid(j):
                        last = residual(bank, j, 1)
                    if valid(m):
                        wait_fill(dve, qn_full, qn_order, i - 1, ("up", 2))
                        last = v.tensor_tensor(fxn[:, :, :].rearrange("p b t -> p (b t)"),
                                               fc[:, :, :].rearrange("p b t -> p (b t)"), ps_pv[bank][:, DOWN], ALU.mult)
                    last.then_inc(pv_done[bank], 1)
                    if valid(m):
                        dve.wait_ge(pv_done[bank], k)
                        dve.wait_ge(gb_in, (layer_of(m) + 1) * 16)
                        v.tensor_scalar(fxn[:, :, :], fxn[:, :, :], ln_gb[:, SM_G:SM_G + 1], ln_gb[:, SM_B:SM_B + 1],
                                        ALU.mult, ALU.add).then_inc(fxn_ready, 1)

                def ffn_shift(i):
                    n = i - 3
                    if not valid(n):
                        return
                    for b in range(B):
                        wait_fill(dve, pv_done, pv_order, i - 1, ("out", b))
                    if not (isinstance(n, int) and n == 0):
                        wait_fill(dve, qn_full, qn_order, i - 1, "centre")
                    v.tensor_copy(fx[0:64, :, :], xmid[0:64, :, cols(n, 1)])
                    v.tensor_copy(fx[64:P, :, :], xmid[64:P, :, cols(n, 0)]).then_inc(fx_ready, 1)

                def ffn_diag(i):
                    n = i - 3
                    if not valid(n):
                        return
                    dve.wait_ge(newton[0], NEWTON * (i + 1))
                    if not (isinstance(n, int) and n == 0):
                        wait_fill(dve, pv_full, pv_order, i - 1, ("out", 1))
                    for s in range(B):
                        last = v.tensor_scalar(diag[:, s, :], ident[:, :], rinv[0][:, 2 * HEADS + s:2 * HEADS + s + 1], None,
                                               ALU.mult)
                    last.then_inc(diag_ready, 1)

                def ffn_gate(i, c):
                    m = i - 4
                    if not valid(m):
                        return
                    w = FF_CHUNKS[c][1]
                    bank, k = fill(qn_order, i, ("up", c))
                    dve.wait_ge(gel_ready, 3 * m + c + 1)
                    gel = hid[0:w, c, :, :].rearrange("p b t -> p (b t)")
                    v.scalar_tensor_tensor(gel, ps_qn[bank][0:w, 0:B * P], b1[0:w, c:c + 1], gel,
                                           ALU.add, ALU.mult).then_inc(qn_done[bank], 1)

                def half0(i):
                    def root(*ks):
                        for k in ks:
                            inverse_root(i - 1, 1, None, k)

                    s, j = i - 1, i - 2
                    take_out1(i)
                    evac_probs(i, 0)
                    carry_k(i, 0)
                    masked(j, 1)
                    ffn_shift(i)
                    sine(s, 1, 0)
                    maxima(j, 1)
                    cosine(s, 1, 0)
                    less_max(j, 1)
                    square_sums(s, 1)
                    sine(s, 1, 1)
                    floor(s, 1)
                    cosine(s, 1, 1)
                    root(0)
                    row_sums(j, 1)
                    root(1)
                    row_recips(j, 1)
                    root(2)
                    shift_in(i, 1)
                    root(*range(3, NEWTON))

                def half1(i):
                    def root(*ks):
                        for k in ks:
                            inverse_root(i, 0, i - 3, k)

                    s, j = i, i - 1
                    take_out0(i)
                    evac_probs(i, 1)
                    carry_k(i, 1)
                    masked(j, 0)
                    sine(s, 0, 0)
                    maxima(j, 0)
                    cosine(s, 0, 0)
                    less_max(j, 0)
                    square_sums(s, 0)
                    sine(s, 0, 1)
                    floor(s, 0)
                    cosine(s, 0, 1)
                    root(0)
                    row_sums(j, 0)
                    root(1)
                    row_recips(j, 0)
                    root(2)
                    shift_in(i + 1, 0)
                    root(3)
                    ffn_gate(i, 0)
                    root(4)
                    ffn_gate(i, 1)
                    root(*range(5, NEWTON))
                    ffn_diag(i)
                    ffn_gate(i, 2)

                def half(i, b):
                    if b:
                        half1(i)
                    else:
                        half0(i)

                for b in range(B):
                    v.memset(kT[b][:, :, :], 0.0)
                    v.memset(v_own[b][:, :], 0.0)
                    v.memset(v_back[b][:, :], 0.0)
                v.memset(qbd[:, :, :, :, :], 0.0)
                v.memset(pbd[:, :, :, :, :, :], 0.0)
                v.memset(xmid[:, :, 0:1], 0.0)
                v.memset(ones[:, :], 1.0)
                v.memset(mean_col[:, :], 1.0 / DIM).then_inc(cleared, 1)
                v.tensor_scalar(centre_w[:, :], ident[:, :], -1.0 / DIM, None, ALU.add).then_inc(centre_ready, 1)
                dve.wait_ge(cleared, 1)
                dve.wait_ge(consts, 64)
                shift_in(0, 0)
                steps(dve, half)
                wait_fill(dve, pv_done, pv_order, STEPS + DRAIN - 1, ("out", 0))

            @block.gpsimd
            def _(pool):
                g = nc.gpsimd

                def tables(i):
                    if not valid(i):
                        return
                    wait_prev(pool, rotated[1], 4 * i, i)
                    g.tensor_tensor(tab[:, :, :].rearrange("p k d -> p (k d)").unsqueeze(1),
                                    rot[:, at(i), :], scales[:, bass.ds(layer_of(i), 1), :],
                                    ALU.mult).then_inc(tab_ready, 1)

                def add(s, b, k):
                    if not valid(s):
                        return
                    wait_fill(pool, tr_full, tr_order, s, ("qk", b, 2))
                    wait_fill(pool, tr_full, tr_order, s, ("qk", b, 3))
                    pool.wait_ge(rotated[b], 4 * s + 2 * k + 2)
                    part = slice(k * INNER, (k + 1) * INNER)
                    g.tensor_tensor(qkr[b][:, part], qk[b][:, part], t2[:, part], ALU.add).then_inc(added[b], 1)

                def scale(s, b, k):
                    if not valid(s):
                        return
                    if k == 0:
                        pool.wait_ge(newton[b], NEWTON * (s + 1))
                    pool.wait_ge(added[b], 2 * s + k + 1)
                    part = qkr[b][:, k * INNER:(k + 1) * INNER].rearrange("p (h d) -> p h d", d=DH)
                    g.tensor_tensor(part, part, rinv[b][:, k * HEADS:(k + 1) * HEADS].unsqueeze(2)
                                    .broadcast_to([P, HEADS, DH]), ALU.mult).then_inc(qk_ready[b], 1)

                def scale_probs(j, b):
                    if not valid(j):
                        return
                    pool.wait_ge(rec_ready[b], j + 1)
                    rows = pr[b][:, :, :, :].rearrange("p m u k -> p (m u) k")
                    g.tensor_tensor(rows, rows, rrec[b][:, :].unsqueeze(2).broadcast_to([P, 2 * HP, 2 * WINDOW]),
                                    ALU.mult).then_inc(probs_ready[b], 1)

                def half(i, b):
                    s, j, other = (i, i - 1, 0) if b else (i - 1, i - 2, 1)
                    if b:
                        tables(i)
                    add(s, other, 0)
                    add(s, other, 1)
                    scale_probs(j, other)
                    scale(s, other, 0)
                    scale(s, other, 1)

                pool.wait_ge(consts, 64)
                steps(pool, half)


def combine(nc, a, x, branch, ident):
    with ExitStack() as ctx:
        def sem(name):
            return ctx.enter_context(nc.semaphore(name))

        NT = B * TILES
        sig = ctx.enter_context(nc.sbuf_tensor("sig", [P, B, SEQ], F32))
        xin = ctx.enter_context(nc.sbuf_tensor("xin", [P, NT, DIM], F32))
        out = ctx.enter_context(nc.sbuf_tensor("outs", [P, NT, DIM], F32))
        ps = ctx.enter_context(nc.psum_tensor("ps_out", [P, 4, COLS], F32))
        xin_in, sig_ready, silu_ready, prod_ready, tr_full, sum_ready, out_sent = map(sem, (
            "c_input", "c_sigmoid", "c_silu", "c_product", "c_transposed", "c_sum", "c_out"))
        with nc.Block() as block:
            @block.sync
            def _(sp):
                sp.dma_start(xin[:, :, :], a["x"].rearrange("b (t p) d -> p (b t) d", p=P)).then_inc(xin_in, 16)
                for q in range(4):
                    sp.wait_ge(sum_ready, q + 1)
                    sp.dma_start(a["out"].rearrange("b (t p) d -> p (b t) d", p=P)[:, 4 * q:4 * q + 4, :],
                                 out[:, 4 * q:4 * q + 4, :]).then_inc(out_sent, 16)
                sp.wait_ge(out_sent, 64)

            @block.scalar
            def _(act):
                for b in range(B):
                    nc.scalar.activation(sig[:, b, :], x[:, b, 1:1 + SEQ], ACT.Sigmoid).then_inc(sig_ready, 1)

            @block.vector
            def _(dve):
                for b in range(B):
                    dve.wait_ge(sig_ready, b + 1)
                    nc.vector.tensor_tensor(sig[:, b, :], sig[:, b, :], x[:, b, 1:1 + SEQ], ALU.mult).then_inc(silu_ready, 1)
                    dve.wait_ge(silu_ready, b + 1)
                    nc.vector.tensor_tensor(sig[:, b, :], sig[:, b, :], branch[:, b, :], ALU.mult).then_inc(prod_ready, 1)
                dve.wait_ge(xin_in, 16)
                for q in range(4):
                    dve.wait_ge(tr_full, q + 1)
                    nc.vector.tensor_tensor(out[:, 4 * q:4 * q + 4, :].rearrange("p t d -> p (t d)"), ps[:, q, :],
                                            xin[:, 4 * q:4 * q + 4, :].rearrange("p t d -> p (t d)"), ALU.add).then_inc(sum_ready, 1)

            @block.tensor
            def _(pe):
                for t in range(NT):
                    b, k = t // TILES, t % TILES
                    if k == 0:
                        pe.wait_ge(prod_ready, b + 1)
                    m = nc.tensor.transpose(ps[:, t // 4, (t % 4) * P:(t % 4 + 1) * P], sig[:, b, k * P:(k + 1) * P], ident[:, :])
                    if t % 4 == 3:
                        m.then_inc(tr_full, 1)


def rotary_constants():
    f = np.float32
    half = np.arange(0, DH, 2, dtype=f)
    inv_freq = (f(1.0) / np.power(f(10000.0), half / f(DH))).astype(f)
    t = np.arange(SEQ, dtype=f)
    freqs = (t[:, None] * inv_freq[None, :]).astype(f)
    base = ((half + f(0.4 * DH)) / f(1.4 * DH)).astype(f)
    power = ((t - f(SEQ // 2)) / f(WINDOW // 2)).astype(f)
    scale = np.power(base[None, :], power[:, None]).astype(f)
    cos, sin, inv = np.cos(freqs), np.sin(freqs), (f(1.0) / scale)
    parts = []
    for s in (scale, inv):
        c, n = cos * s, sin * s
        parts += [c, c, -n, n]
    tab = np.concatenate(parts, 1).astype(f)
    return np.ascontiguousarray(tab.reshape(TILES, P, 4 * DH).transpose(1, 0, 2))


def mask_constants():
    m = np.full((2, 2, WINDOW, TILES, 2, 2 * WINDOW), MASKED, np.float32)
    q = np.arange(WINDOW)[:, None]
    k = np.arange(2 * WINDOW)[None, :]
    ok = (k >= q) & (k <= q + WINDOW)
    for par in range(2):
        for t in range(TILES):
            for u in range(2):
                valid = ok & ((k >= WINDOW) if t == 0 and u == 0 and par == 0 else True)
                m[par, :, :, t, u, :] = np.where(valid, 0.0, MASKED)
    return m.reshape(P, TILES, P)


def kernel(L0_attn_x, L0_attn_W_in, L0_attn_conv_w, L0_attn_conv_b, L0_attn_W_gates, L0_attn_b_gates,
           L0_attn_forget_base, L0_attn_W_out, L0_ffn_Wqkv, L0_ffn_q_scale, L0_ffn_k_scale, L0_ffn_Wo, L0_ffn_ln_g,
           L0_ffn_ln_b, L0_ffn_W1, L0_ffn_b1, L0_ffn_W2, L0_ffn_b2):
    import concourse.bacc as bacc
    from concourse.bass_utils import run_bass_kernel_spmd

    def arr(v):
        return np.ascontiguousarray(v)

    by_channel = np.stack([*np.asarray(L0_attn_conv_w).T, np.asarray(L0_attn_conv_b),
                           *np.asarray(L0_attn_b_gates).reshape(2, HIDDEN), np.asarray(L0_attn_forget_base)], 1)
    rec_par = np.stack([by_channel[0:HID_LO], np.concatenate([by_channel[HID_LO:], by_channel[HID_LO:]])], 1)
    qs, ks = np.asarray(L0_ffn_q_scale), np.asarray(L0_ffn_k_scale)
    swap = np.r_[DH // 2:DH, 0:DH // 2]
    scales = np.concatenate([qs, qs[:, swap], ks, ks[:, swap]], 1).reshape(-1)
    small = np.zeros((DEPTH, P, SMALL), np.float32)
    small[:, :, SM_G], small[:, :, SM_B], small[:, :, SM_B2] = np.asarray(L0_ffn_ln_g), np.asarray(L0_ffn_ln_b), np.asarray(L0_ffn_b2)
    b1 = np.asarray(L0_ffn_b1)
    for c, (r, m) in enumerate(FF_CHUNKS):
        small[:, 0:m, SM_VAL + c] = b1[:, r:r + m]
        small[:, 0:m, SM_GATE + c] = b1[:, FF + r:FF + r + m]
    first = np.ones((P, TILES, WINDOW), np.float32)
    first[:, 0, :] = 0.0
    arrays = {
        "x": arr(L0_attn_x), "w_in_t": arr(np.asarray(L0_attn_W_in).T), "w_gates_t": arr(np.asarray(L0_attn_W_gates).T),
        "w_out_t": arr(np.asarray(L0_attn_W_out).T), "rec_par": arr(rec_par), "Wqkv": arr(L0_ffn_Wqkv), "Wo": arr(L0_ffn_Wo),
        "W1": arr(L0_ffn_W1), "W2": arr(L0_ffn_W2), "scales": arr(scales), "small": small,
        "rot": rotary_constants(), "mask": mask_constants(), "first": first, "ident": np.eye(P, dtype=np.float32),
    }
    nc = bacc.Bacc("TRN2", target_bir_lowering=False, num_devices=1)
    aps = {n: nc.dram_tensor(f"in_{n}", v.shape, F32, kind="ExternalInput").ap() for n, v in arrays.items()}
    aps["out"] = nc.dram_tensor("out", (B, SEQ, DIM), F32, kind="ExternalOutput").ap()
    build(nc, aps)
    r = run_bass_kernel_spmd(nc, [{f"in_{n}": v for n, v in arrays.items()}], core_ids=[0])
    return r.results[0]["out"]
```

```python
import math
from contextlib import ExitStack

import numpy as np

import concourse.bass as bass
from concourse import mybir

F32 = mybir.dt.float32
I32 = mybir.dt.int32
F32R = mybir.dt.float32r
ALU = mybir.AluOpType
ACT = mybir.ActivationFunctionType
AX = mybir.AxisListType

P = 128
B, SEQ, DIM = 2, 1024, 128
TILES = SEQ // P
HIDDEN, CONV_K = 192, 4
HID_LO, HID_HI = P, HIDDEN - P
DEPTH, HEADS, DH, WINDOW = 6, 16, 64, 32
INNER = HEADS * DH
HP = HEADS // 2
FF = int(DIM * 4 * 2 / 3)
FF_CHUNKS = [(c, min(P, FF - c)) for c in range(0, FF, P)]
QK_SCALE = 8.0
MASKED = -1e30
LN_EPS = 1e-5
NORM_FLOOR_SQ = 1e-24
STEPS = DEPTH * TILES
LOOP = 6
DRAIN = 5
COLS = 512

SM_G, SM_B, SM_B2, SM_VAL, SM_GATE = 0, 1, 2, 3, 6
SMALL = 9


def valid(step):
    return not isinstance(step, int) or 0 <= step < STEPS


def valid(step):
    return not isinstance(step, int) or 0 <= step < STEPS


def qn_order(i):
    order = []
    for b in range(B):
        if valid(i):
            order += [("qkv", b, 0), ("qkv", b, 1)]
        if b == 0 and valid(i - 3):
            order += ["centre"]
        if valid(i):
            order += [("qkv", b, c) for c in range(2, 6)]
        if b == 1 and valid(i - 4):
            order += [("up", c) for c in range(3)]
    return order


def tr_order(i):
    order = []
    for b in range(B):
        if valid(i - 2):
            order += [("probs", b, f) for f in range(2)]
        if valid(i - 1):
            order += [("qk", b, f) for f in (2, 3, 0, 1)]
    return order


def pv_order(i):
    order = []
    for b in range(B):
        if valid(i - 2):
            order += [("pv", b, f) for f in range(2)]
        if valid(i - 2) or valid(i - 3) or (b == 0 and valid(i - 5)):
            order += [("out", b)]
    return order


def fill(order, i, what):
    if isinstance(i, int):
        n = sum(len(order(k)) for k in range(i)) + order(i).index(what)
        return n % 2, n // 2 + 1
    full = order(LOOP)
    n = sum(len(order(k)) for k in range(LOOP)) + full.index(what)
    return n % 2, (i - LOOP) * (len(full) // 2) + (n // 2 + 1)


def exists(order, i, what):
    return not isinstance(i, int) or (i >= 0 and what in order(i))


def build(nc, a):
    with ExitStack() as ctx:
        def sb(name, shape, dt=F32):
            return ctx.enter_context(nc.sbuf_tensor(name, shape, dt))

        def sem(name):
            return ctx.enter_context(nc.semaphore(name))

        x = sb("x", [P, B, 1 + SEQ])
        xmid = sb("xmid", [P, B, 1 + SEQ])
        branch = sb("branch", [P, B, SEQ])
        ident = sb("ident", [P, P])
        eps_col = sb("eps_col", [P, 1])
        s_const = sem("const_loaded")

        w = layer_tiles(nc, ctx, a, xmid)
        recurrent_branch(nc, a, x, branch, ident, eps_col, s_const, w)
        layers(nc, a, x, xmid, ident, w)
        combine(nc, a, x, branch, ident)


def recurrent_branch(nc, a, x, branch, ident, eps_col, s_const, w):
    with ExitStack() as ctx:
        def sb(name, shape, dt=F32):
            return ctx.enter_context(nc.sbuf_tensor(name, shape, dt))

        def sem(name):
            return ctx.enter_context(nc.semaphore(name))

        NT = B * TILES
        X_PARTS = 4
        PART = NT // X_PARTS
        xt = sb("xt", [P, NT, DIM])
        stats = sb("stats", [P, NT, 6])
        mv = sb("mv", [P, NT, 2])
        lnv = sb("lnv", [P, NT])
        rstd = sb("rstd", [P, NT])
        nw = sb("nw", [P, NT])
        ve = sb("ve", [P, NT])
        w_in = sb("w_in", [P, 2 * HIDDEN])
        wg_lo = sb("wg_lo", [P, 2 * HIDDEN])
        wg_hi = sb("wg_hi", [P, 2 * HIDDEN])
        wo_lo = sb("wo_lo", [P, DIM])
        wo_hi = sb("wo_hi", [P, DIM])
        par = sb("par", [P, 2, 8])
        c8 = sb("c8", [P, 2, 1])
        one_col = sb("one_col", [P, 1])
        tmp = [sb(f"sp{i}", [P, 2, 1]) for i in range(8)]
        GROUPS = (0, 2, 1)
        xh = sb("xh", [P, 3, CONV_K - 1 + SEQ])
        y = sb("y", [P, 3, SEQ])
        alpha = sb("alpha", [P, 3, SEQ])
        sig_in = sb("sig_in", [P, 3, SEQ])
        drive = sb("drive", [P, 3, SEQ])
        gate = sb("gate", [P, 3, SEQ])
        ps = ctx.enter_context(nc.psum_tensor("ps_rec", [P, 8, COLS], F32))

        s_x = [sem(f"r_x{q}") for q in range(X_PARTS)]
        s_w, s_set = sem("r_w"), sem("r_set")
        s_st, s_ve, s_ln, s_y0, s_nw, s_xn = sem("r_stats"), sem("r_var"), sem("r_lnv"), sem("r_rstd0"), sem("r_newton"), sem("r_xn")
        s_tr, s_xT = sem("r_transposed"), sem("r_xT")
        s_sp, s_spe = sem("r_softplus"), sem("r_softplus_exp")
        s_pe = sem("r_phase_done")
        s_xh, s_conv, s_f, s_i, s_al, s_a2, s_be, s_g = (sem("r_xh"), sem("r_conv"), sem("r_forget"), sem("r_input"),
                                                         sem("r_alpha"), sem("r_alpha_sq"), sem("r_beta"), sem("r_gate"))
        s_dr, s_h = sem("r_drive"), sem("r_h")
        s_out = sem("r_branch")
        XH, GATE, FORGET, INPUT, OUT = range(5)

        def bank(g, half):
            return 2 * g + half

        def both(g):
            return ps[:, 2 * g:2 * g + 2, :].rearrange("p a b -> p (a b)")

        def phase_group(phase, g):
            return 2 * phase + (1 if g == 0 else 2)

        with nc.Block() as block:
            @block.sync
            def _(sp):
                xin = a["x"].rearrange("b (t p) d -> p (b t) d", p=P)
                for q in range(X_PARTS):
                    sp.dma_start(xt[:, q * PART:(q + 1) * PART, :], xin[:, q * PART:(q + 1) * PART, :]).then_inc(s_x[q], 16)
                sp.dma_start(ident[:, :], a["ident"]).then_inc(s_const, 16)
                sp.dma_start(w_in[:, :], a["w_in_t"]).then_inc(s_w, 16)
                sp.dma_start(par[:, :, :], a["rec_par"]).then_inc(s_w, 16)
                sp.dma_start(wg_lo[:, :], a["w_gates_t"][0:HID_LO, :]).then_inc(s_w, 16)
                sp.dma_start(wg_hi[0:HID_HI, :], a["w_gates_t"][HID_LO:HIDDEN, :]).then_inc(s_w, 16)
                sp.dma_start(wg_hi[HID_HI:P, :], a["w_gates_t"][HID_LO:HIDDEN, :]).then_inc(s_w, 16)
                sp.dma_start(wo_lo[:, :], a["w_out_t"][0:HID_LO, :]).then_inc(s_w, 16)
                sp.dma_start(wo_hi[0:HID_HI, :], a["w_out_t"][HID_LO:HIDDEN, :]).then_inc(s_w, 16)
                sp.dma_start(wo_hi[HID_HI:P, :], a["w_out_t"][HID_LO:HIDDEN, :]).then_inc(s_w, 16)
                sp.wait_ge(s_w, 8 * 16)
                sp.dma_start(w.rot[:, :, :], a["rot"]).then_inc(w.consts, 16)
                sp.dma_start(w.scales[:, :, :].rearrange("p l d -> p (l d)"), a["scales"].partition_broadcast(P)).then_inc(w.consts, 16)
                sp.dma_start(w.mask[:, :, :], a["mask"]).then_inc(w.consts, 16)
                sp.dma_start(w.first[:, :, :], a["first"]).then_inc(w.consts, 16)
                w.load_first(sp)

            @block.gpsimd
            def _(pool):
                nc.gpsimd.memset(eps_col[:, :], LN_EPS).then_inc(s_set, 1)
                nc.gpsimd.memset(one_col[:, :], 1e-6).then_inc(s_set, 1)
                nc.gpsimd.memset(xh[:, :, 0:CONV_K - 1], 0.0).then_inc(s_set, 1)
                nc.gpsimd.memset(x[:, :, 0:1], 0.0).then_inc(s_set, 1)
                w.clear(nc.gpsimd)
                pool.wait_ge(s_const, 16)
                nc.gpsimd.tensor_scalar(w.centre_w[:, :], ident[:, :], -1.0 / DIM, None, ALU.add).then_inc(w.centre_ready, 1)
                for part in range(3):
                    w.split_high(nc.gpsimd.tensor_copy, pool, 0, part)
                    w.split_low(nc.gpsimd, pool, 0, part)

            @block.vector
            def _(dve):
                v = nc.vector
                for t in range(NT):
                    dve.wait_ge(s_x[t // PART], 16)
                    v.bn_stats(stats[:, t, :], xt[:, t, :]).then_inc(s_st, 1)
                dve.wait_ge(s_st, NT)
                for t in range(NT):
                    v.bn_aggr(mv[:, t, :], stats[:, t, :]).then_inc(s_st, 1)
                dve.wait_ge(s_st, 2 * NT)
                v.tensor_scalar(ve[:, :], mv[:, :, 1], LN_EPS, None, ALU.add).then_inc(s_ve, 1)
                dve.wait_ge(s_y0, 1)
                v.tensor_tensor(nw[:, :], rstd[:, :], rstd[:, :], ALU.mult).then_inc(s_nw, 1)
                dve.wait_ge(s_nw, 1)
                v.tensor_tensor(nw[:, :], nw[:, :], ve[:, :], ALU.mult).then_inc(s_nw, 1)
                dve.wait_ge(s_nw, 2)
                v.tensor_scalar(nw[:, :], nw[:, :], -0.5, 1.5, ALU.mult, ALU.add).then_inc(s_nw, 1)
                dve.wait_ge(s_nw, 3)
                v.tensor_tensor(rstd[:, :], rstd[:, :], nw[:, :], ALU.mult).then_inc(s_nw, 1)
                dve.wait_ge(s_nw, 4)
                for t in range(NT):
                    v.tensor_scalar(xt[:, t, :], xt[:, t, :], mv[:, t, 0:1], rstd[:, t:t + 1],
                                    ALU.subtract, ALU.mult).then_inc(s_xn, 1)
                dve.wait_ge(s_w, 8 * 16)
                n = 0
                fb = par[:, :, 7:8]

                def link(ins):
                    nonlocal n
                    n += 1
                    ins.then_inc(s_sp, 1)
                    dve.wait_ge(s_sp, n)

                link(v.tensor_scalar(tmp[0][:, :, :], fb, -1.0, None, ALU.mult))
                link(v.tensor_tensor(tmp[0][:, :, :], tmp[0][:, :, :], fb, ALU.max))
                dve.wait_ge(s_spe, 1)
                e = tmp[1]
                link(v.tensor_scalar(tmp[2][:, :, :], e[:, :, :], 2.0, None, ALU.add))
                link(v.reciprocal(tmp[3][:, :, :], tmp[2][:, :, :]))
                link(v.tensor_tensor(tmp[3][:, :, :], tmp[3][:, :, :], e[:, :, :], ALU.mult))
                link(v.tensor_tensor(tmp[4][:, :, :], tmp[3][:, :, :], tmp[3][:, :, :], ALU.mult))
                link(v.tensor_scalar(tmp[5][:, :, :], tmp[4][:, :, :], 1.0 / 17, 1.0 / 15, ALU.mult, ALU.add))
                for k in (13, 11, 9, 7, 5, 3, 1):
                    link(v.tensor_tensor(tmp[5][:, :, :], tmp[5][:, :, :], tmp[4][:, :, :], ALU.mult))
                    link(v.tensor_scalar(tmp[5][:, :, :], tmp[5][:, :, :], 1.0 / k, None, ALU.add))
                link(v.tensor_tensor(tmp[5][:, :, :], tmp[5][:, :, :], tmp[3][:, :, :], ALU.mult))
                link(v.tensor_scalar(tmp[6][:, :, :], fb, 0.0, None, ALU.max))
                link(v.tensor_scalar(tmp[5][:, :, :], tmp[5][:, :, :], 2.0, None, ALU.mult))
                link(v.tensor_tensor(tmp[6][:, :, :], tmp[6][:, :, :], tmp[5][:, :, :], ALU.add))
                link(v.tensor_scalar(c8[:, :, :], tmp[6][:, :, :], -8.0, None, ALU.mult))
                for q, g in enumerate(GROUPS):
                    dve.wait_ge(s_xh, q + 1)
                    pg = g // 2
                    for k in range(CONV_K):
                        src = xh[:, g, k:k + SEQ]
                        if k == 0:
                            v.tensor_scalar(y[:, g, :], src, par[:, pg, 0:1], par[:, pg, 4:5],
                                            ALU.mult, ALU.add).then_inc(s_conv, 1)
                        else:
                            dve.wait_ge(s_conv, CONV_K * q + k)
                            v.scalar_tensor_tensor(y[:, g, :], src, par[:, pg, k:k + 1], y[:, g, :],
                                                   ALU.mult, ALU.add).then_inc(s_conv, 1)
                dve.wait_ge(s_conv, 3 * CONV_K)
                for q, g in enumerate(GROUPS):
                    dve.wait_ge(s_al, q + 1)
                    v.tensor_tensor(drive[:, g, :], alpha[:, g, :], alpha[:, g, :], ALU.mult).then_inc(s_a2, 1)
                    dve.wait_ge(s_a2, 2 * q + 1)
                    v.tensor_scalar(drive[:, g, :], drive[:, g, :], -1.0, 1.0, ALU.mult, ALU.add).then_inc(s_a2, 1)
                for q, g in enumerate(GROUPS):
                    dve.wait_ge(s_be, q + 1)
                    v.tensor_tensor(drive[:, g, :], drive[:, g, :], y[:, g, :], ALU.mult).then_inc(s_dr, 1)
                for q, g in enumerate(GROUPS):
                    dve.wait_ge(s_i, q + 1)
                    dve.wait_ge(s_dr, 3 if q == 0 else 3 + q)
                    v.tensor_tensor(drive[:, g, :], drive[:, g, :], sig_in[:, g, :], ALU.mult).then_inc(s_dr, 1)
                    dve.wait_ge(s_dr, 4 + q)
                    v.tensor_tensor_scan(sig_in[:, g, :], alpha[:, g, :], drive[:, g, :], 0.0,
                                         ALU.mult, ALU.add).then_inc(s_h, 1)
                    dve.wait_ge(s_h, 2 * q + 1)
                    dve.wait_ge(s_g, q + 1)
                    v.tensor_tensor(gate[:, g, :], gate[:, g, :], sig_in[:, g, :], ALU.mult).then_inc(s_h, 1)
                for half in range(2):
                    dve.wait_ge(s_pe, 2 * OUT + 1)
                    v.tensor_copy(branch[:, 0, half * COLS:(half + 1) * COLS], ps[:, half, :]).then_inc(s_out, 1)
                dve.wait_ge(s_out, 4)

            @block.scalar
            def _(act):
                s = nc.scalar
                act.wait_ge(s_ve, 1)
                act.wait_ge(s_set, 4)
                s.activation(lnv[:, :], ve[:, :], ACT.Ln).then_inc(s_ln, 1)
                act.wait_ge(s_ln, 1)
                s.activation(rstd[:, :], lnv[:, :], ACT.Exp, scale=-0.5).then_inc(s_y0, 1)
                for t in range(0, NT, 4):
                    act.wait_ge(s_tr, t // 4 + 1)
                    s.activation(x[:, t // TILES, 1 + (t % TILES) * P:1 + (t % TILES + 4) * P], ps[:, t // 4, :],
                                 ACT.Copy).then_inc(s_xT, 1)
                act.wait_ge(s_sp, 2)
                s.activation(tmp[1][:, :, :], tmp[0][:, :, :], ACT.Exp, scale=-1.0).then_inc(s_spe, 1)
                for g in GROUPS:
                    act.wait_ge(s_pe, phase_group(XH, g))
                    s.activation(xh[:, g, CONV_K - 1:CONV_K - 1 + SEQ], both(g), ACT.Copy).then_inc(s_xh, 1)
                for g in GROUPS:
                    act.wait_ge(s_pe, phase_group(GATE, g))
                    s.activation(gate[:, g, :], both(g), ACT.Gelu).then_inc(s_g, 1)
                for g in GROUPS:
                    act.wait_ge(s_pe, phase_group(FORGET, g))
                    s.activation(alpha[:, g, :], both(g), ACT.Sigmoid, bias=par[:, g // 2, 5:6], scale=1.0).then_inc(s_f, 1)
                act.wait_ge(s_sp, 26)
                for q, g in enumerate(GROUPS):
                    act.wait_ge(s_f, q + 1)
                    s.activation(alpha[:, g, :], alpha[:, g, :], ACT.Exp, scale=c8[:, g // 2, :]).then_inc(s_al, 1)
                for q, g in enumerate(GROUPS):
                    act.wait_ge(s_a2, 2 * q + 2)
                    s.activation(drive[:, g, :], drive[:, g, :], ACT.Sqrt, bias=one_col[:, :], scale=1.0).then_inc(s_be, 1)
                for g in GROUPS:
                    act.wait_ge(s_pe, phase_group(INPUT, g))
                    s.activation(sig_in[:, g, :], both(g), ACT.Sigmoid, bias=par[:, g // 2, 6:7], scale=1.0).then_inc(s_i, 1)
                for half in range(2):
                    act.wait_ge(s_pe, 2 * OUT + 2)
                    s.activation(branch[:, 1, half * COLS:(half + 1) * COLS], ps[:, 2 + half, :], ACT.Copy).then_inc(s_out, 1)

            @block.tensor
            def _(pe):
                mm = nc.tensor.matmul
                pe.wait_ge(s_const, 16)
                for t in range(NT):
                    pe.wait_ge(s_xn, t + 1)
                    m = nc.tensor.transpose(ps[:, t // 4, (t % 4) * P:(t % 4 + 1) * P], xt[:, t, :], ident[:, :])
                    if t % 4 == 3:
                        m.then_inc(s_tr, 1)
                pe.wait_ge(s_w, 8 * 16)

                def from_x(c0, b):
                    for half in range(2):
                        pe.wait_ge(s_xT, 2 * b + half + 1)
                        rhs = x[:, b, 1 + half * COLS:1 + (half + 1) * COLS]
                        mm(ps[:, bank(b, half), :], w_in[:, c0:c0 + HID_LO], rhs, start=True, stop=True)
                        m = mm(ps[HID_HI * b:HID_HI * (b + 1), bank(2, half), :], w_in[:, c0 + HID_LO:c0 + HIDDEN], rhs,
                               start=True, stop=True)
                    m.then_inc(s_pe, 1)

                def from_y(c0, b):
                    hi = slice(HID_HI * b, HID_HI * (b + 1))
                    for half in range(2):
                        cols = slice(half * COLS, (half + 1) * COLS)
                        for out, m0, m1 in ((ps[:, bank(b, half), :], c0, c0 + HID_LO),
                                            (ps[hi, bank(2, half), :], c0 + HID_LO, c0 + HIDDEN)):
                            mm(out, wg_lo[:, m0:m1], y[:, b, cols], start=True, stop=False)
                            m = mm(out, wg_hi[hi, m0:m1], y[hi, 2, cols], start=False, stop=True)
                    m.then_inc(s_pe, 1)

                for b in range(B):
                    from_x(HIDDEN, b)
                for b in range(B):
                    pe.wait_ge(s_xh, 2 + b)
                    from_x(0, b)
                for b in range(B):
                    pe.wait_ge(s_g, 2 + b)
                    pe.wait_ge(s_conv, (2 + b) * CONV_K)
                    from_y(0, b)
                for b in range(B):
                    pe.wait_ge(s_f, 2 + b)
                    from_y(HIDDEN, b)
                for b in range(B):
                    pe.wait_ge(s_i, 3)
                    pe.wait_ge(s_h, 4 + 2 * b)
                    hi = slice(HID_HI * b, HID_HI * (b + 1))
                    for half in range(2):
                        cols = slice(half * COLS, (half + 1) * COLS)
                        mm(ps[:, 2 * b + half, :], wo_lo[:, :], gate[:, b, cols], start=True, stop=False)
                        m = mm(ps[:, 2 * b + half, :], wo_hi[hi, :], gate[hi, 2, cols], start=False, stop=True)
                    m.then_inc(s_pe, 1)


class LayerTiles:
    pass


def layer_tiles(nc, ctx, a, xmid):
    def sb(name, shape, dt=F32):
        return ctx.enter_context(nc.sbuf_tensor(name, shape, dt))

    def sem(name):
        return ctx.enter_context(nc.semaphore(name))

    def per_stream(name, shape):
        return [sb(f"{name}{b}", shape) for b in range(B)]

    w = LayerTiles()
    w.w_raw = sb("w_raw", [P, INNER])
    w.w_hi, w.w_lo = sb("w_hi", [P, 3 * INNER], F32R), sb("w_lo", [P, 3 * INNER], F32R)
    w.wo = sb("wo", [P, HP, DIM])
    w.w1 = sb("w1", [P, 2 * FF])
    w.w2 = sb("w2", [P, len(FF_CHUNKS), DIM])
    w.ln_gb = sb("ln_gb", [P, SM_B2])
    w.b2 = sb("b2", [P, 2])
    w.b1 = sb("b1", [P, SMALL - SM_VAL])
    w.rot = sb("rot", [P, TILES, 4 * DH])
    w.scales = sb("scales", [P, DEPTH, 4 * DH])
    w.mask = sb("mask", [P, 2, P])
    w.first = sb("first", [P, 2, WINDOW])
    w.centre_w = sb("centre_w", [P, P])
    w.mean_col = sb("mean_col", [P, 1])
    w.ones = sb("ones", [P, P])
    w.v_own = per_stream("v_own", [P, INNER])
    w.v_back = per_stream("v_back", [P, INNER])
    w.qbd = sb("qbd", [P, HP, 4, 2, WINDOW])
    w.kT = per_stream("kT", [P, HP, WINDOW + P])
    w.pbd = sb("pbd", [P, HP, 2, 2, 2, WINDOW])
    w.consts, w.cleared, w.centre_ready = sem("consts_loaded"), sem("cleared"), sem("centre_w_ready")
    w.wqkv_in, w.hi_ready, w.lo_ready = [[sem(f"w{n}_{what}") for n in "qkv"] for what in ("loaded", "high", "low")]
    w.wo_in, w.gb_in, w.w1_in, w.w2_in, w.b2_in = map(sem, (
        "wo_loaded", "ln_gb_loaded", "w1_loaded", "w2_loaded", "b2_loaded"))

    def load_wqkv(sp, l, part):
        c = slice(part * INNER, (part + 1) * INNER)
        sp.dma_start(w.w_raw[:, :], a["Wqkv"][l, :, c]).then_inc(w.wqkv_in[part], 16)

    def split_high(copy, eng, l, part):
        c = slice(part * INNER, (part + 1) * INNER)
        eng.wait_ge(w.wqkv_in[part], (l + 1) * 16)
        copy(w.w_hi[:, c], w.w_raw[:, :]).then_inc(w.hi_ready[part], 1)

    def split_low(e, eng, l, part):
        c = slice(part * INNER, (part + 1) * INNER)
        eng.wait_ge(w.hi_ready[part], l + 1)
        e.tensor_tensor(w.w_lo[:, c], w.w_raw[:, :], w.w_hi[:, c].bitcast(F32), ALU.subtract).then_inc(w.lo_ready[part], 1)

    def load_wo(sp, l):
        sp.dma_start(w.wo[:, :, :], a["Wo"][l, :, :].rearrange("(c p) n -> p c n", p=P)).then_inc(w.wo_in, 16)

    def load_gb(sp, l):
        sp.dma_start(w.ln_gb[:, :], a["small"][l, :, 0:SM_B2]).then_inc(w.gb_in, 16)

    def load_w1(sp, l):
        sp.dma_start(w.w1[:, :], a["W1"][l, :, :]).then_inc(w.w1_in, 16)

    def load_b1(sp, l):
        sp.dma_start(w.b1[:, :], a["small"][l, :, SM_VAL:SMALL]).then_inc(w.w1_in, 16)

    def load_w2(sp, l):
        sp.dma_start(w.w2[:, 0:2, :], a["W2"][l, 0:2 * P, :].rearrange("(c p) n -> p c n", p=P)).then_inc(w.w2_in, 16)
        sp.dma_start(w.w2[0:FF - 2 * P, 2, :], a["W2"][l, 2 * P:FF, :]).then_inc(w.w2_in, 16)

    def load_b2(sp, l):
        sp.dma_start(w.b2[:, :], a["small"][l, :, SM_B2:SM_B2 + 2]).then_inc(w.b2_in, 16)

    def load_first(sp):
        load_wqkv(sp, 0, 0)
        load_wo(sp, 0)
        load_gb(sp, 0)
        load_w1(sp, 0)
        load_b1(sp, 0)
        load_w2(sp, 0)
        load_b2(sp, 0)
        for part in (1, 2):
            sp.wait_ge(w.lo_ready[part - 1], 1)
            load_wqkv(sp, 0, part)

    def clear(g):
        for b in range(B):
            g.memset(w.kT[b][:, :, :], 0.0)
            g.memset(w.v_own[b][:, :], 0.0)
            g.memset(w.v_back[b][:, :], 0.0)
        g.memset(w.qbd[:, :, :, :, :], 0.0)
        g.memset(w.pbd[:, :, :, :, :, :], 0.0)
        g.memset(xmid[:, :, 0:1], 0.0)
        g.memset(w.ones[:, :], 1.0)
        g.memset(w.mean_col[:, :], 1.0 / DIM).then_inc(w.cleared, 1)

    w.load_wqkv, w.load_wo, w.load_gb, w.load_w1, w.load_b1, w.load_w2, w.load_b2 = (
        load_wqkv, load_wo, load_gb, load_w1, load_b1, load_w2, load_b2)
    w.load_first, w.clear, w.split_high, w.split_low = load_first, clear, split_high, split_low
    return w


def layers(nc, a, x, xmid, ident, w):
    with ExitStack() as ctx:
        def sb(name, shape, dt=F32):
            return ctx.enter_context(nc.sbuf_tensor(name, shape, dt))

        def sem(name):
            return ctx.enter_context(nc.semaphore(name))

        def per_stream(name, shape):
            return [sb(f"{name}{b}", shape) for b in range(B)]

        w_hi, w_lo, wo, w1, w2, ln_gb, b2, b1, rot, scales, mask, first, centre_w, mean_col, ones, v_own, v_back, qbd, kT, pbd = (
            w.w_hi, w.w_lo, w.wo, w.w1, w.w2, w.ln_gb, w.b2, w.b1, w.rot, w.scales, w.mask, w.first, w.centre_w, w.mean_col, w.ones, w.v_own, w.v_back, w.qbd, w.kT, w.pbd)
        tab = sb("tab", [P, 4, DH])
        xs_hi, xs_lo = ([sb(f"xs_{n}{b}", [P, P], F32R) for b in range(B)] for n in ("hi", "lo"))
        qk = per_stream("qk", [P, 2 * INNER])
        sq = per_stream("sq", [P, 2 * INNER])
        ss, rinv, newt = (per_stream(n, [P, 2 * HEADS + B]) for n in ("ss", "rinv", "newt"))
        t2 = sb("t2", [P, 2 * INNER])
        qkr = per_stream("qkr", [P, 2 * INNER])
        v_new = per_stream("v_new", [P, INNER])
        pr = per_stream("pr", [P, HP, 2, 2 * WINDOW])
        rmax, rsum, rrec = (per_stream(n, [P, 2 * HP]) for n in ("rmax", "rsum", "rrec"))
        oT = sb("oT", [P, HP, 2, 2 * WINDOW])
        fx, fc, fsq, fxn, diag = (sb(n, [P, B, P]) for n in ("fx", "fc", "fsq", "fxn", "diag"))
        hid = sb("hid", [P, len(FF_CHUNKS), B, P])

        ps_qn = [ctx.enter_context(nc.psum_tensor(f"ps_qn{i}", [P, COLS], F32)) for i in range(2)]
        ps_tr = [ctx.enter_context(nc.psum_tensor(f"ps_tr{i}", [P, COLS], F32)) for i in range(2)]
        ps_s = ctx.enter_context(nc.psum_tensor("ps_s", [P, HP, 2, 2 * WINDOW], F32))
        ps_pv = [ctx.enter_context(nc.psum_tensor(f"ps_pv{i}", [P, COLS], F32)) for i in range(2)]
        DOWN = slice(P, P + B * P)
        VAR = P + B * P

        consts, cleared, centre_ready, lo_ready, wo_in, gb_in, w1_in, w2_in, b2_in = (
            w.consts, w.cleared, w.centre_ready, w.lo_ready, w.wo_in, w.gb_in, w.w1_in, w.w2_in, w.b2_in)
        qn_full, qn_done = [[sem(f"qn_{n}{i}") for i in range(2)] for n in ("filled", "evacuated")]
        tr_full, tr_done = [[sem(f"tr_{n}{i}") for i in range(2)] for n in ("filled", "evacuated")]
        pv_full, pv_done = [[sem(f"pv_{n}{i}") for i in range(2)] for n in ("filled", "evacuated")]

        def streams(name):
            return [sem(f"{name}{b}") for b in range(B)]

        tab_ready = sem("tab_ready")
        xs_high, xs_ready, ss_sum, ss_ready, newton = map(streams, ("xs_high", "xs_ready", "ss_sum", "ss_ready", "newton"))
        rotated, added, qk_ready = map(streams, ("rotated", "added", "qk_ready"))
        v_carried, v_moved = map(streams, ("v_carried", "v_moved"))
        k_carried = streams("k_carried")
        s_full, s_read = sem("scores_filled"), sem("scores_read")
        max_ready, shifted, exp_ready, sum_ready, rec_ready, probs_ready = map(streams, (
            "max_ready", "shifted", "exp_ready", "sum_ready", "rec_ready", "probs_ready"))
        fx_ready, diag_ready, fxn_ready, gel_ready = map(sem, (
            "fx_ready", "diag_ready", "fxn_ready", "gelu_ready"))
        NEWTON = 11

        def layer_of(step):
            return step // TILES

        def cols(step, lead):
            return bass.ds((step % TILES) * P + lead, P)

        def at(step):
            return bass.ds(step % TILES, 1)

        def later(step):
            return bass.ds((step % TILES + TILES - 1) // TILES, 1)

        def wait_prev(eng, semaphore, value, step):
            if not (isinstance(step, int) and step == 0):
                eng.wait_ge(semaphore, value)

        def wait_fill(eng, sems, order, i, what):
            if exists(order, i, what):
                bank, n = fill(order, i, what)
                eng.wait_ge(sems[bank], n)

        def ring_free(eng, done, bank, count):
            if not (isinstance(count, int) and count == 1):
                eng.wait_ge(done[bank], count - 1)

        def steps(eng, half):
            def change(i):
                half(i, 0, None)
                half(i, 1, layer_of(i + 1))
                half(i + 1, 0, layer_of(i + 1))
                half(i + 1, 1, None)

            def plain(i):
                half(i, 0, None)
                half(i, 1, None)

            for i in range(TILES - 1):
                plain(i)
            change(TILES - 1)
            with eng.Fori(TILES + 1, STEPS - TILES, TILES) as i0:
                with eng.Fori(i0, i0 + TILES - 2) as i:
                    plain(i)
                change(i0 + TILES - 2)
            with eng.Fori(STEPS - TILES + 1, STEPS) as i:
                plain(i)
            for i in range(STEPS, STEPS + DRAIN):
                plain(i)

        with nc.Block() as block:
            @block.sync
            def _(sp):
                def move_v(i, b):
                    j = i - 1
                    if not valid(j):
                        return
                    if isinstance(j, int) and j == 0:
                        sp.wait_ge(cleared, 1)
                    else:
                        wait_fill(sp, pv_full, pv_order, i, ("pv", b, 1))
                    sp.dma_start(v_back[b][0:WINDOW, :], v_own[b][P - WINDOW:P, :]).then_inc(v_carried[b], 16)
                    wait_fill(sp, qn_done, qn_order, j, ("qkv", b, 5))
                    sp.dma_start(v_back[b][WINDOW:P, :], v_new[b][0:P - WINDOW, :]).then_inc(v_moved[b], 16)
                    sp.wait_ge(v_carried[b], (j + 1) * 16)
                    sp.dma_start(v_own[b][:, :], v_new[b][:, :]).then_inc(v_moved[b], 16)

                def load_next_wqkv(l):
                    i = l * TILES + TILES - 1
                    wait_fill(sp, qn_full, qn_order, i, ("qkv", 1, 1))
                    w.load_wqkv(sp, l + 1, 0)
                    move_v(i, 1)
                    wait_fill(sp, qn_full, qn_order, i, ("qkv", 1, 3))
                    sp.wait_ge(lo_ready[0], l + 2)
                    w.load_wqkv(sp, l + 1, 1)
                    wait_fill(sp, qn_full, qn_order, i, ("qkv", 1, 5))
                    sp.wait_ge(lo_ready[1], l + 2)
                    w.load_wqkv(sp, l + 1, 2)

                for l in range(DEPTH + 1):
                    i = l * TILES
                    again = 0 < l < DEPTH
                    for b in range(B):
                        move_v(i, b)
                    for b in range(B):
                        move_v(i + 1, b)
                    if again:
                        wait_fill(sp, pv_full, pv_order, i + 1, ("out", 1))
                        w.load_wo(sp, l)
                    for b in range(B):
                        move_v(i + 2, b)
                    if again:
                        sp.wait_ge(fxn_ready, i)
                        w.load_gb(sp, l)
                    for b in range(B):
                        move_v(i + 3, b)
                    if again:
                        wait_fill(sp, qn_full, qn_order, i + 3, ("up", 2))
                        w.load_w1(sp, l)
                        wait_fill(sp, qn_done, qn_order, i + 3, ("up", 2))
                        w.load_b1(sp, l)
                    move_v(i + 4, 0)
                    if again:
                        wait_fill(sp, pv_full, pv_order, i + 4, ("out", 0))
                        w.load_w2(sp, l)
                        wait_fill(sp, pv_done, pv_order, i + 4, ("out", 0))
                        w.load_b2(sp, l)
                    move_v(i + 4, 1)
                    if l == 0:
                        for t in range(5, TILES - 1):
                            for b in range(B):
                                move_v(t, b)
                    elif l < DEPTH:
                        with sp.Fori(5, TILES - 1) as t:
                            for b in range(B):
                                move_v(i + t, b)
                    move_v(i + TILES - 1, 0)
                    if l < DEPTH - 1:
                        load_next_wqkv(l)
                    else:
                        move_v(i + TILES - 1, 1)

            @block.tensor
            def _(pe):
                mm, tr = nc.tensor.matmul, nc.tensor.transpose

                def flat(t):
                    return t[:, :, :].rearrange("p b t -> p (b t)")

                def next_bank(i, what):
                    bank, n = fill(qn_order, i, what)
                    ring_free(pe, qn_done, bank, n)
                    return bank

                def qkv(i, b, chunks):
                    if not valid(i):
                        return
                    if 0 in chunks:
                        pe.wait_ge(xs_ready[b], i + 1)
                    pe.wait_ge(lo_ready[chunks[0] // 2], layer_of(i) + 1)
                    for c in chunks:
                        bank = next_bank(i, ("qkv", b, c))
                        part = slice(c * COLS, (c + 1) * COLS)
                        mm(ps_qn[bank][:, :], xs_hi[b][:, :], w_hi[:, part], start=True, stop=False)
                        mm(ps_qn[bank][:, :], xs_hi[b][:, :], w_lo[:, part], start=False, stop=False)
                        mm(ps_qn[bank][:, :], xs_lo[b][:, :], w_hi[:, part], start=False, stop=True).then_inc(qn_full[bank], 1)

                def transpose_probs(i, b):
                    j = i - 2
                    if not valid(j):
                        return
                    pe.wait_ge(probs_ready[b], j + 1)
                    for f in range(2):
                        bank, n = fill(tr_order, i, ("probs", b, f))
                        ring_free(pe, tr_done, bank, n)
                        for m in range(4):
                            last = tr(ps_tr[bank][:, m * P:(m + 1) * P],
                                      pr[b][:, 4 * f + m, :, :].rearrange("p u k -> p (u k)"), ident[:, :])
                        last.then_inc(tr_full[bank], 1)

                def transpose_qk(i, b, k):
                    j = i - 1
                    if not valid(j):
                        return
                    pe.wait_ge(qk_ready[b], 2 * j + k + 1)
                    for f in (2 * k, 2 * k + 1):
                        bank, n = fill(tr_order, i, ("qk", b, f))
                        ring_free(pe, tr_done, bank, n)
                        for m in range(4):
                            last = tr(ps_tr[bank][:, m * P:(m + 1) * P], qkr[b][:, (4 * f + m) * P:(4 * f + m + 1) * P],
                                      ident[:, :])
                        last.then_inc(tr_full[bank], 1)

                def scores(i, b):
                    j = i - 1
                    if not valid(j):
                        return
                    for f in (2, 3):
                        wait_fill(pe, tr_done, tr_order, i, ("qk", b, f))
                    if b:
                        pe.wait_ge(s_read, 2 * j + 1)
                    else:
                        wait_prev(pe, s_read, 2 * j, j)
                    for hp in range(HP):
                        if hp % 4 == 0:
                            wait_fill(pe, tr_done, tr_order, i, ("qk", b, hp // 4))
                        for u in range(2):
                            for odd in range(2):
                                w = 2 * u + odd
                                last = mm(ps_s[64 * odd:64 * odd + 64, hp, u, :],
                                          qbd[:, hp, w, :, :].rearrange("p h q -> p (h q)"),
                                          kT[b][:, hp, WINDOW * w:WINDOW * (w + 2)], start=True, stop=True)
                    last.then_inc(s_full, 1)

                def probs_v(i, b):
                    j = i - 2
                    if not valid(j):
                        return
                    pe.wait_ge(v_moved[b], (j + 1) * 32)
                    pe.wait_ge(v_carried[b], (j + 1) * 16)
                    for f in range(2):
                        wait_fill(pe, tr_done, tr_order, i, ("probs", b, f))
                        bank, n = fill(pv_order, i, ("pv", b, f))
                        ring_free(pe, pv_done, bank, n)
                        for m in range(8):
                            hp, odd = 4 * f + m // 2, m % 2
                            v = (v_own if odd else v_back)[b]
                            for h in range(2):
                                head = 2 * hp + h
                                last = mm(ps_pv[bank][DH * h:DH * (h + 1), m * DH:(m + 1) * DH], v[:, head * DH:(head + 1) * DH],
                                          pbd[:, hp, odd, h, :, :].rearrange("p u q -> p (u q)"), start=True, stop=True)
                        last.then_inc(pv_full[bank], 1)

                def out_projection(i, b):
                    if not exists(pv_order, i, ("out", b)):
                        return
                    j, n, m = i - 2, i - 3, i - 5
                    bank, k = fill(pv_order, i, ("out", b))
                    ring_free(pe, pv_done, bank, k)
                    if valid(j):
                        pe.wait_ge(wo_in, (layer_of(j) + 1) * 16)
                        for f in range(2):
                            wait_fill(pe, pv_done, pv_order, i, ("pv", b, f))
                        for hp in range(HP):
                            last = mm(ps_pv[bank][:, 0:P], wo[:, hp, :], oT[:, hp, :, :].rearrange("p a c -> p (a c)"),
                                      start=(hp == 0), stop=(hp == HP - 1))
                    if b == 0 and valid(m):
                        pe.wait_ge(w2_in, (layer_of(m) + 1) * 32)
                        wait_fill(pe, qn_done, qn_order, i - 1, ("up", 2))
                        for c, (r, w) in enumerate(FF_CHUNKS):
                            last = mm(ps_pv[bank][:, DOWN], w2[0:w, c, :], hid[0:w, c, :, :].rearrange("p b t -> p (b t)"),
                                      start=(c == 0), stop=(c == len(FF_CHUNKS) - 1))
                    if b == 0 and valid(n):
                        wait_fill(pe, qn_done, qn_order, i, "centre")
                        for s in range(B):
                            last = mm(ps_pv[bank][:, VAR + s:VAR + s + 1], fsq[:, s, :], mean_col[:, :], start=True, stop=True)
                    if b == 0 or not valid(n):
                        last.then_inc(pv_full[bank], 1)

                def ffn_broadcast(i):
                    n = i - 3
                    if not valid(n):
                        return
                    bank, k = fill(pv_order, i, ("out", 1))
                    pe.wait_ge(diag_ready, n + 1)
                    mm(ps_pv[bank][:, DOWN], ones[:, :], flat(diag), start=True, stop=True).then_inc(pv_full[bank], 1)

                def ffn_centre(i):
                    n = i - 3
                    if not valid(n):
                        return
                    pe.wait_ge(fx_ready, n + 1)
                    bank = next_bank(i, "centre")
                    mm(ps_qn[bank][:, 0:B * P], centre_w[:, :], flat(fx), start=True, stop=True).then_inc(qn_full[bank], 1)

                def ffn_up(i, c):
                    m = i - 4
                    if not valid(m):
                        return
                    if c == 0:
                        pe.wait_ge(w1_in, (layer_of(m) + 1) * 32)
                        pe.wait_ge(fxn_ready, m + 1)
                    r, w = FF_CHUNKS[c]
                    bank = next_bank(i, ("up", c))
                    mm(ps_qn[bank][0:w, 0:B * P], w1[:, r:r + w], flat(fxn), start=True, stop=True)
                    mm(ps_qn[bank][0:w, B * P:2 * B * P], w1[:, FF + r:FF + r + w], flat(fxn),
                       start=True, stop=True).then_inc(qn_full[bank], 1)

                def half(i, b, change):
                    transpose_probs(i, b)
                    qkv(i, b, (0, 1))
                    probs_v(i, b)
                    if b == 0:
                        ffn_centre(i)
                    qkv(i, b, (2, 3))
                    out_projection(i, b)
                    transpose_qk(i, b, 1)
                    qkv(i, b, (4,))
                    transpose_qk(i, b, 0)
                    qkv(i, b, (5,))
                    scores(i, b)
                    if b == 1:
                        ffn_up(i, 0)
                        ffn_up(i, 1)
                        ffn_broadcast(i)
                        ffn_up(i, 2)

                pe.wait_ge(cleared, 1)
                pe.wait_ge(centre_ready, 1)
                steps(pe, half)

            @block.scalar
            def _(act):
                f = nc.scalar.activation

                def before(i, b):
                    return (i, 0) if b else (i - 1, 1)

                def evac_probs(i, b):
                    j = i - 2
                    if not valid(j):
                        return
                    pi, pb = before(i, b)
                    wait_fill(act, pv_full, pv_order, pi, ("pv", pb, 1))
                    for k in range(2):
                        bank, n = fill(tr_order, i, ("probs", b, k))
                        act.wait_ge(tr_full[bank], n)
                        for u in range(2):
                            rows = slice(DH * u, DH * (u + 1))
                            last = f(pbd[rows, 4 * k:4 * k + 4, :, :, u, :].rearrange("p m a h q -> p (m a h) q"),
                                     ps_tr[bank][rows, :].rearrange("p (x q) -> p x q", q=WINDOW), ACT.Copy)
                        last.then_inc(tr_done[bank], 1)

                def evac_qkv(i, b, chunks):
                    if not valid(i):
                        return
                    for c in chunks:
                        bank, n = fill(qn_order, i, ("qkv", b, c))
                        act.wait_ge(qn_full[bank], n)
                        if c < 4:
                            if c == 0:
                                wait_prev(act, added[b], i * 2, i)
                            f(qk[b][:, c * COLS:(c + 1) * COLS], ps_qn[bank][:, :], ACT.Copy)
                            if c == 0:
                                wait_prev(act, ss_sum[b], i, i)
                            f(sq[b][:, c * COLS:(c + 1) * COLS], ps_qn[bank][:, :], ACT.Square).then_inc(qn_done[bank], 1)
                        else:
                            if c == 4:
                                wait_prev(act, v_moved[b], i * 32, i)
                            f(v_new[b][:, (c - 4) * COLS:(c - 3) * COLS], ps_qn[bank][:, :], ACT.Copy).then_inc(qn_done[bank], 1)

                def evac_pv(i, b):
                    j = i - 2
                    if not valid(j):
                        return
                    pi, pb = before(i, b)
                    wait_fill(act, pv_full, pv_order, pi, ("out", pb))
                    for k in range(2):
                        bank, n = fill(pv_order, i, ("pv", b, k))
                        act.wait_ge(pv_full[bank], n)
                        f(oT[:, 4 * k:4 * k + 4, :, :].rearrange("p m a c -> p (m a c)"), ps_pv[bank][:, :],
                          ACT.Copy).then_inc(pv_done[bank], 1)

                def evac_qk(i, b):
                    j = i - 1
                    if not valid(j):
                        return
                    act.wait_ge(k_carried[b], j + 1)
                    for k in range(2):
                        bank, n = fill(tr_order, i, ("qk", b, 2 + k))
                        act.wait_ge(tr_full[bank], n)
                        f(kT[b][:, 4 * k:4 * k + 4, WINDOW:],
                          ps_tr[bank][:, :].rearrange("p (m t) -> p m t", m=4), ACT.Copy).then_inc(tr_done[bank], 1)
                    if b:
                        act.wait_ge(s_full, 2 * j + 1)
                    else:
                        wait_prev(act, s_full, 2 * j, j)
                    for k in range(2):
                        bank, n = fill(tr_order, i, ("qk", b, k))
                        act.wait_ge(tr_full[bank], n)
                        for h in range(2):
                            rows = slice(DH * h, DH * (h + 1))
                            last = f(qbd[rows, 4 * k:4 * k + 4, :, h, :],
                                     ps_tr[bank][rows, :].rearrange("p (m w q) -> p m w q", m=4, w=4), ACT.Copy)
                        last.then_inc(tr_done[bank], 1)

                def exps(j, b):
                    if not valid(j):
                        return
                    act.wait_ge(shifted[b], j + 1)
                    f(pr[b][:, :, :, :], pr[b][:, :, :, :], ACT.Exp, scale=QK_SCALE).then_inc(exp_ready[b], 1)

                def ffn_square(i):
                    n = i - 3
                    if not valid(n):
                        return
                    bank, k = fill(qn_order, i, "centre")
                    act.wait_ge(qn_full[bank], k)
                    if not (isinstance(n, int) and n == 0):
                        wait_fill(act, pv_done, pv_order, i - 1, ("out", 1))
                    f(fc[:, :, :].rearrange("p b t -> p (b t)"), ps_qn[bank][:, 0:B * P], ACT.Copy)
                    if not (isinstance(n, int) and n == 0):
                        wait_fill(act, pv_full, pv_order, i - 1, ("out", 0))
                    f(fsq[:, :, :].rearrange("p b t -> p (b t)"), ps_qn[bank][:, 0:B * P], ACT.Square).then_inc(qn_done[bank], 1)

                def ffn_gelu(i, c):
                    m = i - 4
                    if not valid(m):
                        return
                    bank, k = fill(qn_order, i, ("up", c))
                    act.wait_ge(qn_full[bank], k)
                    if c == 0 and not (isinstance(m, int) and m == 0):
                        wait_fill(act, pv_full, pv_order, i, ("out", 0))
                    w = FF_CHUNKS[c][1]
                    f(hid[0:w, c, :, :].rearrange("p b t -> p (b t)"), ps_qn[bank][0:w, B * P:2 * B * P], ACT.Gelu,
                      bias=b1[0:w, len(FF_CHUNKS) + c:len(FF_CHUNKS) + c + 1], scale=1.0).then_inc(gel_ready, 1)

                def half(i, b, change):
                    evac_probs(i, b)
                    evac_qkv(i, b, (0, 1))
                    evac_pv(i, b)
                    if b == 0:
                        ffn_square(i)
                    evac_qkv(i, b, (2, 3))
                    if b == 0:
                        exps(i - 2, 1)
                    else:
                        exps(i - 1, 0)
                    if b == 1 and change is not None:
                        w.split_high(round_weights, act, change, 0)
                    if b == 0 and change is not None:
                        w.split_high(round_weights, act, change, 2)
                    evac_qk(i, b)
                    evac_qkv(i, b, (4, 5))
                    if b == 1:
                        for c in range(3):
                            ffn_gelu(i, c)
                    if b == 1 and change is not None:
                        w.split_high(round_weights, act, change, 1)

                def round_weights(out, weights):
                    return f(out, weights, ACT.Copy)

                act.wait_ge(cleared, 1)
                steps(act, half)

            @block.vector
            def _(dve):
                v = nc.vector

                def shift_in(i, b):
                    if not valid(i):
                        return
                    if not (isinstance(i, int) and i == 0):
                        wait_fill(dve, qn_full, qn_order, i - 1, ("qkv", b, 5))
                    v.tensor_scalar(xs_hi[b][0:64, :], x[0:64, b, cols(i, 1)], 1.0, None, ALU.mult)
                    v.tensor_scalar(xs_hi[b][64:P, :], x[64:P, b, cols(i, 0)], 1.0, None, ALU.mult).then_inc(xs_high[b], 1)

                def shift_in_low(i, b):
                    if not valid(i):
                        return
                    dve.wait_ge(xs_high[b], i + 1)
                    for rows, lead in ((slice(0, 64), 1), (slice(64, P), 0)):
                        last = v.tensor_tensor(xs_lo[b][rows, :], x[rows, b, cols(i, lead)], xs_hi[b][rows, :].bitcast(F32),
                                               ALU.subtract)
                    last.then_inc(xs_ready[b], 1)

                def square_sums(s, b):
                    if not valid(s):
                        return
                    for c in (2, 3):
                        wait_fill(dve, qn_done, qn_order, s, ("qkv", b, c))
                    wait_prev(dve, newton[b], NEWTON * s, s)
                    v.tensor_reduce(ss[b][:, 0:2 * HEADS], sq[b][:, :].rearrange("p (h d) -> p h d", d=DH),
                                    AX.X, ALU.add).then_inc(ss_sum[b], 1)

                def floor(s, b):
                    if not valid(s):
                        return
                    dve.wait_ge(ss_sum[b], s + 1)
                    v.tensor_scalar(ss[b][:, 0:2 * HEADS], ss[b][:, 0:2 * HEADS], NORM_FLOOR_SQ, None,
                                    ALU.max).then_inc(ss_ready[b], 1)

                def sine(s, b, k):
                    if not valid(s):
                        return
                    if b:
                        dve.wait_ge(added[0], 2 * s + k + 1)
                    elif not (isinstance(s, int) and s == 0):
                        dve.wait_ge(added[1], 2 * (s - 1) + k + 1)
                    dve.wait_ge(tab_ready, s + 1)
                    for c in (2 * k, 2 * k + 1):
                        wait_fill(dve, qn_done, qn_order, s, ("qkv", b, c))
                    part = slice(k * INNER, (k + 1) * INNER)
                    swapped = qk[b][:, part].rearrange("p (h s d) -> p h s d", s=2, d=DH // 2)[:, :, ::-1, :]
                    v.tensor_tensor(t2[:, part].rearrange("p (h s d) -> p h s d", s=2, d=DH // 2), swapped,
                                    tab[:, 2 * k + 1:2 * k + 2, :].rearrange("p o (s d) -> p o s d", s=2)
                                    .broadcast_to([P, HEADS, 2, DH // 2]), ALU.mult).then_inc(rotated[b], 1)

                def cosine(s, b, k):
                    if not valid(s):
                        return
                    dve.wait_ge(rotated[b], 4 * s + 2 * k + 1)
                    src = qk[b][:, k * INNER:(k + 1) * INNER].rearrange("p (h d) -> p h d", d=DH)
                    v.tensor_tensor(src, src, tab[:, 2 * k:2 * k + 1, :].broadcast_to([P, HEADS, DH]),
                                    ALU.mult).then_inc(rotated[b], 1)

                def inverse_root(s, b, n, k):
                    lo = 0 if valid(s) else 2 * HEADS
                    hi = 2 * HEADS + B if b == 0 and valid(n) else 2 * HEADS
                    if lo == hi:
                        return
                    y, t, w = rinv[b][:, lo:hi], newt[b][:, lo:hi], ss[b][:, lo:hi]
                    if k > 0:
                        dve.wait_ge(newton[b], NEWTON * s + k)
                    if k == 0:
                        if valid(s):
                            dve.wait_ge(ss_ready[b], s + 1)
                            wait_prev(dve, qk_ready[b], 2 * s, s)
                        if hi > 2 * HEADS:
                            wait_fill(dve, pv_done, pv_order, s, ("out", 0))
                            wait_prev(dve, diag_ready, n, n)
                        ins = v.tensor_scalar(y.bitcast(I32), w.bitcast(I32), 1, None, ALU.logical_shift_right)
                    elif k == 1:
                        ins = v.tensor_scalar(y.bitcast(I32), y.bitcast(I32), -1.0, float(0x5f3759df), ALU.mult, ALU.add)
                    elif k % 3 == 2:
                        ins = v.tensor_tensor(t, y, y, ALU.mult)
                    elif k % 3 == 0:
                        ins = v.scalar_tensor_tensor(t, t, -0.5, w, ALU.mult, ALU.mult)
                    else:
                        ins = v.scalar_tensor_tensor(y, t, 1.5, y, ALU.add, ALU.mult)
                    ins.then_inc(newton[b], 1)

                def carry_k(i, b):
                    j = i - 1
                    if not valid(j):
                        return
                    wait_prev(dve, s_full, 2 * j + b - 1, j)
                    v.tensor_tensor(kT[b][:, :, 0:WINDOW], kT[b][:, :, P:P + WINDOW],
                                    first[:, later(j), :].broadcast_to([P, HP, WINDOW]), ALU.mult).then_inc(k_carried[b], 1)

                def masked(j, b):
                    if not valid(j):
                        return
                    dve.wait_ge(s_full, 2 * j + b + 1)
                    wait_fill(dve, tr_full, tr_order, j + 1, ("probs", b, 1))
                    flat = pr[b][:, :, :, :].rearrange("p m u k -> p m (u k)")
                    v.tensor_tensor(flat, ps_s[:, :, :, :].rearrange("p m u k -> p m (u k)"),
                                    mask[:, later(j), :].broadcast_to([P, HP, P]), ALU.add).then_inc(s_read, 1)

                def maxima(j, b):
                    if not valid(j):
                        return
                    dve.wait_ge(s_read, 2 * j + b + 1)
                    v.tensor_reduce(rmax[b][:, :], pr[b][:, :, :, :].rearrange("p m u k -> p (m u) k"), AX.X,
                                    ALU.max).then_inc(max_ready[b], 1)

                def row_sums(j, b):
                    if not valid(j):
                        return
                    dve.wait_ge(exp_ready[b], j + 1)
                    v.tensor_reduce(rsum[b][:, :], pr[b][:, :, :, :].rearrange("p m u k -> p (m u) k"), AX.X,
                                    ALU.add).then_inc(sum_ready[b], 1)

                def row_recips(j, b):
                    if not valid(j):
                        return
                    dve.wait_ge(sum_ready[b], j + 1)
                    wait_prev(dve, probs_ready[b], j, j)
                    v.reciprocal(rrec[b][:, :], rsum[b][:, :]).then_inc(rec_ready[b], 1)

                def residual(bank, j, b):
                    return v.tensor_tensor(xmid[:, b, cols(j, 1)].rearrange("p (u a q) -> p a u q", u=2, a=2),
                                           ps_pv[bank][:, 0:P].rearrange("p (a u q) -> p a u q", u=2, a=2),
                                           x[:, b, cols(j, 1)].rearrange("p (u a q) -> p a u q", u=2, a=2), ALU.add)

                def take_out0(i):
                    if not exists(pv_order, i, ("out", 0)):
                        return
                    j, n, m = i - 2, i - 3, i - 5
                    bank, k = fill(pv_order, i, ("out", 0))
                    dve.wait_ge(pv_full[bank], k)
                    if valid(n):
                        if not (isinstance(n, int) and n == 0):
                            dve.wait_ge(newton[0], NEWTON * i)
                        last = v.tensor_scalar(ss[0][:, 2 * HEADS:], ps_pv[bank][:, VAR:VAR + B], LN_EPS, None, ALU.add)
                    if valid(j):
                        last = residual(bank, j, 0)
                    if valid(m):
                        dve.wait_ge(b2_in, (layer_of(m) + 1) * 16)
                        last = v.scalar_tensor_tensor(x[:, :, cols(m, 1)],
                                                      ps_pv[bank][:, DOWN].rearrange("p (b t) -> p b t", b=B),
                                                      b2[:, 0:1], xmid[:, :, cols(m, 1)], ALU.add, ALU.add)
                    last.then_inc(pv_done[bank], 1)

                def take_out1(i):
                    if not exists(pv_order, i - 1, ("out", 1)):
                        return
                    j, m = i - 3, i - 4
                    bank, k = fill(pv_order, i - 1, ("out", 1))
                    dve.wait_ge(pv_full[bank], k)
                    if valid(j):
                        last = residual(bank, j, 1)
                    if valid(m):
                        wait_fill(dve, qn_full, qn_order, i - 1, ("up", 2))
                        last = v.tensor_tensor(fxn[:, :, :].rearrange("p b t -> p (b t)"),
                                               fc[:, :, :].rearrange("p b t -> p (b t)"), ps_pv[bank][:, DOWN], ALU.mult)
                    last.then_inc(pv_done[bank], 1)
                    if valid(m):
                        dve.wait_ge(pv_done[bank], k)
                        dve.wait_ge(gb_in, (layer_of(m) + 1) * 16)
                        v.tensor_scalar(fxn[:, :, :], fxn[:, :, :], ln_gb[:, SM_G:SM_G + 1], ln_gb[:, SM_B:SM_B + 1],
                                        ALU.mult, ALU.add).then_inc(fxn_ready, 1)

                def ffn_shift(i):
                    n = i - 3
                    if not valid(n):
                        return
                    for b in range(B):
                        wait_fill(dve, pv_done, pv_order, i - 1, ("out", b))
                    if not (isinstance(n, int) and n == 0):
                        wait_fill(dve, qn_full, qn_order, i - 1, "centre")
                    v.tensor_scalar(fx[0:64, :, :], xmid[0:64, :, cols(n, 1)], 1.0, None, ALU.mult)
                    v.tensor_scalar(fx[64:P, :, :], xmid[64:P, :, cols(n, 0)], 1.0, None, ALU.mult).then_inc(fx_ready, 1)

                def ffn_diag(i):
                    n = i - 3
                    if not valid(n):
                        return
                    dve.wait_ge(newton[0], NEWTON * (i + 1))
                    if not (isinstance(n, int) and n == 0):
                        wait_fill(dve, pv_full, pv_order, i - 1, ("out", 1))
                    for s in range(B):
                        last = v.tensor_scalar(diag[:, s, :], ident[:, :], rinv[0][:, 2 * HEADS + s:2 * HEADS + s + 1], None,
                                               ALU.mult)
                    last.then_inc(diag_ready, 1)

                def ffn_gate(i, c):
                    m = i - 4
                    if not valid(m):
                        return
                    w = FF_CHUNKS[c][1]
                    bank, k = fill(qn_order, i, ("up", c))
                    dve.wait_ge(gel_ready, 3 * m + c + 1)
                    gel = hid[0:w, c, :, :].rearrange("p b t -> p (b t)")
                    v.scalar_tensor_tensor(gel, ps_qn[bank][0:w, 0:B * P], b1[0:w, c:c + 1], gel,
                                           ALU.add, ALU.mult).then_inc(qn_done[bank], 1)

                def half0(i, change):
                    def root(*ks):
                        for k in ks:
                            inverse_root(i - 1, 1, None, k)

                    s, j = i - 1, i - 2
                    take_out1(i)
                    carry_k(i, 0)
                    masked(j, 1)
                    ffn_shift(i)
                    maxima(j, 1)
                    if change is not None:
                        w.split_low(v, dve, change, 1)
                    square_sums(s, 1)
                    sine(s, 1, 0)
                    floor(s, 1)
                    cosine(s, 1, 0)
                    root(0)
                    sine(s, 1, 1)
                    root(1)
                    if change is not None:
                        w.split_low(v, dve, change, 2)
                    row_sums(j, 1)
                    root(2)
                    row_recips(j, 1)
                    root(3)
                    cosine(s, 1, 1)
                    root(4)
                    shift_in(i, 1)
                    root(5)
                    shift_in_low(i, 1)
                    root(*range(6, NEWTON))

                def half1(i, change):
                    def root(*ks):
                        for k in ks:
                            inverse_root(i, 0, i - 3, k)

                    s, j = i, i - 1
                    take_out0(i)
                    carry_k(i, 1)
                    masked(j, 0)
                    maxima(j, 0)
                    square_sums(s, 0)
                    sine(s, 0, 0)
                    floor(s, 0)
                    cosine(s, 0, 0)
                    root(0)
                    sine(s, 0, 1)
                    root(1)
                    row_sums(j, 0)
                    root(2)
                    row_recips(j, 0)
                    root(3)
                    cosine(s, 0, 1)
                    root(4)
                    if change is not None:
                        w.split_low(v, dve, change, 0)
                    shift_in(i + 1, 0)
                    root(5)
                    shift_in_low(i + 1, 0)
                    root(*range(6, NEWTON))
                    ffn_diag(i)
                    for c in range(3):
                        ffn_gate(i, c)
                def half(i, b, change):
                    if b:
                        half1(i, change)
                    else:
                        half0(i, change)

                dve.wait_ge(consts, 64)
                shift_in(0, 0)
                shift_in_low(0, 0)
                steps(dve, half)
                wait_fill(dve, pv_done, pv_order, STEPS + DRAIN - 1, ("out", 0))

            @block.gpsimd
            def _(pool):
                g = nc.gpsimd

                def tables(i):
                    if not valid(i):
                        return
                    wait_prev(pool, rotated[1], 4 * i, i)
                    g.tensor_tensor(tab[:, :, :].rearrange("p k d -> p (k d)").unsqueeze(1),
                                    rot[:, at(i), :], scales[:, bass.ds(layer_of(i), 1), :],
                                    ALU.mult).then_inc(tab_ready, 1)

                def add(s, b, k):
                    if not valid(s):
                        return
                    wait_fill(pool, tr_full, tr_order, s, ("qk", b, 0))
                    wait_fill(pool, tr_full, tr_order, s, ("qk", b, 1))
                    pool.wait_ge(rotated[b], 4 * s + 2 * k + 2)
                    part = slice(k * INNER, (k + 1) * INNER)
                    g.tensor_tensor(qkr[b][:, part], qk[b][:, part], t2[:, part], ALU.add).then_inc(added[b], 1)

                def scale(s, b, k):
                    if not valid(s):
                        return
                    if k == 0:
                        pool.wait_ge(newton[b], NEWTON * (s + 1))
                    pool.wait_ge(added[b], 2 * s + k + 1)
                    part = qkr[b][:, k * INNER:(k + 1) * INNER].rearrange("p (h d) -> p h d", d=DH)
                    g.tensor_tensor(part, part, rinv[b][:, k * HEADS:(k + 1) * HEADS].unsqueeze(2)
                                    .broadcast_to([P, HEADS, DH]), ALU.mult).then_inc(qk_ready[b], 1)

                def less_max(j, b):
                    if not valid(j):
                        return
                    pool.wait_ge(max_ready[b], j + 1)
                    rows = pr[b][:, :, :, :].rearrange("p m u k -> p (m u) k")
                    g.tensor_tensor(rows, rows, rmax[b][:, :].unsqueeze(2).broadcast_to([P, 2 * HP, 2 * WINDOW]),
                                    ALU.subtract).then_inc(shifted[b], 1)

                def scale_probs(j, b):
                    if not valid(j):
                        return
                    pool.wait_ge(rec_ready[b], j + 1)
                    rows = pr[b][:, :, :, :].rearrange("p m u k -> p (m u) k")
                    g.tensor_tensor(rows, rows, rrec[b][:, :].unsqueeze(2).broadcast_to([P, 2 * HP, 2 * WINDOW]),
                                    ALU.mult).then_inc(probs_ready[b], 1)

                def half(i, b, change):
                    s, j, other = (i, i - 1, 0) if b else (i - 1, i - 2, 1)
                    add(s, other, 0)
                    scale_probs(j, other)
                    add(s, other, 1)
                    if b == 0:
                        tables(i)
                    scale(s, other, 0)
                    less_max(i - 1, b)
                    scale(s, other, 1)

                pool.wait_ge(consts, 64)
                steps(pool, half)


def combine(nc, a, x, branch, ident):
    with ExitStack() as ctx:
        def sem(name):
            return ctx.enter_context(nc.semaphore(name))

        NT = B * TILES
        sig = ctx.enter_context(nc.sbuf_tensor("sig", [P, B, SEQ], F32))
        xin = ctx.enter_context(nc.sbuf_tensor("xin", [P, NT, DIM], F32))
        out = ctx.enter_context(nc.sbuf_tensor("outs", [P, NT, DIM], F32))
        ps = ctx.enter_context(nc.psum_tensor("ps_out", [P, 4, COLS], F32))
        xin_in, sig_ready, silu_ready, prod_ready, tr_full, sum_ready, out_sent = map(sem, (
            "c_input", "c_sigmoid", "c_silu", "c_product", "c_transposed", "c_sum", "c_out"))
        QUARTERS = 4

        def quarter(t, q, lead=0):
            return t[:, q // 2, lead + (q % 2) * COLS:lead + (q % 2 + 1) * COLS]

        with nc.Block() as block:
            @block.sync
            def _(sp):
                tokens = a["x"].rearrange("b (t p) d -> p (b t) d", p=P)
                for q in range(QUARTERS):
                    sp.dma_start(xin[:, 4 * q:4 * q + 4, :], tokens[:, 4 * q:4 * q + 4, :]).then_inc(xin_in, 16)
                for q in range(QUARTERS):
                    sp.wait_ge(sum_ready, q + 1)
                    sp.dma_start(a["out"].rearrange("b (t p) d -> p (b t) d", p=P)[:, 4 * q:4 * q + 4, :],
                                 out[:, 4 * q:4 * q + 4, :]).then_inc(out_sent, 16)
                sp.wait_ge(out_sent, 16 * QUARTERS)

            @block.scalar
            def _(act):
                for q in range(QUARTERS):
                    nc.scalar.activation(quarter(sig, q), quarter(x, q, 1), ACT.Sigmoid).then_inc(sig_ready, 1)

            @block.vector
            def _(dve):
                v = nc.vector

                def add_input(q):
                    dve.wait_ge(xin_in, 16 * QUARTERS)
                    dve.wait_ge(tr_full, q + 1)
                    v.tensor_tensor(out[:, 4 * q:4 * q + 4, :].rearrange("p t d -> p (t d)"), ps[:, q, :],
                                    xin[:, 4 * q:4 * q + 4, :].rearrange("p t d -> p (t d)"), ALU.add).then_inc(sum_ready, 1)

                for q in range(QUARTERS):
                    dve.wait_ge(sig_ready, q + 1)
                    v.tensor_tensor(quarter(sig, q), quarter(sig, q), quarter(x, q, 1), ALU.mult).then_inc(silu_ready, 1)
                    dve.wait_ge(silu_ready, q + 1)
                    v.tensor_tensor(quarter(sig, q), quarter(sig, q), quarter(branch, q), ALU.mult).then_inc(prod_ready, 1)
                    if q > 0:
                        add_input(q - 1)
                add_input(QUARTERS - 1)

            @block.tensor
            def _(pe):
                for t in range(NT):
                    b, k = t // TILES, t % TILES
                    if t % 4 == 0:
                        pe.wait_ge(prod_ready, t // 4 + 1)
                    m = nc.tensor.transpose(ps[:, t // 4, (t % 4) * P:(t % 4 + 1) * P], sig[:, b, k * P:(k + 1) * P], ident[:, :])
                    if t % 4 == 3:
                        m.then_inc(tr_full, 1)


def rotary_constants():
    f = np.float32
    half = np.arange(0, DH, 2, dtype=f)
    inv_freq = (f(1.0) / np.power(f(10000.0), half / f(DH))).astype(f)
    t = np.arange(SEQ, dtype=f)
    freqs = (t[:, None] * inv_freq[None, :]).astype(f)
    base = ((half + f(0.4 * DH)) / f(1.4 * DH)).astype(f)
    power = ((t - f(SEQ // 2)) / f(WINDOW // 2)).astype(f)
    scale = np.power(base[None, :], power[:, None]).astype(f)
    cos, sin, inv = np.cos(freqs), np.sin(freqs), (f(1.0) / scale)
    parts = []
    for s in (scale, inv):
        c, n = cos * s, sin * s
        parts += [c, c, -n, n]
    tab = np.concatenate(parts, 1).astype(f)
    return np.ascontiguousarray(tab.reshape(TILES, P, 4 * DH).transpose(1, 0, 2))


def mask_constants():
    m = np.full((2, 2, WINDOW, 2, 2, 2 * WINDOW), MASKED, np.float32)
    q = np.arange(WINDOW)[:, None]
    k = np.arange(2 * WINDOW)[None, :]
    ok = (k >= q) & (k <= q + WINDOW)
    for par in range(2):
        for t in range(2):
            for u in range(2):
                valid = ok & ((k >= WINDOW) if t == 0 and u == 0 and par == 0 else True)
                m[par, :, :, t, u, :] = np.where(valid, 0.0, MASKED)
    return m.reshape(P, 2, P)


def kernel(L0_attn_x, L0_attn_W_in, L0_attn_conv_w, L0_attn_conv_b, L0_attn_W_gates, L0_attn_b_gates,
           L0_attn_forget_base, L0_attn_W_out, L0_ffn_Wqkv, L0_ffn_q_scale, L0_ffn_k_scale, L0_ffn_Wo, L0_ffn_ln_g,
           L0_ffn_ln_b, L0_ffn_W1, L0_ffn_b1, L0_ffn_W2, L0_ffn_b2):
    import concourse.bacc as bacc
    from concourse.bass_utils import run_bass_kernel_spmd

    def arr(v):
        return np.ascontiguousarray(v)

    by_channel = np.stack([*np.asarray(L0_attn_conv_w).T, np.asarray(L0_attn_conv_b),
                           *np.asarray(L0_attn_b_gates).reshape(2, HIDDEN), np.asarray(L0_attn_forget_base)], 1)
    rec_par = np.stack([by_channel[0:HID_LO], np.concatenate([by_channel[HID_LO:], by_channel[HID_LO:]])], 1)
    qs, ks = np.asarray(L0_ffn_q_scale), np.asarray(L0_ffn_k_scale)
    swap = np.r_[DH // 2:DH, 0:DH // 2]
    scales = np.concatenate([qs, qs[:, swap], ks, ks[:, swap]], 1).reshape(-1)
    small = np.zeros((DEPTH, P, SMALL), np.float32)
    small[:, :, SM_G], small[:, :, SM_B], small[:, :, SM_B2] = np.asarray(L0_ffn_ln_g), np.asarray(L0_ffn_ln_b), np.asarray(L0_ffn_b2)
    b1 = np.asarray(L0_ffn_b1)
    for c, (r, m) in enumerate(FF_CHUNKS):
        small[:, 0:m, SM_VAL + c] = b1[:, r:r + m]
        small[:, 0:m, SM_GATE + c] = b1[:, FF + r:FF + r + m]
    first = np.ones((P, 2, WINDOW), np.float32)
    first[:, 0, :] = 0.0
    arrays = {
        "x": arr(L0_attn_x), "w_in_t": arr(np.asarray(L0_attn_W_in).T), "w_gates_t": arr(np.asarray(L0_attn_W_gates).T),
        "w_out_t": arr(np.asarray(L0_attn_W_out).T), "rec_par": arr(rec_par), "Wqkv": arr(L0_ffn_Wqkv), "Wo": arr(L0_ffn_Wo),
        "W1": arr(L0_ffn_W1), "W2": arr(L0_ffn_W2), "scales": arr(scales), "small": small,
        "rot": rotary_constants(), "mask": mask_constants(), "first": first, "ident": np.eye(P, dtype=np.float32),
    }
    nc = bacc.Bacc("TRN2", target_bir_lowering=False, num_devices=1)
    aps = {n: nc.dram_tensor(f"in_{n}", v.shape, F32, kind="ExternalInput").ap() for n, v in arrays.items()}
    aps["out"] = nc.dram_tensor("out", (B, SEQ, DIM), F32, kind="ExternalOutput").ap()
    build(nc, aps)
    r = run_bass_kernel_spmd(nc, [{f"in_{n}": v for n, v in arrays.items()}], core_ids=[0])
    return r.results[0]["out"]
```
